# Optimizing a Trainium2 kernel written in Bass

```python
import numpy as np
import jax
import jax.numpy as jnp

def _softmax(x, axis=-1):
    return jax.nn.softmax(x, axis=axis)

def _gelu(x):
    return jax.nn.gelu(x, approximate=True)

def _silu(x):
    return jax.nn.silu(x)

def _sigmoid(x):
    return jax.nn.sigmoid(x)

def _layernorm(x, axis=-1, eps=1e-05):
    m = jnp.mean(x, axis=axis, keepdims=True)
    v = jnp.var(x, axis=axis, keepdims=True)
    return (x - m) / jnp.sqrt(v + eps)

def _scatter_add(tgt, idx, src, axis=0):
    return tgt.at[idx].add(src)

def _segment_sum(src, seg, n):
    return jax.ops.segment_sum(src, seg, n)
kernel_name = 'mk_flamingo_gated_d2_seqx_r8_4c889a'

def setup_inputs(seed: int=0):
    np.random.seed(seed)
    _w = jnp.asarray

    def _rec_inputs():
        import jax
        import jax.numpy as jnp
        _rk = jax.random.key(seed)
        x = -0.0002928 + 1 * jax.random.normal(jax.random.fold_in(_rk, 1), (16, 128, 128), jnp.float32)
        _lenS = 128 - jax.random.randint(jax.random.fold_in(_rk, 7), (16,), 0, max(1, 128 // 4) + 1, jnp.int32)
        _lenS2 = 128 - jax.random.randint(jax.random.fold_in(_rk, 8), (16,), 0, max(1, 128 // 4) + 1, jnp.int32)
        _ctx_1024P = jax.random.normal(jax.random.fold_in(_rk, 11), (16, 16, 128), jnp.float32)
        _ctx_1024c = jax.random.dirichlet(jax.random.fold_in(_rk, 511), 0.3 * jnp.ones((16,), jnp.float32), (16, 128))
        _ctx_1024t = jnp.einsum('bsk,bkd->bsd', _ctx_1024c, _ctx_1024P)
        _ctx_1024t = _ctx_1024t * jax.lax.rsqrt(jnp.mean(jnp.square(_ctx_1024t)) + 1e-12) * 0.953939
        ctx_1024 = -1.39393e-06 + 0.999914 * (_ctx_1024t + 0.3 * jax.random.normal(jax.random.fold_in(_rk, 611), (16, 128, 128), jnp.float32))
        _validS = jnp.arange(128)[None, :] < _lenS[:, None]
        _validS2 = jnp.arange(128)[None, :] < _lenS2[:, None]
        _causal = jnp.tril(jnp.ones((128, 128), dtype=bool))
        mask_1x1xSxS2_bf1 = jnp.ones((1, 1, 128, 128), dtype=bool)
        _g = jax.random.normal(jax.random.fold_in(_rk, 9001), (2, 2), jnp.float32)
        _g = jnp.sign(_g) * jnp.maximum(jnp.abs(_g), 1.0) + (_g == 0) * 1.0
        g_xattn = _g[0]
        g_ffn = _g[1]
        return (x, ctx_1024, mask_1x1xSxS2_bf1, g_xattn, g_ffn)
    x, ctx_1024, mask_1x1xSxS2_bf1, g_xattn, g_ffn = _rec_inputs()

    def _L0_xattn_setup():
        import jax, jax.numpy as jnp
        import numpy as np
        H = 16
        HID = 64

        def _gelu(x):
            return jax.nn.gelu(x, approximate=False)
        key = jax.random.key(seed)
        ks = jax.random.split(key, 12)
        B, N, D = (2, 256, 128)
        Dh = D // H
        inp = {'query': jax.random.normal(ks[0], (B, N, D), jnp.float32), 'key': jax.random.normal(ks[1], (B, N, D), jnp.float32), 'value': jax.random.normal(ks[2], (B, N, D), jnp.float32), 'allowed_mask': jnp.ones((1, 1, N, N), dtype=bool), 'wq': jax.random.normal(ks[3], (D, D), jnp.float32) * D ** (-0.5), 'wk': jax.random.normal(ks[4], (D, D), jnp.float32) * D ** (-0.5), 'wv': jax.random.normal(ks[5], (D, D), jnp.float32) * D ** (-0.5), 'wo': jax.random.normal(ks[6], (D, D), jnp.float32) * D ** (-0.5), 'wb1': jax.random.normal(ks[7], (HID, 1), jnp.float32), 'wb2': jax.random.normal(ks[8], (H * Dh, HID), jnp.float32) * HID ** (-0.5), 'wg1': jax.random.normal(ks[9], (HID, Dh), jnp.float32) * Dh ** (-0.5), 'wg2': jax.random.normal(ks[10], (Dh, HID), jnp.float32) * HID ** (-0.5), 'n_context': 256}
        return inp
    _L0_xattn_all = _L0_xattn_setup()
    _L0_xattn_in = {k: v for k, v in _L0_xattn_all.items() if k in ('wq', 'wk', 'wv', 'wo', 'wb1', 'wb2', 'wg1', 'wg2')}
    del _L0_xattn_all

    def _L0_ffn_setup():
        import jax, jax.numpy as jnp
        import numpy as np
        D_MODEL, D_FF, N_EXPERTS, TOP_K = (128, 256, 8, 2)
        B, S = (2, 256)
        key = jax.random.key(seed)
        ks = jax.random.split(key, 6)
        sd = 1.0 / np.sqrt(D_MODEL)
        sf = 1.0 / np.sqrt(D_FF)
        return {'x': jax.random.normal(ks[0], (B, S, D_MODEL), jnp.float32), 'router_w': jax.random.normal(ks[1], (N_EXPERTS, D_MODEL), jnp.float32) * sd, 'gate_w': jax.random.normal(ks[2], (N_EXPERTS, D_MODEL, D_FF), jnp.float32) * sd, 'gate_b': jnp.zeros((N_EXPERTS, D_FF), jnp.float32), 'up_w': jax.random.normal(ks[3], (N_EXPERTS, D_MODEL, D_FF), jnp.float32) * sd, 'up_b': jnp.zeros((N_EXPERTS, D_FF), jnp.float32), 'down_w': jax.random.normal(ks[4], (N_EXPERTS, D_FF, D_MODEL), jnp.float32) * sf, 'down_b': jnp.zeros((N_EXPERTS, D_MODEL), jnp.float32)}
    _L0_ffn_all = _L0_ffn_setup()
    _L0_ffn_in = {k: v for k, v in _L0_ffn_all.items() if k in ('router_w', 'gate_w', 'gate_b', 'up_w', 'up_b', 'down_w', 'down_b')}
    del _L0_ffn_all

    def _L1_xattn_setup():
        import jax, jax.numpy as jnp
        import numpy as np
        B, T, C, H = (4, 512, 128, 16)
        D = C // H

        def _heads(t):
            b, n, c = t.shape
            return t.reshape(b, n, H, D).transpose(0, 2, 1, 3)
        key = jax.random.key(seed)
        ks = jax.random.split(key, 10)
        s = 1.0 / np.sqrt(C)
        return {'x': jax.random.normal(ks[0], (B, T, C), jnp.float32), 'y': jax.random.normal(ks[1], (B, T, C), jnp.float32), 'Wq': jax.random.normal(ks[2], (C, C), jnp.float32) * s, 'bq': jnp.zeros((C,), jnp.float32), 'Wk': jax.random.normal(ks[3], (C, C), jnp.float32) * s, 'bk': jnp.zeros((C,), jnp.float32), 'Wv': jax.random.normal(ks[4], (C, C), jnp.float32) * s, 'bv': jnp.zeros((C,), jnp.float32), 'Wp': jax.random.normal(ks[5], (C, C), jnp.float32) * s, 'bp': jnp.zeros((C,), jnp.float32)}
    _L1_xattn_all = _L1_xattn_setup()
    _L1_xattn_in = {k: v for k, v in _L1_xattn_all.items() if k in ('Wq', 'bq', 'Wk', 'bk', 'Wv', 'bv', 'Wp', 'bp')}
    del _L1_xattn_all

    def _L1_ffn_setup():
        import jax, jax.numpy as jnp
        import numpy as np
        key = jax.random.key(seed)
        k0, k1, k2, k3 = jax.random.split(key, 4)
        B, S, D, F, E = (8, 256, 128, 256, 8)
        x = jax.random.normal(k0, (B, S, D), dtype=jnp.float32)
        Wg = jax.random.normal(k1, (D, E), dtype=jnp.float32) * 0.02
        W1 = jax.random.normal(k2, (E, D, F), dtype=jnp.float32) * 0.02
        W2 = jax.random.normal(k3, (E, F, D), dtype=jnp.float32) * 0.02
        return {'x': x, 'Wg': Wg, 'W1': W1, 'W2': W2}
    _L1_ffn_all = _L1_ffn_setup()
    _L1_ffn_in = {k: v for k, v in _L1_ffn_all.items() if k in ('Wg', 'W1', 'W2')}
    del _L1_ffn_all
    return {'x': x, 'ctx_1024': ctx_1024, 'mask_1x1xSxS2_bf1': mask_1x1xSxS2_bf1, 'g_xattn': g_xattn, 'g_ffn': g_ffn, 'L0_xattn_wq': _L0_xattn_in['wq'], 'L0_xattn_wk': _L0_xattn_in['wk'], 'L0_xattn_wv': _L0_xattn_in['wv'], 'L0_xattn_wo': _L0_xattn_in['wo'], 'L0_xattn_wb1': _L0_xattn_in['wb1'], 'L0_xattn_wb2': _L0_xattn_in['wb2'], 'L0_xattn_wg1': _L0_xattn_in['wg1'], 'L0_xattn_wg2': _L0_xattn_in['wg2'], 'L0_ffn_router_w': _L0_ffn_in['router_w'], 'L0_ffn_gate_w': _L0_ffn_in['gate_w'], 'L0_ffn_gate_b': _L0_ffn_in['gate_b'], 'L0_ffn_up_w': _L0_ffn_in['up_w'], 'L0_ffn_up_b': _L0_ffn_in['up_b'], 'L0_ffn_down_w': _L0_ffn_in['down_w'], 'L0_ffn_down_b': _L0_ffn_in['down_b'], 'L1_xattn_Wq': _L1_xattn_in['Wq'], 'L1_xattn_bq': _L1_xattn_in['bq'], 'L1_xattn_Wk': _L1_xattn_in['Wk'], 'L1_xattn_bk': _L1_xattn_in['bk'], 'L1_xattn_Wv': _L1_xattn_in['Wv'], 'L1_xattn_bv': _L1_xattn_in['bv'], 'L1_xattn_Wp': _L1_xattn_in['Wp'], 'L1_xattn_bp': _L1_xattn_in['bp'], 'L1_ffn_Wg': _L1_ffn_in['Wg'], 'L1_ffn_W1': _L1_ffn_in['W1'], 'L1_ffn_W2': _L1_ffn_in['W2']}

def reference(x, ctx_1024, mask_1x1xSxS2_bf1, g_xattn, g_ffn, L0_xattn_wq, L0_xattn_wk, L0_xattn_wv, L0_xattn_wo, L0_xattn_wb1, L0_xattn_wb2, L0_xattn_wg1, L0_xattn_wg2, L0_ffn_router_w, L0_ffn_gate_w, L0_ffn_gate_b, L0_ffn_up_w, L0_ffn_up_b, L0_ffn_down_w, L0_ffn_down_b, L1_xattn_Wq, L1_xattn_bq, L1_xattn_Wk, L1_xattn_bk, L1_xattn_Wv, L1_xattn_bv, L1_xattn_Wp, L1_xattn_bp, L1_ffn_Wg, L1_ffn_W1, L1_ffn_W2):
    import jax
    import jax.numpy as jnp

    def _L0_xattn_ref(query, key, value, allowed_mask, wq, wk, wv, wo, wb1, wb2, wg1, wg2, n_context):
        import jax, jax.numpy as jnp
        import numpy as np
        H = 16
        HID = 64

        def _gelu(x):
            return jax.nn.gelu(x, approximate=False)
        B, N, D = query.shape
        Dh = D // H

        def split_heads(x):
            return x.reshape(B, N, H, Dh).transpose(0, 2, 1, 3)
        q = split_heads(query @ wq.T)
        k = split_heads(key @ wk.T)
        v = split_heads(value @ wv.T)
        log_n = jnp.log(jnp.asarray(n_context, jnp.float32))
        base = (_gelu(log_n * wb1[:, 0]) @ wb2.T).reshape(1, H, 1, Dh)
        gate = 1.0 + jnp.tanh(_gelu(q @ wg1.T) @ wg2.T)
        q = q * base * gate
        scores = jnp.einsum('bhnd,bhmd->bhnm', q, k) / jnp.sqrt(jnp.float32(Dh))
        scores = jnp.where(allowed_mask, scores, -jnp.inf)
        attn = jax.nn.softmax(scores, axis=-1)
        out = jnp.einsum('bhnm,bhmd->bhnd', attn, v)
        out = out.transpose(0, 2, 1, 3).reshape(B, N, D)
        return out @ wo.T

    def _L0_ffn_ref(x, router_w, gate_w, gate_b, up_w, up_b, down_w, down_b):
        import jax, jax.numpy as jnp
        import numpy as np
        D_MODEL, D_FF, N_EXPERTS, TOP_K = (128, 256, 8, 2)
        B, S = (2, 256)
        b, s, d = x.shape
        xf = x.reshape(b * s, d)
        n = xf.shape[0]
        router_logits = xf @ router_w.T
        probs = jax.nn.softmax(router_logits, axis=-1)
        topv, topi = jax.lax.top_k(probs, TOP_K)
        mask = jnp.zeros_like(probs).at[jnp.arange(n)[:, None], topi].set(1.0)
        probs = probs * mask
        probs = probs / (probs.sum(axis=-1, keepdims=True) + 1e-09)
        g = jnp.einsum('nd,edf->nef', xf, gate_w) + gate_b
        u = jnp.einsum('nd,edf->nef', xf, up_w) + up_b
        h = jax.nn.silu(g) * u
        expert_out = jnp.einsum('nef,efd->ned', h, down_w) + down_b
        y = jnp.einsum('ne,ned->nd', probs, expert_out)
        return y.reshape(b, s, d)

    def _L1_xattn_ref(x, y, Wq, bq, Wk, bk, Wv, bv, Wp, bp):
        import jax, jax.numpy as jnp
        import numpy as np
        B, T, C, H = (4, 512, 128, 16)
        D = C // H

        def _heads(t):
            b, n, c = t.shape
            return t.reshape(b, n, H, D).transpose(0, 2, 1, 3)
        q = jax.nn.softmax(_heads(x @ Wq.T + bq), axis=-1)
        k = jax.nn.softmax(_heads(y @ Wk.T + bk), axis=-1)
        v = _heads(y @ Wv.T + bv)
        k_cumsum = jnp.sum(k, axis=-2, keepdims=True)
        D_inv = 1.0 / jnp.sum(q * k_cumsum, axis=-1, keepdims=True)
        kv = jnp.einsum('bhnd,bhne->bhde', k, v)
        out = q + jnp.einsum('bhnd,bhde->bhne', q, kv) * D_inv
        out = out.transpose(0, 2, 1, 3).reshape(x.shape[0], x.shape[1], C)
        return out @ Wp.T + bp

    def _L1_ffn_ref(x, Wg, W1, W2):
        import jax, jax.numpy as jnp
        import numpy as np
        B, S, D = x.shape
        E = Wg.shape[1]
        T = B * S
        cap = max(1, T // E)
        xt = x.reshape(T, D)
        logits = xt @ Wg
        probs = jax.nn.softmax(logits, axis=-1)
        pT = probs.T
        _, top_idx = jax.lax.top_k(pT, cap)
        sel = jnp.zeros((E, T), dtype=bool).at[jnp.arange(E)[:, None], top_idx].set(True)
        masked = jnp.where(sel, pT, -jnp.inf)
        assigned = sel.any(axis=0)
        tok2exp = jnp.where(assigned, jnp.argmax(masked, axis=0), jnp.argmax(pT, axis=0))
        weights = jnp.take_along_axis(probs, tok2exp[:, None], axis=1)[:, 0]
        out = jnp.zeros_like(xt)
        for e in range(E):
            gate = jnp.where(tok2exp == e, weights, 0.0)
            h = jax.nn.gelu(xt @ W1[e], approximate=False) @ W2[e]
            out = out + gate[:, None] * h
        return out.reshape(B, S, D)
    x = x + jnp.tanh(g_xattn[0]) * _L0_xattn_ref(_layernorm(x, axis=-1), ctx_1024, ctx_1024, mask_1x1xSxS2_bf1, L0_xattn_wq, L0_xattn_wk, L0_xattn_wv, L0_xattn_wo, L0_xattn_wb1, L0_xattn_wb2, L0_xattn_wg1, L0_xattn_wg2, 256)
    x = x + jnp.tanh(g_ffn[0]) * _L0_ffn_ref(_layernorm(x, axis=-1), L0_ffn_router_w, L0_ffn_gate_w, L0_ffn_gate_b, L0_ffn_up_w, L0_ffn_up_b, L0_ffn_down_w, L0_ffn_down_b)
    x = x + jnp.tanh(g_xattn[1]) * _L1_xattn_ref(_layernorm(x, axis=-1), ctx_1024, L1_xattn_Wq, L1_xattn_bq, L1_xattn_Wk, L1_xattn_bk, L1_xattn_Wv, L1_xattn_bv, L1_xattn_Wp, L1_xattn_bp)
    x = x + jnp.tanh(g_ffn[1]) * _L1_ffn_ref(_layernorm(x, axis=-1), L1_ffn_Wg, L1_ffn_W1, L1_ffn_W2)
    return x

_drawn_inputs = setup_inputs


def setup_inputs(seed=0):
    import zlib

    import numpy as np

    out = dict(_drawn_inputs(seed))
    spreads = {'g_ffn': (-1.0, 0.6),
     'L0_ffn_gate_b': (0.0, 0.32),
     'L0_ffn_up_b': (0.0, 0.322),
     'L0_ffn_down_b': (0.0, 0.1),
     'L1_xattn_bq': (0.0, 0.761),
     'L1_xattn_bk': (0.0, 0.8),
     'L1_xattn_bv': (0.0, 0.1),
     'L1_xattn_bp': (0.0, 0.1)}
    factors = {'L1_ffn_Wg': 8.0, 'L1_ffn_W1': 8.0, 'L1_ffn_W2': 8.0}
    for name, (base, spread) in spreads.items():
        noise = np.random.default_rng([zlib.crc32(name.encode()), seed]).standard_normal(out[name].shape)
        drawn = base * np.exp(spread * noise) if base else spread * noise
        out[name] = jnp.asarray(drawn.astype(out[name].dtype))
    for name, factor in factors.items():
        out[name] = (out[name] * factor).astype(out[name].dtype)
    return out
```

```python
import concourse.bass as bass
from concourse import mybir
from contextlib import ExitStack

P = 128
NB = 16
D = 128
H = 16
DH = D // H
HQ = 4
HID = 64
NCH = 4
TPC = NB // NCH
CH = TPC * P
NE = 8
FF = 256
NF = FF // P
CAP = NB * P // NE
EPS = 1e-5
MASKED = -1e30
THRESHOLD_BITS = 30

C_IDENT, C_BLOCK, C_SUM16, C_TRI16 = 0, 128, 256, 384
C_HEAD, C_QUAD, C_KEY, C_END = 512, 528, 532, 540
W_Q0, W_K0, W_V0, W_O0, W_Q1, W_K1, W_V1, W_P1 = range(8)


class Count:

    def __init__(self, engine, semaphore):
        self.engine, self.semaphore, self.base, self.k = engine, semaphore, 0, 0

    def done(self, instruction):
        self.k += 1
        return instruction.then_inc(self.semaphore, 1)

    def wait(self):
        self.engine.wait_ge(self.semaphore, self.base + self.k)

    def enter(self, index, per):
        self.start, self.base, self.k = self.base + self.k, self.base + self.k + index * per, 0
        self.per = per

    def leave(self, iterations):
        assert self.k == self.per, (self.k, self.per)
        self.base, self.k = self.start + iterations * self.per, 0


def build(nc, i, out):
    fp32, bf16, i32 = mybir.dt.float32, mybir.dt.bfloat16, mybir.dt.int32
    ALU, ACT, AX = mybir.AluOpType, mybir.ActivationFunctionType, mybir.AxisListType
    ctx = ExitStack()
    with ctx:
        def sb(name, shape, dt=fp32):
            return ctx.enter_context(nc.sbuf_tensor(name, shape, dt))

        def sem(name):
            return ctx.enter_context(nc.semaphore(name))

        x = sb("x", [P, NB, D])
        cst = sb("cst", [P, C_END])
        w = sb("w", [P, 8 * D])
        wg1 = sb("wg1", [P, 2, P])
        wg2 = sb("wg2", [P, 2, 32])
        wb = sb("wb", [HID, D + 1])
        routers = sb("routers", [P, 2, NE])
        rows = sb("rows", [P, 4 * D + 4])
        mask_u8 = sb("mask_u8", [P, 2, P], mybir.dt.uint8)
        gate_w = sb("gate_w", [P, NE, FF])
        up_w = sb("up_w", [P, NE, FF])
        down_w = sb("down_w", [P, NE, NF, D])
        ffn_b = sb("ffn_b", [P, 2, NE, NF])
        down_b = sb("down_b", [NE, D])
        w1 = sb("w1", [P, NE, FF])
        w2 = sb("w2", [P, NE, NF, D])
        ident_b = sb("ident_b", [P, P], bf16)
        mask_b = sb("mask_b", [P, 2, P], bf16)
        mask_f = sb("mask_f", [P, 2, P])
        visible = sb("visible", [P, 2])
        tg = sb("tg", [P, 4])
        base_h = sb("base_h", [HID, 1])
        kscale = sb("kscale", [P, 1])
        minus_half = sb("minus_half", [P, TPC])
        stats = sb("stats", [P, TPC, 6])
        mv = sb("mv", [P, TPC, 3])
        var_eps = sb("var_eps", [P, TPC])
        rstd = sb("rstd", [P, TPC])
        xn = sb("xn", [P, TPC, D])
        xnT = sb("xnT", [P, CH])
        xnT_all = sb("xnT_all", [P, NB * P])
        ctxT = sb("ctxT", [P, CH])
        qT = sb("qT", [P, CH])
        hid = sb("hid", [P, 2 * HQ, CH])
        gate = sb("gate", [P, CH])
        qg_all = sb("qg_all", [P, NB * P])
        k_all = sb("k_all", [P, NB * P])
        v_all = sb("v_all", [P, NB, H, DH])
        q_st = sb("q_st", [P, 2, P], bf16)
        k_st = sb("k_st", [P, 2, P])
        q_bd = sb("q_bd", [P, 2, HQ, P])
        k_bd = sb("k_bd", [P, 2, HQ, P], bf16)
        v_st = sb("v_st", [P, 2, H, 32])
        nmax = sb("nmax", [P, 2, H], bf16)
        pT = sb("pT", [P, H, P])
        avT = sb("avT", [P, CH])
        rsum = sb("rsum", [P, H])
        rinv = sb("rinv", [P, H])
        ao = sb("ao", [P, D])
        aoT = sb("aoT", [P, P])
        silu = sb("silu", [P, NF, CH])
        hT = sb("hT", [P, 2, NF, CH])
        acc = sb("acc", [P, TPC, D])
        wexp = sb("wexp", [P, NB, NE])
        wT = sb("wT", [NE, CH])
        logit = sb("logit", [P, TPC, NE])
        r1 = sb("r1", [P, TPC, NE])
        r2 = sb("r2", [P, TPC, NE])
        sel1 = sb("sel1", [P, TPC, NE])
        rm = sb("rm", [P, TPC])
        rm2 = sb("rm2", [P, TPC])
        ql = sb("ql", [P, 2, TPC * H, DH])
        qm = sb("qm", [P, 2, TPC * H])
        vl = sb("vl", [P, TPC, D + 1])
        kvd = sb("kvd", [P, TPC, D + H])
        qnT = sb("qnT", [P, CH])
        dinv = sb("dinv", [P, TPC, H])
        lo = sb("lo", [P, TPC, D])
        probs = sb("probs", [P, NE, NB])
        pS = sb("pS", [P, P])
        ind = sb("ind", [P, P])
        ind2 = sb("ind2", [P, P])
        scan = sb("scan", [P, P])
        thr = sb("thr", [P, 1], i32)
        cand = sb("cand", [P, 1], i32)
        inc = sb("inc", [P, 1], i32)
        cnt = sb("cnt", [P, 2])
        need = sb("need", [P, 1])
        off = sb("off", [P, 1])
        selT = sb("selT", [P, P])
        c1 = sb("c1", [P, NE, NB])
        c2 = sb("c2", [P, NE, NB])
        cm = sb("cm", [P, NB])
        gates = sb("gates", [P, NE, NB])

        ps = ctx.enter_context(nc.psum_tensor("ps", [P, 8, 512], fp32))

        def bank(n, parts=TPC):
            return ps[:, n, :].rearrange("p (t n) -> p t n", t=parts)

        ident = cst[:, C_IDENT:C_IDENT + P]
        block_mask = cst[:, C_BLOCK:C_BLOCK + P]
        sum16 = cst[:, C_SUM16:C_SUM16 + P]
        tri16 = cst[:, C_TRI16:C_TRI16 + P]
        head_sel = cst[:, C_HEAD:C_HEAD + H]
        quad_sel = cst[:, C_QUAD:C_QUAD + HQ]
        key = cst[:, C_KEY:C_KEY + NE]

        def square(n):
            return w[:, n * D:(n + 1) * D]

        ld_x, ld_w, ld_ffn, ld_ctx = sem("ld_x"), sem("ld_w"), sem("ld_ffn"), sem("ld_ctx")
        stored = sem("stored")
        dve_step, pool_step, act_step = sem("dve_step"), sem("pool_step"), sem("act_step")
        base_hidden, base_out, set_up, tanh_g = sem("base_hidden"), sem("base_out"), sem("set_up"), sem("tanh_g")
        ln_var, ln_rstd, ln_xn, ln_T, ln_Ts = (sem(n) for n in ("ln_var", "ln_rstd", "ln_xn", "ln_T", "ln_Ts"))
        a_q, a_k, a_v, a_qs, a_ks, a_vs = (sem(n) for n in ("a_q", "a_k", "a_v", "a_qs", "a_ks", "a_vs"))
        a_hid, a_gelu, a_gate, a_tanh, a_qg = (sem(n) for n in ("a_hid", "a_gelu", "a_gate", "a_tanh", "a_qg"))
        b_prep, b_sn, b_max, b_st, b_exp = (sem(n) for n in ("b_prep", "b_sn", "b_max", "b_st", "b_exp"))
        b_av, b_avs, b_nat, b_ao, b_aoT, b_aoTs, b_y, b_x = (
            sem(n) for n in ("b_av", "b_avs", "b_nat", "b_ao", "b_aoT", "b_aoTs", "b_y", "b_x"))
        c_logit, c_w, c_wT, c_wTs, c_bias, c_acc0 = (sem(n) for n in ("c_logit", "c_w", "c_wT", "c_wTs", "c_bias", "c_acc0"))
        c_gate, c_up, c_silu, c_h, c_down, c_acc, c_x = (sem(n) for n in ("c_gate", "c_up", "c_silu", "c_h", "c_down", "c_acc", "c_x"))
        d_q, d_k, d_v, d_qsh, d_ksh, d_qe, d_ke, d_qn, d_kn, d_vs = (
            sem(n) for n in ("d_q", "d_k", "d_v", "d_qsh", "d_ksh", "d_qe", "d_ke", "d_qn", "d_kn", "d_vs"))
        d_kv, d_kvd, d_qT, d_qTs, d_num, d_o, d_oT, d_oTs, d_y, d_x = (
            sem(n) for n in ("d_kv", "d_kvd", "d_qT", "d_qTs", "d_num", "d_o", "d_oT", "d_oTs", "d_y", "d_x"))
        e_logit, e_shift, e_exp, e_p, e_pT, e_cnt, e_tot, e_ties, e_tie_tot, e_sel, e_selT, e_gates = (
            sem(n) for n in ("e_logit", "e_shift", "e_exp", "e_p", "e_pT", "e_cnt", "e_tot", "e_ties",
                             "e_tie_tot", "e_sel", "e_selT", "e_gates"))
        c_shift, c_exp = sem("c_shift"), sem("c_exp")
        e_h, e_gelu, e_down, e_acc, e_x = (sem(n) for n in ("e_h", "e_gelu", "e_down", "e_acc", "e_x"))
        block = ctx.enter_context(nc.Block())

        N_X, N_W, N_FFN = 16, 9 * 16, 7 * 16

        @block.sync
        def _(sp):
            sp.dma_start(cst[:, :], i["cst"]).then_inc(ld_w, 16)
            sp.dma_start(x[:, :, :], i["x"].rearrange("b p d -> p b d")).then_inc(ld_x, 16)
            sp.dma_start(ctxT[:, :], i["ctxT"][:, 0:CH]).then_inc(ld_ctx, 16)
            sp.dma_start(w[:, :], i["w"]).then_inc(ld_w, 16)
            sp.dma_start(wg1[:, :, :], i["wg1"]).then_inc(ld_w, 16)
            sp.dma_start(wg2[:, :, :], i["wg2"]).then_inc(ld_w, 16)
            sp.dma_start(wb[:, :], i["wb"]).then_inc(ld_w, 16)
            sp.dma_start(rows[:, :], i["rows"].broadcast_to([P, 4 * D + 4])).then_inc(ld_w, 16)
            sp.dma_start(mask_u8[:, :, :], i["mask"]).then_inc(ld_w, 16)
            sp.dma_start(routers[:, :, :], i["routers"]).then_inc(ld_w, 16)
            sp.dma_start(down_b[:, :], i["down_b"]).then_inc(ld_w, 16)
            sp.dma_start(gate_w[:, :, :], i["gate_w"].rearrange("e d f -> d e f")).then_inc(ld_ffn, 16)
            sp.dma_start(up_w[:, :, :], i["up_w"].rearrange("e d f -> d e f")).then_inc(ld_ffn, 16)
            sp.dma_start(down_w[:, :, :, :], i["down_w"].rearrange("e (f p) d -> p e f d", p=P)).then_inc(ld_ffn, 16)
            sp.dma_start(ffn_b[:, 0], i["gate_b"].rearrange("p (e f) -> p e f", e=NE)).then_inc(ld_ffn, 16)
            sp.dma_start(ffn_b[:, 1], i["up_b"].rearrange("p (e f) -> p e f", e=NE)).then_inc(ld_ffn, 16)
            sp.dma_start(w1[:, :, :], i["w1"].rearrange("e d f -> d e f")).then_inc(ld_ffn, 16)
            sp.dma_start(w2[:, :, :, :], i["w2"].rearrange("e (f p) d -> p e f d", p=P)).then_inc(ld_ffn, 16)
            with sp.Fori(1, NCH) as c:
                sp.wait_ge(a_v, c)
                sp.dma_start(ctxT[:, :], i["ctxT"][:, bass.ds(c * CH, CH)]).then_inc(ld_ctx, 16)
            sp.wait_ge(a_v, NCH)
            sp.dma_start(ctxT[:, :], i["ctxT"][:, 0:CH]).then_inc(ld_ctx, 16)
            with sp.Fori(1, NCH) as c:
                sp.wait_ge(d_v, c)
                sp.dma_start(ctxT[:, :], i["ctxT"][:, bass.ds(c * CH, CH)]).then_inc(ld_ctx, 16)
            with sp.Fori(0, NCH) as c:
                sp.wait_ge(e_x, c + 1)
                sp.dma_start(out.rearrange("b p d -> p b d")[:, bass.ds(c * TPC, TPC), :],
                             x[:, bass.ds(c * TPC, TPC), :]).then_inc(stored, 16)
            sp.wait_ge(stored, 16 * NCH)

        @block.gpsimd
        def _(pool):
            step = Count(pool, pool_step)
            step.done(nc.gpsimd.memset(minus_half[:, :], -0.5))
            nc.gpsimd.memset(v_st[:, :, :, :], 0.0).then_inc(pool_step, 1)
            step.k += 1
            step.wait()
            step.done(nc.gpsimd.memset(v_st[:, :, :, DH:DH + 1], 1.0))
            step.wait()

            def layer_norm(k):
                pool.wait_ge(ln_var, k + 1)
                nc.gpsimd.tensor_tensor(rstd[:, :], var_eps[:, :], minus_half[:, :], ALU.pow).then_inc(ln_rstd, 1)

            with pool.Fori(0, NCH) as c:
                layer_norm(c)

            pool.wait_ge(ld_w, N_W)
            pool.wait_ge(a_qg, NCH)
            pool.wait_ge(a_ks, NCH)
            pool.wait_ge(a_vs, NCH)

            def prepare(b, s):
                tok = bass.ds(b * P, P)
                nc.gpsimd.tensor_copy(q_st[:, s, :], qg_all[:, tok]).then_inc(b_prep, 1)
                nc.gpsimd.tensor_tensor(
                    k_bd[:, s], k_all[:, tok].unsqueeze(1).broadcast_to([P, HQ, P]),
                    quad_sel.unsqueeze(2).broadcast_to([P, HQ, P]), ALU.mult).then_inc(b_prep, 1)
                nc.gpsimd.tensor_copy(k_st[:, s, :], k_all[:, tok]).then_inc(b_prep, 1)
                nc.gpsimd.tensor_tensor(
                    q_bd[:, s], qg_all[:, tok].unsqueeze(1).broadcast_to([P, HQ, P]),
                    quad_sel.unsqueeze(2).broadcast_to([P, HQ, P]), ALU.mult).then_inc(b_prep, 1)
                nc.gpsimd.tensor_copy(v_st[:, s, :, 0:DH], v_all[:, b]).then_inc(b_prep, 1)

            prepare(0, 0)
            prepare(1, 1)
            with pool.Fori(1, NB // 2) as g:
                for s in range(2):
                    b = 2 * g + s
                    pool.wait_ge(b_av, b - 1)
                    prepare(b, s)

            with pool.Fori(NCH, 4 * NCH) as k:
                layer_norm(k)

        @block.vector
        def _(dve):
            step = Count(dve, dve_step)
            dve.wait_ge(ld_w, N_W)
            nc.vector.tensor_copy(ident_b[:, :], ident).then_inc(set_up, 1)
            step.done(nc.vector.tensor_copy(mask_f[:, :, :], mask_u8[:, :, :]))
            step.wait()
            nc.vector.tensor_scalar(mask_b[:, :, :], mask_f[:, :, :], -1.0, -MASKED, ALU.add, ALU.mult).then_inc(set_up, 1)
            step.done(nc.vector.tensor_reduce(visible[:, 0:1], mask_f[:, 0, :], AX.X, ALU.add))
            step.wait()
            step.done(nc.vector.reciprocal(visible[:, 0:1], visible[:, 0:1]))
            step.wait()
            step.done(nc.vector.tensor_scalar(visible[:, 1:2], visible[:, 0:1], 0.0, None, ALU.mult))
            dve.wait_ge(base_out, 1)
            step.done(nc.vector.tensor_scalar(kscale[:, :], ps[:, 0, 0:1], float(DH) ** -0.5, None, ALU.mult))
            step.wait()
            dve.wait_ge(ld_x, N_X)

            def layer_norm(k, tile):
                for t in range(TPC):
                    step.done(nc.vector.bn_stats(stats[:, t, :], x[:, tile + t, :]))
                step.wait()
                even, odd = stats[:, :, 0:3], stats[:, :, 3:6]
                step.done(nc.vector.tensor_tensor(mv[:, :, 0], even[:, :, 1], odd[:, :, 1], ALU.add))
                step.done(nc.vector.tensor_tensor(mv[:, :, 1], even[:, :, 1], odd[:, :, 1], ALU.subtract))
                step.done(nc.vector.tensor_tensor(mv[:, :, 2], even[:, :, 2], odd[:, :, 2], ALU.add))
                step.wait()
                step.done(nc.vector.tensor_scalar(mv[:, :, 0], mv[:, :, 0], 0.5, None, ALU.mult))
                step.done(nc.vector.scalar_tensor_tensor(mv[:, :, 1], mv[:, :, 1], 0.25, mv[:, :, 1], ALU.mult, ALU.mult))
                step.done(nc.vector.tensor_scalar(mv[:, :, 2], mv[:, :, 2], 1.0 / D, EPS, ALU.mult, ALU.add))
                step.wait()
                nc.vector.tensor_tensor(var_eps[:, :], mv[:, :, 1], mv[:, :, 2], ALU.add).then_inc(ln_var, 1)
                dve.wait_ge(ln_rstd, k + 1)
                for t in range(TPC):
                    nc.vector.tensor_scalar(xn[:, t, :], x[:, tile + t, :], mv[:, t, 0:1], rstd[:, t:t + 1],
                                            ALU.subtract, ALU.mult).then_inc(ln_xn, 1)

            LN_STEPS = TPC + 6

            with dve.Fori(0, NCH) as c:
                step.enter(c, LN_STEPS)
                layer_norm(c, c * TPC)
                dve.wait_ge(a_k, c + 1)
                nc.vector.tensor_scalar(k_all[:, bass.ds(c * CH, CH)], ps[:, 2, :], kscale[:, 0:1], None,
                                        ALU.mult).then_inc(a_ks, 1)
                dve.wait_ge(a_tanh, c + 1)
                nc.vector.scalar_tensor_tensor(qg_all[:, bass.ds(c * CH, CH)], gate[:, :], 1.0, qT[:, :],
                                               ALU.add, ALU.mult).then_inc(a_qg, 1)
                step.leave(NCH)

            def maximum(b, s, g):
                dve.wait_ge(b_sn, 4 * b + g + 1)
                nc.vector.tensor_reduce(nmax[:, s, HQ * g:HQ * (g + 1)], bank(g % 2), AX.X, ALU.max,
                                        negate=True).then_inc(b_max, 1)

            def normalise(b):
                dve.wait_ge(b_nat, b + 1)
                av = ps[:, 7, :].rearrange("p (h d) -> p h d", h=H)
                step.done(nc.vector.tensor_scalar(rsum[:, :], av[:, :, DH], visible[:, 1:2], None, ALU.add))
                step.wait()
                step.done(nc.vector.reciprocal(rinv[:, :], rsum[:, :]))
                step.wait()
                nc.vector.tensor_tensor(ao[:, :].rearrange("p (a j d) -> p a j d", a=HQ, j=HQ), ps[:, 7, :].rearrange(
                    "p (a j d) -> p a j d", a=HQ, j=HQ)[:, :, :, 0:DH], rinv[:, :].rearrange(
                    "p (a j) -> p a j", a=HQ).unsqueeze(3).broadcast_to([P, HQ, HQ, DH]), ALU.mult).then_inc(b_ao, 1)

            def residual(b):
                dve.wait_ge(b_y, b + 1)
                nc.vector.scalar_tensor_tensor(x[:, b, :], ps[:, 7, P:2 * P], tg[:, 0:1], x[:, b, :],
                                               ALU.mult, ALU.add).then_inc(b_x, 1)

            def slot(b, s, last=False):
                normalise(b - 1)
                if not last:
                    maximum(b + 1, 1 - s, 0)
                    maximum(b + 1, 1 - s, 1)
                    maximum(b + 1, 1 - s, 2)
                    maximum(b + 1, 1 - s, 3)
                residual(b - 1)

            dve.wait_ge(tanh_g, 1)
            for b in range(2):
                for g in range(4):
                    maximum(b, b, g)
            slot(1, 1)
            with dve.Fori(1, NB // 2 - 1) as r:
                step.enter(r - 1, 4)
                slot(2 * r, 0)
                slot(2 * r + 1, 1)
                step.leave(NB // 2 - 2)
            slot(NB - 2, 0)
            slot(NB - 1, 1, last=True)
            normalise(NB - 1)
            residual(NB - 1)
            dve.wait_ge(b_x, NB)

            def router(c, e_layer_done=None):
                dve.wait_ge(c_logit, c + 1)
                lg = ps[:, 6, 0:TPC * NE].rearrange("p (t e) -> p t e", t=TPC)

                def wide(a):
                    return a.unsqueeze(2).broadcast_to([P, TPC, NE])

                def keys():
                    return key.unsqueeze(1).broadcast_to([P, TPC, NE])

                def then(instruction):
                    step.done(instruction)
                    step.wait()

                then(nc.vector.tensor_reduce(rm[:, :], lg, AX.X, ALU.max))
                nc.vector.tensor_tensor(logit[:, :, :], lg, wide(rm[:, :]), ALU.subtract).then_inc(c_shift, 1)
                dve.wait_ge(c_exp, c + 1)
                then(nc.vector.tensor_reduce(rm[:, :], r1[:, :, :], AX.X, ALU.add))
                then(nc.vector.reciprocal(rm2[:, :], rm[:, :]))
                then(nc.vector.tensor_tensor(logit[:, :, :], r1[:, :, :], wide(rm2[:, :]), ALU.mult))
                then(nc.vector.tensor_reduce(rm[:, :], logit[:, :, :], AX.X, ALU.max))
                then(nc.vector.tensor_tensor(r1[:, :, :], logit[:, :, :], wide(rm[:, :]), ALU.is_equal))
                then(nc.vector.tensor_tensor(r2[:, :, :], r1[:, :, :], keys(), ALU.mult))
                then(nc.vector.tensor_reduce(rm[:, :], r2[:, :, :], AX.X, ALU.max))
                then(nc.vector.tensor_tensor(sel1[:, :, :], r2[:, :, :], wide(rm[:, :]), ALU.is_equal))
                then(nc.vector.scalar_tensor_tensor(r1[:, :, :], sel1[:, :, :], -2.0, logit[:, :, :], ALU.mult, ALU.add))
                then(nc.vector.tensor_reduce(rm[:, :], r1[:, :, :], AX.X, ALU.max))
                then(nc.vector.tensor_tensor(r2[:, :, :], r1[:, :, :], wide(rm[:, :]), ALU.is_equal))
                then(nc.vector.tensor_tensor(r1[:, :, :], r2[:, :, :], keys(), ALU.mult))
                then(nc.vector.tensor_reduce(rm[:, :], r1[:, :, :], AX.X, ALU.max))
                then(nc.vector.tensor_tensor(r2[:, :, :], r1[:, :, :], wide(rm[:, :]), ALU.is_equal))
                then(nc.vector.tensor_tensor(r1[:, :, :], sel1[:, :, :], r2[:, :, :], ALU.add))
                then(nc.vector.tensor_tensor(r2[:, :, :], r1[:, :, :], logit[:, :, :], ALU.mult))
                then(nc.vector.tensor_reduce(rm[:, :], r2[:, :, :], AX.X, ALU.add))
                then(nc.vector.tensor_scalar(rm2[:, :], rm[:, :], 1e-9, None, ALU.add))
                then(nc.vector.reciprocal(rm[:, :], rm2[:, :]))
                nc.vector.tensor_tensor(r1[:, :, :], r2[:, :, :], wide(rm[:, :]), ALU.mult).then_inc(c_w, 1)
                dve.wait_ge(c_w, 2 * c + 1)
                nc.vector.tensor_copy(wexp[:, bass.ds(c * TPC, TPC), :], r1[:, :, :]).then_inc(c_w, 1)

            ROUTER_STEPS = 20

            def experts(c):
                dve.wait_ge(c_w, 2 * c + 2)
                dve.wait_ge(c_bias, c + 1)
                step.done(nc.vector.tensor_copy(acc[:, :, :], bank(6)))
                for e in range(NE + 1):
                    if e < NE:
                        for f in range(NF):
                            n = NF * e + f
                            dve.wait_ge(c_silu, c * NE * NF + n + 1)
                            dve.wait_ge(c_up, c * NE * NF + n + 1)
                            nc.vector.scalar_tensor_tensor(hT[:, e % 2, f, :], ps[:, 2 + f, :], ffn_b[:, 1, e, f:f + 1],
                                                           silu[:, f, :], ALU.add, ALU.mult).then_inc(c_h, 1)
                    if e:
                        dve.wait_ge(c_down, c * NE + e)
                        step.wait()
                        for t in range(TPC):
                            step.done(nc.vector.scalar_tensor_tensor(
                                acc[:, t, :], ps[:, 4 + (e - 1) % 2, t * P:(t + 1) * P], wexp[:, c * TPC + t, e - 1:e],
                                acc[:, t, :], ALU.mult, ALU.add))
                        step.wait()
                step.wait()
                nc.vector.scalar_tensor_tensor(x[:, bass.ds(c * TPC, TPC), :], acc[:, :, :], tg[:, 2:3],
                                               x[:, bass.ds(c * TPC, TPC), :], ALU.mult, ALU.add).then_inc(c_x, 1)
                dve.wait_ge(c_x, c + 1)

            with dve.Fori(0, NCH) as c:
                step.enter(c, LN_STEPS + ROUTER_STEPS + 1 + NE * TPC)
                layer_norm(NCH + c, c * TPC)
                router(c)
                experts(c)
                step.leave(NCH)

            with dve.Fori(0, NCH) as c:
                step.enter(c, LN_STEPS + 2 * 4 + 2 + 1)
                layer_norm(2 * NCH + c, c * TPC)

                def soften(m, ready, bias, shifted, exped, out_sem):
                    flat = ql[:, m].rearrange("p (t h) d -> p t (h d)", t=TPC)
                    dve.wait_ge(ready, c + 1)
                    step.done(nc.vector.tensor_tensor(flat, bank(m), bias.unsqueeze(1).broadcast_to([P, TPC, D]), ALU.add))
                    step.wait()
                    step.done(nc.vector.tensor_reduce(qm[:, m], ql[:, m], AX.X, ALU.max))
                    step.wait()
                    nc.vector.tensor_tensor(ql[:, m], ql[:, m], qm[:, m].unsqueeze(2).broadcast_to([P, TPC * H, DH]),
                                            ALU.subtract).then_inc(shifted, 1)
                    dve.wait_ge(exped, c + 1)
                    step.done(nc.vector.tensor_reduce(qm[:, m], ql[:, m], AX.X, ALU.add))
                    step.wait()
                    step.done(nc.vector.reciprocal(qm[:, m], qm[:, m]))
                    step.wait()
                    nc.vector.tensor_tensor(ql[:, m], ql[:, m], qm[:, m].unsqueeze(2).broadcast_to([P, TPC * H, DH]),
                                            ALU.mult).then_inc(out_sem, 1)

                dve.wait_ge(d_v, c + 1)
                if True:
                    nc.vector.tensor_tensor(vl[:, :, 0:D], bank(2), rows[:, 2 * D:3 * D].unsqueeze(1).broadcast_to([P, TPC, D]),
                                            ALU.add).then_inc(d_vs, 1)
                    nc.vector.memset(vl[:, :, D:D + 1], 1.0).then_inc(d_vs, 1)
                soften(1, d_k, rows[:, D:2 * D], d_ksh, d_ke, d_kn)
                soften(0, d_q, rows[:, 0:D], d_qsh, d_qe, d_qn)
                dve.wait_ge(d_kv, c + 1)
                for t in range(TPC):
                    kv = ps[:, 3 + t // 2, (t % 2) * 256:(t % 2) * 256 + D + 1]
                    nc.vector.tensor_tensor(kvd[:, t, 0:D], kv[:, 0:D], block_mask, ALU.mult).then_inc(d_kvd, 1)
                    nc.vector.tensor_scalar(kvd[:, t, D:D + H], head_sel, kv[:, D:D + 1], None, ALU.mult).then_inc(d_kvd, 1)
                dve.wait_ge(d_num, c + 1)
                for t in range(2):
                    two = ps[:, 5 + t, :].rearrange("p (t n) -> p t n", t=2)
                    step.done(nc.vector.reciprocal(dinv[:, 2 * t:2 * t + 2, :], two[:, :, D:D + H]))
                step.wait()
                for t in range(TPC):
                    nc.vector.tensor_tensor(
                        lo[:, t, :].rearrange("p (h d) -> p h d", h=H),
                        ps[:, 5 + t // 2, (t % 2) * 256:(t % 2) * 256 + D].rearrange("p (h d) -> p h d", h=H),
                        dinv[:, t, :].unsqueeze(2).broadcast_to([P, H, DH]), ALU.mult).then_inc(d_o, 1)
                dve.wait_ge(d_o, (c + 1) * (TPC + 1) - 1)
                nc.vector.tensor_tensor(lo[:, :, :], lo[:, :, :], ql[:, 0].rearrange("p (t h) d -> p t (h d)", t=TPC),
                                        ALU.add).then_inc(d_o, 1)
                dve.wait_ge(d_y, c + 1)
                step.done(nc.vector.tensor_tensor(acc[:, :, :], bank(7), rows[:, 3 * D:4 * D].unsqueeze(1).broadcast_to([P, TPC, D]),
                                                  ALU.add))
                step.wait()
                nc.vector.scalar_tensor_tensor(x[:, bass.ds(c * TPC, TPC), :], acc[:, :, :], tg[:, 1:2],
                                               x[:, bass.ds(c * TPC, TPC), :], ALU.mult, ALU.add).then_inc(d_x, 1)
                dve.wait_ge(d_x, c + 1)
                step.leave(NCH)

            with dve.Fori(0, NCH) as c:
                step.enter(c, LN_STEPS + 3)
                layer_norm(3 * NCH + c, c * TPC)
                dve.wait_ge(e_logit, c + 1)
                lg = ps[:, 6, 0:TPC * NE].rearrange("p (t e) -> p t e", t=TPC)
                step.done(nc.vector.tensor_reduce(rm[:, :], lg, AX.X, ALU.max))
                step.wait()
                nc.vector.tensor_tensor(logit[:, :, :], lg, rm[:, :].unsqueeze(2).broadcast_to([P, TPC, NE]),
                                        ALU.subtract).then_inc(e_shift, 1)
                dve.wait_ge(e_exp, c + 1)
                step.done(nc.vector.tensor_reduce(rm[:, :], r1[:, :, :], AX.X, ALU.add))
                step.wait()
                step.done(nc.vector.reciprocal(rm2[:, :], rm[:, :]))
                step.wait()
                nc.vector.tensor_tensor(probs[:, :, bass.ds(c * TPC, TPC)], r1[:, :, :].rearrange("p t e -> p e t"),
                                        rm2[:, :].unsqueeze(1).broadcast_to([P, NE, TPC]), ALU.mult).then_inc(e_p, 1)
                step.leave(NCH)

            def then(instruction):
                step.done(instruction)
                step.wait()

            dve.wait_ge(e_pT, 1)
            step.done(nc.vector.tensor_copy(pS[:, :], ps[:, 0, 0:P]))
            step.done(nc.vector.memset(thr[:, :], 0))
            step.wait()
            for n in range(THRESHOLD_BITS):
                bit = 1 << (THRESHOLD_BITS - 1 - n)
                then(nc.vector.tensor_scalar(cand[:, :], thr[:, :], bit, None, ALU.bitwise_or))
                nc.vector.tensor_scalar(ind[:, :], pS[:, :], cand[:, :].bitcast(fp32), 0.0, ALU.is_ge, ALU.add,
                                        accum_out=cnt[:, 0:1]).then_inc(e_cnt, 1)
                dve.wait_ge(e_tot, n + 1)
                then(nc.vector.tensor_scalar(inc[:, :], ps[:, 1, 0:1], CAP - 0.5, float(bit), ALU.is_ge, ALU.mult))
                then(nc.vector.tensor_tensor(thr[:, :], thr[:, :], inc[:, :], ALU.bitwise_or))
            level = thr[:, :].bitcast(fp32)
            then(nc.vector.tensor_scalar(ind[:, :], pS[:, :], level, 0.0, ALU.is_gt, ALU.add, accum_out=cnt[:, 0:1]))
            nc.vector.tensor_scalar(ind2[:, :], pS[:, :], level, 0.0, ALU.is_equal, ALU.add,
                                    accum_out=cnt[:, 1:2]).then_inc(e_ties, 1)
            dve.wait_ge(e_ties, 1)
            then(nc.vector.tensor_tensor_scan(scan[:, :], ind2[:, :], ind2[:, :], 0.0, ALU.add, ALU.bypass))
            dve.wait_ge(e_tie_tot, 1)
            then(nc.vector.tensor_scalar(need[:, :], ps[:, 2, 0:1], -1.0, CAP + 0.5, ALU.mult, ALU.add))
            then(nc.vector.tensor_tensor(off[:, :], need[:, :], ps[:, 2, 1:2], ALU.subtract))
            then(nc.vector.tensor_scalar(scan[:, :], scan[:, :], off[:, 0:1], None, ALU.is_le))
            then(nc.vector.tensor_tensor(scan[:, :], scan[:, :], ind2[:, :], ALU.mult))
            nc.vector.tensor_tensor(selT[:, :], scan[:, :], ind[:, :], ALU.add).then_inc(e_sel, 1)
            dve.wait_ge(e_selT, 1)

            def over_experts(a):
                return a.rearrange("p e t -> p t e")

            def wide(a):
                return a.unsqueeze(1).broadcast_to([P, NE, NB])

            chosen = ps[:, 7, 0:P].rearrange("p (e t) -> p e t", e=NE)
            then(nc.vector.tensor_reduce(cm[:, :], over_experts(chosen), AX.X, ALU.max))
            then(nc.vector.tensor_scalar(cm[:, :], cm[:, :], -1.0, 1.0, ALU.mult, ALU.add))
            then(nc.vector.tensor_tensor(c1[:, :, :], chosen, wide(cm[:, :]), ALU.add))
            then(nc.vector.tensor_tensor(c2[:, :, :], c1[:, :, :], probs[:, :, :], ALU.mult))
            then(nc.vector.scalar_tensor_tensor(c1[:, :, :], c1[:, :, :], -1.0, c2[:, :, :], ALU.add, ALU.add))
            then(nc.vector.tensor_reduce(cm[:, :], over_experts(c1[:, :, :]), AX.X, ALU.max))
            then(nc.vector.tensor_tensor(c2[:, :, :], c1[:, :, :], wide(cm[:, :]), ALU.is_equal))
            then(nc.vector.tensor_tensor(c1[:, :, :], c2[:, :, :], key.unsqueeze(2).broadcast_to([P, NE, NB]), ALU.mult))
            then(nc.vector.tensor_reduce(cm[:, :], over_experts(c1[:, :, :]), AX.X, ALU.max))
            then(nc.vector.tensor_tensor(c2[:, :, :], c1[:, :, :], wide(cm[:, :]), ALU.is_equal))
            then(nc.vector.tensor_tensor(gates[:, :, :], c2[:, :, :], probs[:, :, :], ALU.mult))

            with dve.Fori(0, NCH) as c:
                for e in range(NE):
                    dve.wait_ge(e_down, c * NE + e + 1)
                    for t in range(TPC):
                        part, share = ps[:, 4 + e % 2, t * P:(t + 1) * P], gates[:, e, bass.ds(c * TPC + t, 1)]
                        if e == 0:
                            last = nc.vector.tensor_scalar(acc[:, t, :], part, share, None, ALU.mult)
                        else:
                            last = nc.vector.scalar_tensor_tensor(acc[:, t, :], part, share, acc[:, t, :],
                                                                  ALU.mult, ALU.add)
                    last.then_inc(e_acc, 1)
                    dve.wait_ge(e_acc, c * NE + e + 1)
                nc.vector.scalar_tensor_tensor(x[:, bass.ds(c * TPC, TPC), :], acc[:, :, :], tg[:, 3:4],
                                               x[:, bass.ds(c * TPC, TPC), :], ALU.mult, ALU.add).then_inc(e_x, 1)
                dve.wait_ge(e_x, c + 1)

        @block.scalar
        def _(act):
            act.wait_ge(ld_w, N_W)
            nc.scalar.activation(base_h[:, :], wb[:, D:D + 1], ACT.Gelu, scale=5.545177444479562).then_inc(base_hidden, 1)

            def transposed(k, also=None):
                act.wait_ge(ln_T, k + 1)
                nc.scalar.activation(xnT[:, :], ps[:, 7, :], ACT.Copy).then_inc(ln_Ts, 1)
                if also is not None:
                    nc.scalar.activation(xnT_all[:, also], ps[:, 7, :], ACT.Copy).then_inc(ln_Ts, 1)

            with act.Fori(0, NCH) as c:
                transposed(c)
                act.wait_ge(a_q, c + 1)
                nc.scalar.activation(qT[:, :], ps[:, 1, :], ACT.Copy).then_inc(a_qs, 1)
                act.wait_ge(a_v, c + 1)
                nc.scalar.activation(v_all[:, bass.ds(c * TPC, TPC)].rearrange("p t h d -> p t (h d)"), bank(3),
                                     ACT.Copy).then_inc(a_vs, 1)
                for n in range(2 * HQ):
                    act.wait_ge(a_hid, 2 * HQ * c + n + 1)
                    nc.scalar.activation(hid[:, n, :], ps[:, 4 + n % 2, :], ACT.Gelu).then_inc(a_gelu, 1)
                act.wait_ge(a_gate, c + 1)
                nc.scalar.activation(gate[:, :], ps[:, 0, :], ACT.Tanh).then_inc(a_tanh, 1)

            nc.scalar.activation(tg[:, :], rows[:, 4 * D:4 * D + 4], ACT.Tanh).then_inc(tanh_g, 1)

            def probabilities(b, half):
                act.wait_ge(b_st, 2 * b + half + 1)
                nc.scalar.activation(pT[:, 8 * half:8 * half + 8, :].rearrange("p (a h) n -> p a (h n)", a=2),
                                     ps[:, 2 + 2 * half:4 + 2 * half, :], ACT.Exp).then_inc(b_exp, 1)

            def attended(b):
                act.wait_ge(b_av, b + 1)
                nc.scalar.activation(avT[:, :], ps[:, 6, :], ACT.Copy).then_inc(b_avs, 1)

            def output(b):
                act.wait_ge(b_aoT, b + 1)
                nc.scalar.activation(aoT[:, :], ps[:, 7, 0:P], ACT.Copy).then_inc(b_aoTs, 1)

            probabilities(0, 0)
            probabilities(0, 1)
            with act.Fori(1, NB) as b:
                attended(b - 1)
                probabilities(b, 0)
                probabilities(b, 1)
                output(b - 1)
            attended(NB - 1)
            output(NB - 1)

            act.wait_ge(ld_ffn, N_FFN)
            with act.Fori(0, NCH) as c:
                transposed(NCH + c)
                act.wait_ge(c_shift, c + 1)
                nc.scalar.activation(r1[:, :, :], logit[:, :, :], ACT.Exp).then_inc(c_exp, 1)
                act.wait_ge(c_wT, c + 1)
                nc.scalar.activation(wT[:, :], ps[0:NE, 6, :], ACT.Copy).then_inc(c_wTs, 1)
                for n in range(NE * NF):
                    e, f = n // NF, n % NF
                    act.wait_ge(c_gate, c * NE * NF + n + 1)
                    if n >= NF:
                        act.wait_ge(c_h, c * NE * NF + n - NF + 1)
                    nc.scalar.activation(silu[:, f, :], ps[:, f, :], ACT.Silu, bias=ffn_b[:, 0, e, f:f + 1]).then_inc(c_silu, 1)

            with act.Fori(0, NCH) as c:
                transposed(2 * NCH + c)
                act.wait_ge(d_ksh, c + 1)
                nc.scalar.activation(ql[:, 1], ql[:, 1], ACT.Exp).then_inc(d_ke, 1)
                act.wait_ge(d_qsh, c + 1)
                nc.scalar.activation(ql[:, 0], ql[:, 0], ACT.Exp).then_inc(d_qe, 1)
                act.wait_ge(d_qT, c + 1)
                nc.scalar.activation(qnT[:, :], ps[:, 0, :], ACT.Copy).then_inc(d_qTs, 1)
                act.wait_ge(d_oT, c + 1)
                nc.scalar.activation(qT[:, :], ps[:, 0, :], ACT.Copy).then_inc(d_oTs, 1)

            with act.Fori(0, NCH) as c:
                transposed(3 * NCH + c, bass.ds(c * CH, CH))
                act.wait_ge(e_shift, c + 1)
                nc.scalar.activation(r1[:, :, :], logit[:, :, :], ACT.Exp).then_inc(e_exp, 1)
            with act.Fori(0, NCH) as c:
                for e in range(NE):
                    for f in range(NF):
                        act.wait_ge(e_h, (c * NE + e) * NF + f + 1)
                        if e >= 2:
                            act.wait_ge(e_down, c * NE + e - 1)
                        nc.scalar.activation(hT[:, e % 2, f, :], ps[:, 2 * (e % 2) + f, :], ACT.Gelu).then_inc(e_gelu, 1)

        @block.tensor
        def _(pe):
            mm, tr = nc.tensor.matmul, nc.tensor.transpose
            pe.wait_ge(ld_w, N_W)
            pe.wait_ge(base_hidden, 1)
            mm(ps[:, 0, 0:1], wb[:, 0:D], base_h[:, :], start=True, stop=True).then_inc(base_out, 1)
            pe.wait_ge(set_up, 2)

            def transpose_chunk(k):
                pe.wait_ge(ln_xn, TPC * (k + 1))
                for t in range(TPC):
                    last = tr(ps[:, 7, t * P:(t + 1) * P], xn[:, t, :], ident)
                last.then_inc(ln_T, 1)

            with pe.Fori(0, NCH) as c:
                transpose_chunk(c)
                pe.wait_ge(ld_ctx, 16 * (c + 1))
                mm(ps[:, 2, :], square(W_K0), ctxT[:, :], start=True, stop=True).then_inc(a_k, 1)
                for t in range(TPC):
                    last = mm(ps[:, 3, t * P:(t + 1) * P], ctxT[:, t * P:(t + 1) * P], square(W_V0), start=True, stop=True)
                last.then_inc(a_v, 1)
                pe.wait_ge(ln_Ts, c + 1)
                mm(ps[:, 1, :], square(W_Q0), xnT[:, :], start=True, stop=True).then_inc(a_q, 1)
                pe.wait_ge(a_qs, c + 1)
                for n in range(2 * HQ):
                    g, h = n // 2, n % 2
                    if n >= 2:
                        pe.wait_ge(a_gelu, 2 * HQ * c + n - 1)
                    mm(ps[:, 4 + n % 2, :], wg1[32 * g:32 * g + 32, h, :], qT[32 * g:32 * g + 32, :],
                       start=True, stop=True).then_inc(a_hid, 1)
                pe.wait_ge(a_gelu, 2 * HQ * (c + 1))
                for h in range(2):
                    for g in range(HQ):
                        last = mm(ps[32 * g:32 * g + 32, 0, :], wg2[:, h, :], hid[:, 2 * g + h, :],
                                  start=(h == 0), stop=(h == 1))
                last.then_inc(a_gate, 1)
                pe.wait_ge(a_tanh, c + 1)
                pe.wait_ge(a_ks, c + 1)
                pe.wait_ge(a_vs, c + 1)

            def scores(b, s, g):
                if g == 0:
                    pe.wait_ge(b_prep, 5 * b + 5)
                n = 4 * b + g
                if not isinstance(n, int) or n >= 2:
                    pe.wait_ge(b_max, n - 1)
                mm(ps[:, g % 2, :], q_st[32 * g:32 * g + 32, s, :],
                   k_bd[32 * g:32 * g + 32, s].rearrange("p j m -> p (j m)"), start=True, stop=False)
                mm(ps[:, g % 2, :], ident_b[:, :], mask_b[:, 0, :].unsqueeze(1).broadcast_to([P, HQ, P]),
                   start=False, stop=True).then_inc(b_sn, 1)

            def scores_T(b, s, g):
                if g == 0:
                    pe.wait_ge(b_max, 4 * b + 4)
                if g % 2 == 0 and (not isinstance(b, int) or b >= 1):
                    pe.wait_ge(b_exp, 2 * b + g // 2 - 1)
                mm(ps[:, 2 + g, :], k_st[32 * g:32 * g + 32, s, :],
                   q_bd[32 * g:32 * g + 32, s].rearrange("p j n -> p (j n)"), start=True, stop=False)
                for j in range(HQ):
                    h = HQ * g + j
                    mm(ps[:, 2 + g, j * P:(j + 1) * P], nmax[:, s, h:h + 1].to_broadcast([P, P]), ident_b[:, :],
                       start=False, stop=False)
                last = mm(ps[:, 2 + g, :], ident_b[:, :], mask_b[:, 1, :].unsqueeze(1).broadcast_to([P, HQ, P]),
                          start=False, stop=True)
                if g % 2:
                    last.then_inc(b_st, 1)

            def attend(b, s):
                pe.wait_ge(b_exp, 2 * b + 2)
                for a in range(HQ):
                    for j in range(HQ):
                        last = mm(ps[32 * j:32 * j + 32, 6, a * P:(a + 1) * P], v_st[:, s, HQ * a + j, :],
                                  pT[:, HQ * a + j, :], start=True, stop=True)
                last.then_inc(b_av, 1)

            def natural(b):
                pe.wait_ge(b_avs, b + 1)
                if not isinstance(b, int) or b >= 1:
                    pe.wait_ge(b_x, b)
                for a in range(HQ):
                    last = tr(ps[:, 7, a * P:(a + 1) * P], avT[:, a * P:(a + 1) * P], ident)
                last.then_inc(b_nat, 1)

            def out_T(b):
                pe.wait_ge(b_ao, b + 1)
                tr(ps[:, 7, 0:P], ao[:, :], ident).then_inc(b_aoT, 1)

            def project(b):
                pe.wait_ge(b_aoTs, b + 1)
                mm(ps[:, 7, P:2 * P], aoT[:, :], square(W_O0), start=True, stop=True).then_inc(b_y, 1)

            def slot(b, s, last=False):
                attend(b - 1, 1 - s)
                scores_T(b, s, 0)
                scores_T(b, s, 1)
                natural(b - 1)
                if not last:
                    scores(b + 1, 1 - s, 0)
                scores_T(b, s, 2)
                if not last:
                    scores(b + 1, 1 - s, 1)
                scores_T(b, s, 3)
                out_T(b - 1)
                if not last:
                    scores(b + 1, 1 - s, 2)
                    scores(b + 1, 1 - s, 3)
                project(b - 1)

            for g in range(4):
                scores(0, 0, g)
            for g in range(4):
                scores_T(0, 0, g)
            for g in range(4):
                scores(1, 1, g)
            slot(1, 1)
            with pe.Fori(1, NB // 2 - 1) as r:
                slot(2 * r, 0)
                slot(2 * r + 1, 1)
            slot(NB - 2, 0)
            slot(NB - 1, 1, last=True)
            attend(NB - 1, 1)
            natural(NB - 1)
            out_T(NB - 1)
            project(NB - 1)

            pe.wait_ge(ld_ffn, N_FFN)
            pe.wait_ge(b_x, NB)

            def route(r, ready):
                for t in range(TPC):
                    last = mm(ps[:, 6, t * NE:(t + 1) * NE], xnT[:, t * P:(t + 1) * P], routers[:, r, :],
                              start=True, stop=True)
                last.then_inc(ready, 1)

            with pe.Fori(0, NCH) as c:
                transpose_chunk(NCH + c)
                pe.wait_ge(ln_Ts, NCH + c + 1)
                route(0, c_logit)

                def gate_up(e):
                    for f in range(NF):
                        n = c * NE * NF + e * NF + f
                        if e:
                            pe.wait_ge(c_silu, n - NF + 1)
                            pe.wait_ge(c_h, n - NF + 1)
                        mm(ps[:, f, :], gate_w[:, e, f * P:(f + 1) * P], xnT[:, :], start=True, stop=True).then_inc(c_gate, 1)
                        mm(ps[:, 2 + f, :], up_w[:, e, f * P:(f + 1) * P], xnT[:, :], start=True, stop=True).then_inc(c_up, 1)

                def down(e):
                    pe.wait_ge(c_h, (c * NE + e + 1) * NF)
                    for t in range(TPC):
                        for f in range(NF):
                            last = mm(ps[:, 4 + e % 2, t * P:(t + 1) * P], hT[:, e % 2, f, t * P:(t + 1) * P],
                                      down_w[:, e, f, :], start=(f == 0), stop=(f == NF - 1))
                    last.then_inc(c_down, 1)

                gate_up(0)
                pe.wait_ge(c_w, 2 * c + 1)
                for t in range(TPC):
                    last = tr(ps[0:NE, 6, t * P:(t + 1) * P], r1[:, t, :], ident)
                last.then_inc(c_wT, 1)
                pe.wait_ge(c_wTs, c + 1)
                for t in range(TPC):
                    last = mm(ps[:, 6, t * P:(t + 1) * P], wT[:, t * P:(t + 1) * P], down_b[:, :], start=True, stop=True)
                last.then_inc(c_bias, 1)
                for e in range(NE):
                    if e + 1 < NE:
                        gate_up(e + 1)
                    down(e)
                pe.wait_ge(c_x, c + 1)

            with pe.Fori(0, NCH) as c:
                pe.wait_ge(ld_ctx, 16 * (NCH + c + 1))
                for bnk, wn, done in ((1, W_K1, d_k), (2, W_V1, d_v)):
                    for t in range(TPC):
                        last = mm(ps[:, bnk, t * P:(t + 1) * P], ctxT[:, t * P:(t + 1) * P], square(wn), start=True, stop=True)
                    last.then_inc(done, 1)
                transpose_chunk(2 * NCH + c)
                pe.wait_ge(ln_Ts, 2 * NCH + c + 1)
                for t in range(TPC):
                    last = mm(ps[:, 0, t * P:(t + 1) * P], xnT[:, t * P:(t + 1) * P], square(W_Q1), start=True, stop=True)
                last.then_inc(d_q, 1)
                pe.wait_ge(d_kn, c + 1)
                pe.wait_ge(d_vs, 2 * (c + 1))
                for t in range(TPC):
                    last = mm(ps[:, 3 + t // 2, (t % 2) * 256:(t % 2) * 256 + D + 1],
                              ql[:, 1, t * H:(t + 1) * H].rearrange("p h d -> p (h d)"), vl[:, t, :], start=True, stop=True)
                last.then_inc(d_kv, 1)
                pe.wait_ge(d_qn, c + 1)
                for t in range(TPC):
                    last = tr(ps[:, 0, t * P:(t + 1) * P], ql[:, 0, t * H:(t + 1) * H].rearrange("p h d -> p (h d)"), ident)
                last.then_inc(d_qT, 1)
                pe.wait_ge(d_qTs, c + 1)
                pe.wait_ge(d_kvd, 2 * TPC * (c + 1))
                for t in range(TPC):
                    last = mm(ps[:, 5 + t // 2, (t % 2) * 256:(t % 2) * 256 + D + H], qnT[:, t * P:(t + 1) * P], kvd[:, t, :],
                              start=True, stop=True)
                last.then_inc(d_num, 1)
                pe.wait_ge(d_o, (TPC + 1) * (c + 1))
                for t in range(TPC):
                    last = tr(ps[:, 0, t * P:(t + 1) * P], lo[:, t, :], ident)
                last.then_inc(d_oT, 1)
                pe.wait_ge(d_oTs, c + 1)
                for t in range(TPC):
                    last = mm(ps[:, 7, t * P:(t + 1) * P], qT[:, t * P:(t + 1) * P], square(W_P1), start=True, stop=True)
                last.then_inc(d_y, 1)
                pe.wait_ge(d_x, c + 1)

            with pe.Fori(0, NCH) as c:
                transpose_chunk(3 * NCH + c)
                pe.wait_ge(ln_Ts, 3 * NCH + 2 * c + 2)
                route(1, e_logit)
                pe.wait_ge(e_shift, c + 1)
            pe.wait_ge(e_p, NCH)
            tr(ps[:, 0, 0:P], probs[:, :, :].rearrange("p e t -> p (e t)"), ident).then_inc(e_pT, 1)
            with pe.Fori(0, THRESHOLD_BITS) as n:
                pe.wait_ge(e_cnt, n + 1)
                mm(ps[:, 1, 0:1], sum16, cnt[:, 0:1], start=True, stop=True).then_inc(e_tot, 1)
            pe.wait_ge(e_ties, 1)
            mm(ps[:, 2, 0:1], sum16, cnt[:, 0:1], start=True, stop=True)
            mm(ps[:, 2, 1:2], tri16, cnt[:, 1:2], start=True, stop=True).then_inc(e_tie_tot, 1)
            pe.wait_ge(e_sel, 1)
            tr(ps[:, 7, 0:P], selT[:, :], ident).then_inc(e_selT, 1)

            with pe.Fori(0, NCH) as c:
                def first(e):
                    for f in range(NF):
                        n = (c * NE + e) * NF + f
                        mm(ps[:, 2 * (e % 2) + f, :], w1[:, e, f * P:(f + 1) * P], xnT_all[:, bass.ds(c * CH, CH)],
                           start=True, stop=True).then_inc(e_h, 1)

                def second(e):
                    pe.wait_ge(e_gelu, (c * NE + e + 1) * NF)
                    if e >= 2:
                        pe.wait_ge(e_acc, c * NE + e - 1)
                    for t in range(TPC):
                        for f in range(NF):
                            last = mm(ps[:, 4 + e % 2, t * P:(t + 1) * P], hT[:, e % 2, f, t * P:(t + 1) * P],
                                      w2[:, e, f, :], start=(f == 0), stop=(f == NF - 1))
                    last.then_inc(e_down, 1)

                first(0)
                for e in range(NE):
                    if e + 1 < NE:
                        first(e + 1)
                    second(e)
                pe.wait_ge(e_x, c + 1)


def kernel(**inputs):
    import numpy as np
    import concourse.bacc as bacc
    from concourse.bass_utils import run_bass_kernel_spmd

    def a(name):
        return np.asarray(inputs[name])

    f = np.float32
    cst = np.zeros((P, C_END), f)
    r = np.arange(P)
    cst[:, C_IDENT:C_IDENT + P] = np.eye(P)
    cst[:, C_BLOCK:C_BLOCK + P] = r[:, None] // DH == r[None, :] // DH
    cst[:, C_SUM16:C_SUM16 + P] = r[:, None] // NB == r[None, :] // NB
    cst[:, C_TRI16:C_TRI16 + P] = (r[:, None] // NB == r[None, :] // NB) & (r[:, None] < r[None, :])
    cst[:, C_HEAD:C_HEAD + H] = r[:, None] // DH == np.arange(H)[None, :]
    cst[:, C_QUAD:C_QUAD + HQ] = (r[:, None] % 32) // DH == np.arange(HQ)[None, :]
    cst[:, C_KEY:C_KEY + NE] = NE - np.arange(NE)[None, :]
    wg1 = np.zeros((P, 2, P), f)
    wg2 = np.zeros((P, 2, 32), f)
    for g in range(HQ):
        for j in range(HQ):
            wg1[32 * g + DH * j:32 * g + DH * (j + 1), j // 2, HID * (j % 2):HID * (j % 2 + 1)] = a("L0_xattn_wg1").T
    for j in range(HQ):
        wg2[HID * (j % 2):HID * (j % 2 + 1), j // 2, DH * j:DH * (j + 1)] = a("L0_xattn_wg2").T
    squares = ["L0_xattn_wq", "L0_xattn_wk", "L0_xattn_wv", "L0_xattn_wo", "L1_xattn_Wq", "L1_xattn_Wk", "L1_xattn_Wv", "L1_xattn_Wp"]
    mask = a("mask_1x1xSxS2_bf1")[0, 0].view(np.uint8)

    def blocks(b):
        return b.reshape(NE, NF, P).transpose(2, 0, 1).reshape(P, NE * NF)

    data = {
        "cst": cst,
        "x": a("x"),
        "ctxT": a("ctx_1024").transpose(2, 0, 1).reshape(D, NB * P),
        "w": np.concatenate([a(n).T for n in squares], axis=1),
        "wg1": wg1,
        "wg2": wg2,
        "wb": np.concatenate([a("L0_xattn_wb2").T, a("L0_xattn_wb1")], axis=1),
        "rows": np.concatenate([a("L1_xattn_bq"), a("L1_xattn_bk"), a("L1_xattn_bv"), a("L1_xattn_bp"),
                                a("g_xattn"), a("g_ffn")])[None, :],
        "mask": np.stack([mask, mask.T], axis=1),
        "routers": np.stack([a("L0_ffn_router_w").T, a("L1_ffn_Wg")], axis=1),
        "down_b": a("L0_ffn_down_b"),
        "gate_w": a("L0_ffn_gate_w"),
        "up_w": a("L0_ffn_up_w"),
        "down_w": a("L0_ffn_down_w"),
        "gate_b": blocks(a("L0_ffn_gate_b")),
        "up_b": blocks(a("L0_ffn_up_b")),
        "w1": a("L1_ffn_W1"),
        "w2": a("L1_ffn_W2"),
    }
    nc = bacc.Bacc("TRN2", target_bir_lowering=False, num_devices=1)
    arrays, aps = {}, {}
    for name, value in data.items():
        value = np.ascontiguousarray(value)
        arrays[f"in_{name}"] = value
        aps[name] = nc.dram_tensor(f"in_{name}", value.shape, mybir.dt.from_np(value.dtype), kind="ExternalInput").ap()
    out = nc.dram_tensor("out", (NB, P, D), mybir.dt.float32, kind="ExternalOutput").ap()
    build(nc, aps, out)
    ran = run_bass_kernel_spmd(nc, [arrays], core_ids=[0])
    return ran.results[0]["out"]
```

```python
import concourse.bass as bass
from concourse import mybir
from contextlib import ExitStack

P = 128
NB = 16
D = 128
H = 16
DH = D // H
HQ = 4
HID = 64
NCH = 4
TPC = NB // NCH
CH = TPC * P
NE = 8
FF = 256
NF = FF // P
CAP = NB * P // NE
EPS = 1e-5
MASKED = -1e30
THRESHOLD_BITS = 30

C_IDENT, C_BLOCK, C_SUM16, C_TRI16 = 0, 128, 256, 384
C_HEAD, C_QUAD, C_KEY, C_END = 512, 528, 532, 540
W_Q0, W_K0, W_V0, W_O0, W_Q1, W_K1, W_V1, W_P1 = range(8)


class Count:

    def __init__(self, engine, semaphore):
        self.engine, self.semaphore, self.base, self.k = engine, semaphore, 0, 0

    def done(self, instruction):
        self.k += 1
        return instruction.then_inc(self.semaphore, 1)

    def wait(self):
        self.engine.wait_ge(self.semaphore, self.base + self.k)

    def enter(self, index, per):
        self.start, self.base, self.k = self.base + self.k, self.base + self.k + index * per, 0
        self.per = per

    def leave(self, iterations):
        assert self.k == self.per, (self.k, self.per)
        self.base, self.k = self.start + iterations * self.per, 0


def build(nc, i, out):
    fp32, bf16, i32, fp32r = mybir.dt.float32, mybir.dt.bfloat16, mybir.dt.int32, mybir.dt.float32r
    ALU, ACT, AX = mybir.AluOpType, mybir.ActivationFunctionType, mybir.AxisListType
    ctx = ExitStack()
    with ctx:
        def sb(name, shape, dt=fp32):
            return ctx.enter_context(nc.sbuf_tensor(name, shape, dt))

        def sem(name):
            return ctx.enter_context(nc.semaphore(name))

        x = sb("x", [P, NB, D])
        cst = sb("cst", [P, C_END])
        w = sb("w", [P, 8 * D])
        wg1 = sb("wg1", [P, 2 * HQ, P])
        wg2 = sb("wg2", [P, 2, 32])
        wb = sb("wb", [HID, D + 1])
        routers = sb("routers", [P, 2, NE])
        rows = sb("rows", [P, 4 * D + 4])
        mask_u8 = sb("mask_u8", [P, 2, P], mybir.dt.uint8)
        down_w = sb("down_w", [P, NE, NF, D])
        ffn_b = sb("ffn_b", [P, 2, NE, NF])
        down_b = sb("down_b", [NE, D])
        w1 = sb("w1", [P, NE, FF])
        w2 = sb("w2", [P, NE, NF, D])
        gate_hi = sb("gate_hi", [P, NE, FF], fp32r)
        up_hi = sb("up_hi", [P, NE, FF], fp32r)
        gate_lo = sb("gate_lo", [P, NE, FF], fp32r)
        up_lo = sb("up_lo", [P, NE, FF], fp32r)
        w1_hi, w1_lo = gate_hi, gate_lo
        SPLIT = 2
        ident_b = sb("ident_b", [P, P], bf16)
        mask_b = sb("mask_b", [P, 2, P], bf16)
        mask_f = sb("mask_f", [P, 2, P])
        visible = sb("visible", [P, 2])
        tg = sb("tg", [P, 4])
        base_h = sb("base_h", [HID, 1])
        kscale = sb("kscale", [P, 1])
        minus_half = sb("minus_half", [P, 2 * TPC])
        stats = sb("stats", [P, NB, 6])
        mv = sb("mv", [P, NB, 3])
        var_eps = sb("var_eps", [P, NB])
        rstd = sb("rstd", [P, NB])
        xn = sb("xn", [P, 2, TPC, D])
        xnT = sb("xnT", [P, 2, CH])
        ctxT = sb("ctxT", [P, NB * P])
        ctxT_c = sb("ctxT_c", [P, CH])
        xn_hi = sb("xn_hi", [P, NB * P], fp32r)
        xn_lo = sb("xn_lo", [P, NB * P], fp32r)
        big = sb("big", [P, 4 * NB * P])
        qg_all = big[:, 0:NB * P]
        k_all = big[:, NB * P:2 * NB * P]
        v_all = big[:, 2 * NB * P:3 * NB * P].rearrange("p (b h d) -> p b h d", b=NB, h=H)
        pT = big[:, 3 * NB * P:].rearrange("p (h n) -> p h n", h=H)
        parts = big[:, :].rearrange("p (c e t n) -> p c e t n", c=2, e=NE, t=TPC)
        kvd_all = sb("kvd_all", [P, NB * (D + H)])
        kvd = kvd_all[:, :].rearrange("p (t n) -> p t n", t=NB)
        gate_w = big[:, 3 * NB * P:].rearrange("p (e f) -> p e f", e=NE)
        up_w = kvd_all[:, 0:NE * FF].rearrange("p (e f) -> p e f", e=NE)
        SPLITS = [(gate_w, gate_hi, gate_lo), (up_w, up_hi, up_lo), (w1, w1_hi, w1_lo)]
        qT = sb("qT", [P, 2, CH])
        hid = sb("hid", [P, 2 * HQ, CH])
        gate = sb("gate", [P, 2, CH])
        q_st = sb("q_st", [P, 2, P], bf16)
        k_st = sb("k_st", [P, 2, P])
        q_bd = sb("q_bd", [P, 2, HQ, P])
        k_bd = sb("k_bd", [P, 2, HQ, P], bf16)
        v_st = sb("v_st", [P, 2, H, 32])
        nmax = sb("nmax", [P, 2, H], bf16)
        avT = sb("avT", [P, CH])
        rsum = sb("rsum", [P, H])
        rinv = sb("rinv", [P, H])
        ao = sb("ao", [P, D])
        aoT = sb("aoT", [P, P])
        silu = hid[:, 0:NF, :]
        hT = hid[:, NF:3 * NF, :].rearrange("p (s f) n -> p s f n", s=2)
        acc = ctxT[:, 0:2 * CH].rearrange("p (c t n) -> p c t n", c=2, t=TPC)
        wexp = sb("wexp", [P, TPC, NE])
        wT = sb("wT", [NE, CH])
        logit = sb("logit", [P, TPC, NE])
        r1 = sb("r1", [P, TPC, NE])
        r2 = sb("r2", [P, TPC, NE])
        sel1 = sb("sel1", [P, TPC, NE])
        rm = sb("rm", [P, TPC])
        rm2 = sb("rm2", [P, TPC])
        half_k = sb("half_k", [P, TPC * H, DH // 2])
        qm = sb("qm", [P, NCH, TPC * H])
        kl = ctxT[:, 2 * CH:3 * CH].rearrange("p (h d) -> p h d", h=TPC * H)
        km = sb("km", [P, TPC * H])
        vl = sb("vl", [P, TPC, D + 1])
        dinv = sb("dinv", [P, NCH, TPC * H])
        elog = sb("elog", [P, NCH, TPC, NE])
        em = sb("em", [P, NCH, TPC])
        one_row = sb("one_row", [1, P])
        xn_d = big[:, 0:NB * P].rearrange("p (t n) -> p t n", t=NB)
        xnT_d = big[:, NB * P:2 * NB * P].rearrange("p (c n) -> p c n", c=NCH)
        ql = big[:, 2 * NB * P:3 * NB * P].rearrange("p (c h d) -> p c h d", c=NCH, h=TPC * H)
        lo = big[:, 3 * NB * P:].rearrange("p (c h d) -> p c h d", c=NCH, h=TPC * H)
        qnT = hid[:, 0:NCH, :]
        loT = hid[:, NCH:2 * NCH, :]
        probs = sb("probs", [P, NE, NB])
        pS, ind, ind2, scan = (ctxT[:, 3 * CH + n * P:3 * CH + (n + 1) * P] for n in range(4))
        thr = sb("thr", [P, 1], i32)
        cand = sb("cand", [P, 1], i32)
        inc = sb("inc", [P, 1], i32)
        cnt = sb("cnt", [P, 2])
        need = sb("need", [P, 1])
        off = sb("off", [P, 1])
        selT = sb("selT", [P, P])
        c1 = sb("c1", [P, NE, NB])
        c2 = sb("c2", [P, NE, NB])
        cm = sb("cm", [P, NB])
        gates = sb("gates", [P, NE, NB])

        ps = ctx.enter_context(nc.psum_tensor("ps", [P, 8, 512], fp32))

        def bank(n, parts=TPC):
            return ps[:, n, :].rearrange("p (t n) -> p t n", t=parts)

        ident = cst[:, C_IDENT:C_IDENT + P]
        block_mask = cst[:, C_BLOCK:C_BLOCK + P]
        sum16 = cst[:, C_SUM16:C_SUM16 + P]
        tri16 = cst[:, C_TRI16:C_TRI16 + P]
        head_sel = cst[:, C_HEAD:C_HEAD + H]
        quad_sel = cst[:, C_QUAD:C_QUAD + HQ]
        key = cst[:, C_KEY:C_KEY + NE]

        def square(n):
            return w[:, n * D:(n + 1) * D]

        ld_x, ld_w, ld_ffn, ld_ctx = sem("ld_x"), sem("ld_w"), sem("ld_ffn"), sem("ld_ctx")
        stored, ld_ctx_c = sem("stored"), sem("ld_ctx_c")
        dve_step, pool_step, act_step = sem("dve_step"), sem("pool_step"), sem("act_step")
        base_hidden, base_out, set_up, tanh_g = sem("base_hidden"), sem("base_out"), sem("set_up"), sem("tanh_g")
        w_hi, w_lo, ln_lo = sem("w_hi"), sem("w_lo"), sem("ln_lo")
        ln_var, ln_rstd, ln_xn, ln_T, ln_Ts, ln_all = (
            sem(n) for n in ("ln_var", "ln_rstd", "ln_xn", "ln_T", "ln_Ts", "ln_all"))
        a_q, a_k, a_v, a_qs, a_ks, a_vs = (sem(n) for n in ("a_q", "a_k", "a_v", "a_qs", "a_ks", "a_vs"))
        a_hid, a_gelu, a_gate, a_tanh, a_qg = (sem(n) for n in ("a_hid", "a_gelu", "a_gate", "a_tanh", "a_qg"))
        b_prep, b_sn, b_max, b_st, b_exp = (sem(n) for n in ("b_prep", "b_sn", "b_max", "b_st", "b_exp"))
        b_av, b_avs, b_nat, b_ao, b_aoT, b_aoTs, b_y, b_x = (
            sem(n) for n in ("b_av", "b_avs", "b_nat", "b_ao", "b_aoT", "b_aoTs", "b_y", "b_x"))
        c_logit, c_w, c_wT, c_wTs, c_bias = (sem(n) for n in ("c_logit", "c_w", "c_wT", "c_wTs", "c_bias"))
        c_gate, c_up, c_silu, c_h, c_down, c_x = (sem(n) for n in ("c_gate", "c_up", "c_silu", "c_h", "c_down", "c_x"))
        d_k, d_v, d_kb, d_kmax, d_ksum, d_kinv, d_ksh, d_ke, d_kn, d_vs, d_kv, d_kvd = (
            sem(n) for n in ("d_k", "d_v", "d_kb", "d_kmax", "d_ksum", "d_kinv", "d_ksh", "d_ke", "d_kn", "d_vs", "d_kv", "d_kvd"))
        d_q, d_qsh, d_qe, d_qinv, d_qn, d_qT, d_qTs, d_num, d_o, d_oT, d_oTs, d_y, d_x = (
            sem(n) for n in ("d_q", "d_qsh", "d_qe", "d_qinv", "d_qn", "d_qT", "d_qTs", "d_num", "d_o", "d_oT", "d_oTs",
                             "d_y", "d_x"))
        e_logit, e_shift, e_exp, e_p, e_pT, e_cnt, e_tot, e_ties, e_tie_tot, e_sel, e_selT, e_gated = (
            sem(n) for n in ("e_logit", "e_shift", "e_exp", "e_p", "e_pT", "e_cnt", "e_tot", "e_ties",
                             "e_tie_tot", "e_sel", "e_selT", "e_gated"))
        c_shift, c_exp, c_biased = sem("c_shift"), sem("c_exp"), sem("c_biased")
        e_h, e_gelu, e_down, e_part, e_acc, e_x = (
            sem(n) for n in ("e_h", "e_gelu", "e_down", "e_part", "e_acc", "e_x"))
        block = ctx.enter_context(nc.Block())

        N_X, N_W, N_FFN = 16, 9 * 16, 7 * 16
        PAIRS = NCH // 2
        LN_D, LN_E = 2 * NCH, 2 * NCH + PAIRS

        @block.sync
        def _(sp):
            sp.dma_start(cst[:, :], i["cst"]).then_inc(ld_w, 16)
            sp.dma_start(x[:, :, :], i["x"].rearrange("b p d -> p b d")).then_inc(ld_x, 16)
            sp.dma_start(w[:, :], i["w"]).then_inc(ld_w, 16)
            sp.dma_start(wg1[:, :, :], i["wg1"]).then_inc(ld_w, 16)
            sp.dma_start(wg2[:, :, :], i["wg2"]).then_inc(ld_w, 16)
            sp.dma_start(wb[:, :], i["wb"]).then_inc(ld_w, 16)
            sp.dma_start(rows[:, :], i["rows"].broadcast_to([P, 4 * D + 4])).then_inc(ld_w, 16)
            sp.dma_start(mask_u8[:, :, :], i["mask"]).then_inc(ld_w, 16)
            sp.dma_start(routers[:, :, :], i["routers"]).then_inc(ld_w, 16)
            sp.dma_start(down_b[:, :], i["down_b"]).then_inc(ld_w, 16)
            sp.dma_start(ctxT[:, :], i["ctxT"]).then_inc(ld_ctx, 16)
            sp.dma_start(gate_w[:, :, :], i["gate_w"].rearrange("e d f -> d e f")).then_inc(ld_ffn, 16)
            sp.dma_start(up_w[:, :, :], i["up_w"].rearrange("e d f -> d e f")).then_inc(ld_ffn, 16)
            sp.dma_start(down_w[:, :, :, :], i["down_w"].rearrange("e (f p) d -> p e f d", p=P)).then_inc(ld_ffn, 16)
            sp.dma_start(ffn_b[:, 0], i["gate_b"].rearrange("p (e f) -> p e f", e=NE)).then_inc(ld_ffn, 16)
            sp.dma_start(ffn_b[:, 1], i["up_b"].rearrange("p (e f) -> p e f", e=NE)).then_inc(ld_ffn, 16)
            sp.dma_start(w1[:, :, :], i["w1"].rearrange("e d f -> d e f")).then_inc(ld_ffn, 16)
            sp.dma_start(w2[:, :, :, :], i["w2"].rearrange("e (f p) d -> p e f d", p=P)).then_inc(ld_ffn, 16)
            sp.dma_start(ctxT_c[:, :], i["ctxT"][:, 0:CH]).then_inc(ld_ctx_c, 16)
            with sp.Fori(1, NCH) as c:
                sp.wait_ge(d_v, c)
                sp.dma_start(ctxT_c[:, :], i["ctxT"][:, bass.ds(c * CH, CH)]).then_inc(ld_ctx_c, 16)
            with sp.Fori(0, NCH) as c:
                sp.wait_ge(e_x, c + 1)
                sp.dma_start(out.rearrange("b p d -> p b d")[:, bass.ds(c * TPC, TPC), :],
                             x[:, bass.ds(c * TPC, TPC), :]).then_inc(stored, 16)
            sp.wait_ge(stored, 16 * NCH)

        @block.gpsimd
        def _(pool):
            step = Count(pool, pool_step)
            step.done(nc.gpsimd.memset(minus_half[:, :], -0.5))
            nc.gpsimd.memset(v_st[:, :, :, :], 0.0).then_inc(pool_step, 1)
            step.k += 1
            step.wait()
            step.done(nc.gpsimd.memset(v_st[:, :, :, DH:DH + 1], 1.0))
            step.wait()

            def layer_norm(k, slot, n=TPC):
                pool.wait_ge(ln_var, k + 1)
                nc.gpsimd.tensor_tensor(rstd[:, slot:slot + n], var_eps[:, slot:slot + n], minus_half[:, 0:n],
                                        ALU.pow).then_inc(ln_rstd, 1)

            def low_weights(first, m):
                full, high, low = SPLITS[m]
                for e in range(0, NE, SPLIT):
                    pool.wait_ge(w_hi, first + e // SPLIT + 1)
                    nc.gpsimd.tensor_tensor(low[:, e:e + SPLIT], full[:, e:e + SPLIT], high[:, e:e + SPLIT],
                                            ALU.subtract).then_inc(w_lo, 1)

            for c in range(NCH):
                layer_norm(c, c % 2 * TPC)
                if c >= NCH - 2:
                    low_weights((c - (NCH - 2)) * NE // SPLIT, c - (NCH - 2))

            pool.wait_ge(ld_w, N_W)
            def prepare(b, s):
                tok = bass.ds(b * P, P)
                nc.gpsimd.tensor_copy(q_st[:, s, :], qg_all[:, tok]).then_inc(b_prep, 1)
                nc.gpsimd.tensor_tensor(
                    k_bd[:, s], k_all[:, tok].unsqueeze(1).broadcast_to([P, HQ, P]),
                    quad_sel.unsqueeze(2).broadcast_to([P, HQ, P]), ALU.mult).then_inc(b_prep, 1)
                nc.gpsimd.tensor_copy(k_st[:, s, :], k_all[:, tok]).then_inc(b_prep, 1)
                nc.gpsimd.tensor_tensor(
                    q_bd[:, s], qg_all[:, tok].unsqueeze(1).broadcast_to([P, HQ, P]),
                    quad_sel.unsqueeze(2).broadcast_to([P, HQ, P]), ALU.mult).then_inc(b_prep, 1)
                if not isinstance(b, int):
                    pool.wait_ge(b_av, b - 1)
                nc.gpsimd.tensor_copy(v_st[:, s, :, 0:DH], v_all[:, b]).then_inc(b_prep, 1)

            pool.wait_ge(a_qg, 1)
            pool.wait_ge(a_ks, 1)
            pool.wait_ge(a_vs, 1)
            prepare(0, 0)
            prepare(1, 1)

            pool.wait_ge(a_qg, NCH)
            pool.wait_ge(a_ks, NCH)
            pool.wait_ge(a_vs, NCH)
            with pool.Fori(1, NB // 2) as g:
                for s in range(2):
                    b = 2 * g + s
                    pool.wait_ge(b_st, 2 * b - 2)
                    prepare(b, s)

            tt = nc.gpsimd.tensor_tensor

            def then(instruction):
                step.done(instruction)
                step.wait()

            def all_keys(a):
                return a.unsqueeze(2).broadcast_to([P, TPC * H, DH])

            def keys(c):
                pool.wait_ge(d_kmax, c + 1)
                tt(kl[:, :, :], kl[:, :, :], all_keys(km[:, :]), ALU.subtract).then_inc(d_ksh, 1)
                pool.wait_ge(d_ke, c + 1)
                then(tt(half_k[:, :, 0:4], kl[:, :, 0:4], kl[:, :, 4:8], ALU.add))
                then(tt(half_k[:, :, 0:2], half_k[:, :, 0:2], half_k[:, :, 2:4], ALU.add))
                tt(km[:, :].unsqueeze(2), half_k[:, :, 0:1], half_k[:, :, 1:2], ALU.add).then_inc(d_ksum, 1)
                pool.wait_ge(d_kinv, c + 1)
                tt(kl[:, :, :], kl[:, :, :], all_keys(km[:, :]), ALU.mult).then_inc(d_kn, 1)

            layer_norm(NCH, 0)
            with pool.Fori(0, NCH - 1) as c:
                step.enter(c, 2)
                layer_norm(NCH + 1 + c, 0)
                keys(c)
                step.leave(NCH - 1)
            keys(NCH - 1)
            for pair in range(PAIRS):
                layer_norm(LN_D + pair, 2 * pair * TPC, 2 * TPC)
            low_weights(2 * NE // SPLIT, 2)
            for c in range(NCH):
                pool.wait_ge(d_qinv, c + 1)
                tt(ql[:, c], ql[:, c], all_keys(qm[:, c]), ALU.mult).then_inc(d_qn, 1)
            for pair in range(PAIRS):
                layer_norm(LN_E + pair, 2 * pair * TPC, 2 * TPC)
            for c in range(NCH):
                tok = slice(c * CH, (c + 1) * CH)
                pool.wait_ge(ln_Ts, 3 * NCH + c + 1)
                pool.wait_ge(ln_all, NCH + c + 1)
                tt(xn_lo[:, tok], xnT_d[:, c, :], xn_hi[:, tok], ALU.subtract).then_inc(ln_lo, 1)

        @block.vector
        def _(dve):
            step = Count(dve, dve_step)
            dve.wait_ge(ld_w, N_W)
            nc.vector.tensor_copy(ident_b[:, :], ident).then_inc(set_up, 1)
            step.done(nc.vector.tensor_copy(mask_f[:, :, :], mask_u8[:, :, :]))
            step.wait()
            nc.vector.tensor_scalar(mask_b[:, :, :], mask_f[:, :, :], -1.0, -MASKED, ALU.add, ALU.mult).then_inc(set_up, 1)
            step.done(nc.vector.tensor_reduce(visible[:, 0:1], mask_f[:, 0, :], AX.X, ALU.add))
            step.wait()
            step.done(nc.vector.reciprocal(visible[:, 0:1], visible[:, 0:1]))
            step.wait()
            step.done(nc.vector.tensor_scalar(visible[:, 1:2], visible[:, 0:1], 0.0, None, ALU.mult))
            dve.wait_ge(base_out, 1)
            step.done(nc.vector.tensor_scalar(kscale[:, :], ps[:, 0, 0:1], float(DH) ** -0.5, None, ALU.mult))
            step.wait()
            dve.wait_ge(ld_x, N_X)

            def variances(slot, tile, n=TPC):
                for t in range(n):
                    step.done(nc.vector.bn_stats(stats[:, slot + t, :], x[:, tile + t, :]))
                step.wait()
                own = stats[:, slot:slot + n]
                even, odd = own[:, :, 0:3], own[:, :, 3:6]
                m = mv[:, slot:slot + n]
                step.done(nc.vector.tensor_tensor(m[:, :, 0], even[:, :, 1], odd[:, :, 1], ALU.add))
                step.done(nc.vector.tensor_tensor(m[:, :, 1], even[:, :, 1], odd[:, :, 1], ALU.subtract))
                step.done(nc.vector.tensor_tensor(m[:, :, 2], even[:, :, 2], odd[:, :, 2], ALU.add))
                step.wait()
                step.done(nc.vector.tensor_scalar(m[:, :, 0], m[:, :, 0], 0.5, None, ALU.mult))
                step.done(nc.vector.scalar_tensor_tensor(m[:, :, 1], m[:, :, 1], 0.25, m[:, :, 1], ALU.mult, ALU.mult))
                step.done(nc.vector.tensor_scalar(m[:, :, 2], m[:, :, 2], 1.0 / D, EPS, ALU.mult, ALU.add))
                step.wait()
                nc.vector.tensor_tensor(var_eps[:, slot:slot + n], m[:, :, 1], m[:, :, 2], ALU.add).then_inc(ln_var, 1)

            def normalised(k, slot, tile, result, n=TPC):
                dve.wait_ge(ln_rstd, k + 1)
                for t in range(n):
                    nc.vector.tensor_scalar(result[:, t, :], x[:, tile + t, :], mv[:, slot + t, 0:1],
                                            rstd[:, slot + t:slot + t + 1], ALU.subtract, ALU.mult).then_inc(ln_xn, 1)

            def layer_norm(k, q, tile):
                variances(q * TPC, tile)
                if not isinstance(k, int) or k >= 1:
                    dve.wait_ge(ln_T, k)
                normalised(k, q * TPC, tile, xn[:, q])

            LN_STEPS = TPC + 6

            layer_norm(0, 0, 0)
            for c in range(NCH):
                dve.wait_ge(a_k, c + 1)
                nc.vector.tensor_scalar(k_all[:, c * CH:(c + 1) * CH], ps[:, 2, :], kscale[:, 0:1], None,
                                        ALU.mult).then_inc(a_ks, 1)
                if c + 1 < NCH:
                    layer_norm(c + 1, (c + 1) % 2, (c + 1) * TPC)
                dve.wait_ge(a_tanh, c + 1)
                nc.vector.scalar_tensor_tensor(qg_all[:, c * CH:(c + 1) * CH], gate[:, c % 2, :], 1.0, qT[:, c % 2, :],
                                               ALU.add, ALU.mult).then_inc(a_qg, 1)

            def maximum(b, s, g):
                dve.wait_ge(b_sn, 4 * b + g + 1)
                nc.vector.tensor_reduce(nmax[:, s, HQ * g:HQ * (g + 1)], bank(g % 2), AX.X, ALU.max,
                                        negate=True).then_inc(b_max, 1)

            def normalise(b):
                dve.wait_ge(b_nat, b + 1)
                av = ps[:, 7, :].rearrange("p (h d) -> p h d", h=H)
                step.done(nc.vector.tensor_scalar(rsum[:, :], av[:, :, DH], visible[:, 1:2], None, ALU.add))
                step.wait()
                step.done(nc.vector.reciprocal(rinv[:, :], rsum[:, :]))
                step.wait()
                nc.vector.tensor_tensor(ao[:, :].rearrange("p (a j d) -> p a j d", a=HQ, j=HQ), ps[:, 7, :].rearrange(
                    "p (a j d) -> p a j d", a=HQ, j=HQ)[:, :, :, 0:DH], rinv[:, :].rearrange(
                    "p (a j) -> p a j", a=HQ).unsqueeze(3).broadcast_to([P, HQ, HQ, DH]), ALU.mult).then_inc(b_ao, 1)

            def residual(b):
                dve.wait_ge(b_y, b + 1)
                nc.vector.scalar_tensor_tensor(x[:, b, :], ps[:, 7, P:2 * P], tg[:, 0:1], x[:, b, :],
                                               ALU.mult, ALU.add).then_inc(b_x, 1)

            def slot(b, s, last=False):
                normalise(b - 1)
                if not last:
                    maximum(b + 1, 1 - s, 0)
                    maximum(b + 1, 1 - s, 1)
                    maximum(b + 1, 1 - s, 2)
                    maximum(b + 1, 1 - s, 3)
                residual(b - 1)

            dve.wait_ge(tanh_g, 1)
            for b in range(2):
                for g in range(4):
                    maximum(b, b, g)
            slot(1, 1)
            with dve.Fori(1, NB // 2 - 1) as r:
                step.enter(r - 1, 4)
                slot(2 * r, 0)
                slot(2 * r + 1, 1)
                step.leave(NB // 2 - 2)
            slot(NB - 2, 0)
            dve.wait_ge(b_x, NB - 3)
            layer_norm(NCH, 0, 0)
            slot(NB - 1, 1, last=True)
            normalise(NB - 1)
            residual(NB - 1)

            def wide(a):
                return a.unsqueeze(2).broadcast_to([P, TPC, NE])

            keys = key.unsqueeze(1).broadcast_to([P, TPC, NE])

            def then(instruction):
                step.done(instruction)
                step.wait()

            def router_1(c, logit_bank):
                dve.wait_ge(c_logit, c + 1)
                lg = ps[:, logit_bank, 0:TPC * NE].rearrange("p (t e) -> p t e", t=TPC)
                then(nc.vector.tensor_reduce(rm[:, :], lg, AX.X, ALU.max))
                nc.vector.tensor_tensor(logit[:, :, :], lg, wide(rm[:, :]), ALU.subtract).then_inc(c_shift, 1)

            def router_2(c):
                dve.wait_ge(c_exp, c + 1)
                then(nc.vector.tensor_reduce(rm[:, :], r1[:, :, :], AX.X, ALU.add))
                then(nc.vector.reciprocal(rm2[:, :], rm[:, :]))
                then(nc.vector.tensor_tensor(logit[:, :, :], r1[:, :, :], wide(rm2[:, :]), ALU.mult))
                then(nc.vector.tensor_reduce(rm[:, :], logit[:, :, :], AX.X, ALU.max))
                then(nc.vector.tensor_tensor(r1[:, :, :], logit[:, :, :], wide(rm[:, :]), ALU.is_equal))
                then(nc.vector.tensor_tensor(r2[:, :, :], r1[:, :, :], keys, ALU.mult))
                then(nc.vector.tensor_reduce(rm[:, :], r2[:, :, :], AX.X, ALU.max))
                then(nc.vector.tensor_tensor(sel1[:, :, :], r2[:, :, :], wide(rm[:, :]), ALU.is_equal))

            def router_3():
                then(nc.vector.scalar_tensor_tensor(r1[:, :, :], sel1[:, :, :], -2.0, logit[:, :, :], ALU.mult, ALU.add))
                then(nc.vector.tensor_reduce(rm[:, :], r1[:, :, :], AX.X, ALU.max))
                then(nc.vector.tensor_tensor(r2[:, :, :], r1[:, :, :], wide(rm[:, :]), ALU.is_equal))
                then(nc.vector.tensor_tensor(r1[:, :, :], r2[:, :, :], keys, ALU.mult))
                then(nc.vector.tensor_reduce(rm[:, :], r1[:, :, :], AX.X, ALU.max))
                then(nc.vector.tensor_tensor(r2[:, :, :], r1[:, :, :], wide(rm[:, :]), ALU.is_equal))
                then(nc.vector.tensor_tensor(r1[:, :, :], sel1[:, :, :], r2[:, :, :], ALU.add))

            def router_4(c):
                then(nc.vector.tensor_tensor(r2[:, :, :], r1[:, :, :], logit[:, :, :], ALU.mult))
                then(nc.vector.tensor_reduce(rm[:, :], r2[:, :, :], AX.X, ALU.add))
                then(nc.vector.tensor_scalar(rm2[:, :], rm[:, :], 1e-9, None, ALU.add))
                then(nc.vector.reciprocal(rm[:, :], rm2[:, :]))
                nc.vector.tensor_tensor(wexp[:, :, :], r2[:, :, :], wide(rm[:, :]), ALU.mult).then_inc(c_w, 1)
                dve.wait_ge(c_w, c + 1)

            ROUTER_STEPS = 1 + 8 + 7 + 4

            def product(e, c, f):
                n = NF * e + f
                dve.wait_ge(c_silu, c * NE * NF + n + 1)
                dve.wait_ge(c_up, c * NE * NF + n + 1)
                nc.vector.scalar_tensor_tensor(hT[:, e % 2, f, :], ps[:, 2 + f, :], ffn_b[:, 1, e, f:f + 1],
                                               silu[:, f, :], ALU.add, ALU.mult).then_inc(c_h, 1)

            def weigh(e, c):
                dve.wait_ge(c_down, c * NE + e + 1)
                step.wait()
                for t in range(TPC):
                    part, share = ps[:, 4 + e % 2, t * P:(t + 1) * P], wexp[:, t, e:e + 1]
                    if e == 0:
                        step.done(nc.vector.tensor_scalar(acc[:, 0, t, :], part, share, None, ALU.mult))
                    else:
                        step.done(nc.vector.scalar_tensor_tensor(acc[:, 0, t, :], part, share, acc[:, 0, t, :],
                                                                 ALU.mult, ALU.add))

            def biased_keys(c):
                dve.wait_ge(d_k, c + 1)
                nc.vector.tensor_tensor(kl[:, :, :].rearrange("p (t h) d -> p t (h d)", t=TPC), bank(7),
                                        rows[:, D:2 * D].unsqueeze(1).broadcast_to([P, TPC, D]), ALU.add).then_inc(d_kb, 1)
                dve.wait_ge(d_kb, c + 1)
                nc.vector.tensor_reduce(km[:, :], kl[:, :, :], AX.X, ALU.max).then_inc(d_kmax, 1)

            def biased_values(c):
                dve.wait_ge(d_v, c + 1)
                nc.vector.tensor_tensor(vl[:, :, 0:D], bank(6), rows[:, 2 * D:3 * D].unsqueeze(1).broadcast_to([P, TPC, D]),
                                        ALU.add).then_inc(d_vs, 1)

            def key_values(c):
                dve.wait_ge(d_kv, c + 1)
                for a in range(2):
                    kv = ps[:, 7 - a, :].rearrange("p (t n) -> p t n", t=2)
                    two = bass.ds(c * TPC + 2 * a, 2)
                    step.done(nc.vector.tensor_tensor(kvd[:, two, 0:D], kv[:, :, 0:D],
                                                      block_mask.unsqueeze(1).broadcast_to([P, 2, D]), ALU.mult))
                    last = nc.vector.tensor_tensor(kvd[:, two, D:D + H], kv[:, :, D:D + 1].broadcast_to([P, 2, H]),
                                                   head_sel.unsqueeze(1).broadcast_to([P, 2, H]), ALU.mult)
                    if a == 0:
                        step.done(last)
                last.then_inc(d_kvd, 1)

            def low_tokens(c):
                tok = bass.ds(c * CH, CH)
                dve.wait_ge(ln_Ts, NCH + c + 1)
                dve.wait_ge(ln_all, c + 1)
                nc.vector.tensor_tensor(xn_lo[:, tok], xnT[:, 0, :], xn_hi[:, tok], ALU.subtract).then_inc(ln_lo, 1)

            EXPERT_STEPS = NE * TPC + 3 + 1

            def experts(c, last=False):
                for e in range(NE):
                    if e + 1 < NE:
                        for f in range(NF):
                            product(e + 1, c, f)
                    elif not last:
                        for f in range(NF):
                            product(0, c + 1, f)
                    weigh(e, c)
                    if e == 0 and not last:
                        variances(0, (c + 1) * TPC)
                    elif e == 1:
                        biased_keys(c)
                        if not last:
                            dve.wait_ge(ln_T, NCH + 1 + c)
                            normalised(NCH + 1 + c, 0, (c + 1) * TPC, xn[:, 0])
                    elif e == 2:
                        dve.wait_ge(c_bias, c + 1)
                        step.wait()
                        nc.vector.tensor_tensor(acc[:, 0], acc[:, 0], bank(6), ALU.add).then_inc(c_biased, 1)
                        dve.wait_ge(c_biased, c + 1)
                    elif e == 3:
                        if not last:
                            router_1(c + 1, 6)
                    elif e == 4:
                        biased_values(c)
                        if not last:
                            low_tokens(c + 1)
                    elif e == 5:
                        dve.wait_ge(d_ksum, c + 1)
                        nc.vector.reciprocal(km[:, :], km[:, :]).then_inc(d_kinv, 1)
                        if not last:
                            router_2(c + 1)
                    elif e == 6:
                        if not last:
                            router_3()
                    elif e == 7:
                        key_values(c)
                step.wait()
                done = nc.vector.scalar_tensor_tensor(x[:, bass.ds(c * TPC, TPC), :], acc[:, 0], tg[:, 2:3],
                                                      x[:, bass.ds(c * TPC, TPC), :], ALU.mult, ALU.add)
                if last:
                    done.then_inc(c_x, 1)
                else:
                    step.done(done)
                    router_4(c + 1)

            step.done(nc.vector.memset(vl[:, :, D:D + 1], 1.0))
            step.done(nc.vector.memset(one_row[:, :], 1.0))
            low_tokens(0)
            router_1(0, 5)
            for f in range(NF):
                product(0, 0, f)
            router_2(0)
            router_3()
            router_4(0)
            with dve.Fori(0, NCH - 1) as c:
                step.enter(c, EXPERT_STEPS + LN_STEPS + ROUTER_STEPS)
                experts(c)
                step.leave(NCH - 1)
            experts(NCH - 1, last=True)
            dve.wait_ge(c_x, 1)

            for pair in range(PAIRS):
                variances(2 * pair * TPC, 2 * pair * TPC, 2 * TPC)
            for pair in range(PAIRS):
                two = slice(2 * pair * TPC, 2 * (pair + 1) * TPC)
                normalised(LN_D + pair, two.start, two.start, xn_d[:, two], 2 * TPC)

            for c in range(NCH):
                dve.wait_ge(d_q, c + 1)
                logits = ps[:, 2 * c + 1, :].rearrange("p (h d) -> p h d", h=TPC * H)
                then(nc.vector.tensor_reduce(qm[:, c], logits, AX.X, ALU.max))
                nc.vector.tensor_tensor(ql[:, c], logits, qm[:, c].unsqueeze(2).broadcast_to([P, TPC * H, DH]),
                                        ALU.subtract).then_inc(d_qsh, 1)
            for c in range(NCH):
                dve.wait_ge(d_qe, c + 1)
                then(nc.vector.tensor_reduce(qm[:, c], ql[:, c], AX.X, ALU.add))
                nc.vector.reciprocal(qm[:, c], qm[:, c]).then_inc(d_qinv, 1)
            for c in range(NCH):
                dve.wait_ge(d_num, c + 1)
                then(nc.vector.reciprocal(dinv[:, c], ps[:, 2 * c, 0:TPC * H]))
                nc.vector.tensor_tensor(lo[:, c], ps[:, 2 * c + 1, :].rearrange("p (h d) -> p h d", h=TPC * H),
                                        dinv[:, c].unsqueeze(2).broadcast_to([P, TPC * H, DH]), ALU.mult).then_inc(d_o, 1)
            for pair in range(PAIRS):
                for c in (2 * pair, 2 * pair + 1):
                    tiles = x[:, c * TPC:(c + 1) * TPC, :]
                    dve.wait_ge(d_y, c + 1)
                    step.done(nc.vector.scalar_tensor_tensor(tiles, bank(2 * c + 1), tg[:, 1:2], tiles, ALU.mult, ALU.add))
                step.wait()
                variances(2 * pair * TPC, 2 * pair * TPC, 2 * TPC)
            for pair in range(PAIRS):
                two = slice(2 * pair * TPC, 2 * (pair + 1) * TPC)
                normalised(LN_E + pair, two.start, two.start, xn_d[:, two], 2 * TPC)
            for c in range(NCH):
                dve.wait_ge(e_logit, c + 1)
                lgt = ps[:, 2 * c + 1, 0:TPC * NE].rearrange("p (t e) -> p t e", t=TPC)
                then(nc.vector.tensor_reduce(em[:, c], lgt, AX.X, ALU.max))
                nc.vector.tensor_tensor(elog[:, c], lgt, wide(em[:, c]), ALU.subtract).then_inc(e_shift, 1)
            for c in range(NCH):
                dve.wait_ge(e_exp, c + 1)
                then(nc.vector.tensor_reduce(em[:, c], elog[:, c], AX.X, ALU.add))
                then(nc.vector.reciprocal(em[:, c], em[:, c]))
                nc.vector.tensor_tensor(probs[:, :, c * TPC:(c + 1) * TPC], elog[:, c].rearrange("p t e -> p e t"),
                                        em[:, c].unsqueeze(1).broadcast_to([P, NE, TPC]), ALU.mult).then_inc(e_p, 1)

            dve.wait_ge(e_pT, 1)
            step.done(nc.vector.tensor_copy(pS[:, :], ps[:, 7, 0:P]))
            step.done(nc.vector.memset(thr[:, :], 0))
            step.wait()
            for n in range(THRESHOLD_BITS):
                bit = 1 << (THRESHOLD_BITS - 1 - n)
                then(nc.vector.tensor_scalar(cand[:, :], thr[:, :], bit, None, ALU.bitwise_or))
                nc.vector.tensor_scalar(ind[:, :], pS[:, :], cand[:, :].bitcast(fp32), 0.0, ALU.is_ge, ALU.add,
                                        accum_out=cnt[:, 0:1]).then_inc(e_cnt, 1)
                dve.wait_ge(e_tot, n + 1)
                then(nc.vector.tensor_scalar(inc[:, :], ps[:, 6, 0:1], CAP - 0.5, float(bit), ALU.is_ge, ALU.mult))
                then(nc.vector.tensor_tensor(thr[:, :], thr[:, :], inc[:, :], ALU.bitwise_or))
            level = thr[:, :].bitcast(fp32)
            then(nc.vector.tensor_scalar(ind[:, :], pS[:, :], level, 0.0, ALU.is_gt, ALU.add, accum_out=cnt[:, 0:1]))
            nc.vector.tensor_scalar(ind2[:, :], pS[:, :], level, 0.0, ALU.is_equal, ALU.add,
                                    accum_out=cnt[:, 1:2]).then_inc(e_ties, 1)
            dve.wait_ge(e_ties, 1)
            then(nc.vector.tensor_tensor_scan(scan[:, :], ind2[:, :], ind2[:, :], 0.0, ALU.add, ALU.bypass))
            dve.wait_ge(e_tie_tot, 1)
            then(nc.vector.tensor_scalar(need[:, :], ps[:, 6, 0:1], -1.0, CAP + 0.5, ALU.mult, ALU.add))
            then(nc.vector.tensor_tensor(off[:, :], need[:, :], ps[:, 6, 1:2], ALU.subtract))
            then(nc.vector.tensor_scalar(scan[:, :], scan[:, :], off[:, 0:1], None, ALU.is_le))
            then(nc.vector.tensor_tensor(scan[:, :], scan[:, :], ind2[:, :], ALU.mult))
            nc.vector.tensor_tensor(selT[:, :], scan[:, :], ind[:, :], ALU.add).then_inc(e_sel, 1)
            dve.wait_ge(e_selT, 1)

            def over_experts(a):
                return a.rearrange("p e t -> p t e")

            def wide(a):
                return a.unsqueeze(1).broadcast_to([P, NE, NB])

            chosen = ps[:, 7, 0:P].rearrange("p (e t) -> p e t", e=NE)
            then(nc.vector.tensor_reduce(cm[:, :], over_experts(chosen), AX.X, ALU.max))
            then(nc.vector.tensor_scalar(cm[:, :], cm[:, :], -1.0, 1.0, ALU.mult, ALU.add))
            then(nc.vector.tensor_tensor(c1[:, :, :], chosen, wide(cm[:, :]), ALU.add))
            then(nc.vector.tensor_tensor(c2[:, :, :], c1[:, :, :], probs[:, :, :], ALU.mult))
            then(nc.vector.scalar_tensor_tensor(c1[:, :, :], c1[:, :, :], -1.0, c2[:, :, :], ALU.add, ALU.add))
            then(nc.vector.tensor_reduce(cm[:, :], over_experts(c1[:, :, :]), AX.X, ALU.max))
            then(nc.vector.tensor_tensor(c2[:, :, :], c1[:, :, :], wide(cm[:, :]), ALU.is_equal))
            then(nc.vector.tensor_tensor(c1[:, :, :], c2[:, :, :], key.unsqueeze(2).broadcast_to([P, NE, NB]), ALU.mult))
            then(nc.vector.tensor_reduce(cm[:, :], over_experts(c1[:, :, :]), AX.X, ALU.max))
            then(nc.vector.tensor_tensor(c2[:, :, :], c1[:, :, :], wide(cm[:, :]), ALU.is_equal))
            then(nc.vector.tensor_tensor(gates[:, :, :], c2[:, :, :], probs[:, :, :], ALU.mult))

            for c in range(NCH):
                for e in range(NE):
                    dve.wait_ge(e_part, c * NE + e + 1)
                    if c or e:
                        dve.wait_ge(e_acc, c * NE + e)
                    for t in range(TPC):
                        part, share = parts[:, c % 2, e, t, :], gates[:, e, c * TPC + t:c * TPC + t + 1]
                        if e == 0:
                            last = nc.vector.tensor_scalar(acc[:, c % 2, t, :], part, share, None, ALU.mult)
                        else:
                            last = nc.vector.scalar_tensor_tensor(acc[:, c % 2, t, :], part, share, acc[:, c % 2, t, :],
                                                                  ALU.mult, ALU.add)
                    last.then_inc(e_acc, 1)
                dve.wait_ge(e_acc, (c + 1) * NE)
                tiles = x[:, c * TPC:(c + 1) * TPC, :]
                nc.vector.scalar_tensor_tensor(tiles, acc[:, c % 2], tg[:, 3:4], tiles, ALU.mult, ALU.add).then_inc(e_x, 1)

        @block.scalar
        def _(act):
            act.wait_ge(ld_w, N_W)
            nc.scalar.activation(base_h[:, :], wb[:, D:D + 1], ACT.Gelu, scale=5.545177444479562).then_inc(base_hidden, 1)

            def high_weights(m, e):
                full, high, _ = SPLITS[m]
                nc.scalar.activation(high[:, e:e + SPLIT], full[:, e:e + SPLIT], ACT.Copy).then_inc(w_hi, 1)

            def transposed(k, result, n, high=None):
                act.wait_ge(ln_T, k + 1)
                nc.scalar.activation(result, ps[:, n, :], ACT.Copy).then_inc(ln_Ts, 1)
                if high is not None:
                    nc.scalar.activation(xn_hi[:, high], ps[:, n, :], ACT.Copy).then_inc(ln_all, 1)

            def front(c):
                transposed(c, xnT[:, c % 2, :], 7)
                act.wait_ge(a_v, c + 1)
                nc.scalar.activation(v_all[:, c * TPC:(c + 1) * TPC].rearrange("p t h d -> p t (h d)"), bank(3),
                                     ACT.Copy).then_inc(a_vs, 1)
                act.wait_ge(a_q, c + 1)
                if c >= 2:
                    act.wait_ge(a_qg, c - 1)
                nc.scalar.activation(qT[:, c % 2, :], ps[:, 1, :], ACT.Copy).then_inc(a_qs, 1)

            front(0)
            for c in range(NCH):
                for n in range(2 * HQ):
                    act.wait_ge(a_hid, 2 * HQ * c + n + 1)
                    nc.scalar.activation(hid[:, n, :], ps[:, 4 + n % 3, :], ACT.Gelu).then_inc(a_gelu, 1)
                    if n == 4 and c + 1 < NCH:
                        front(c + 1)
                if c == 1 or c == 2:
                    act.wait_ge(ld_ffn, N_FFN)
                    for e in range(0, NE, SPLIT):
                        high_weights(c - 1, e)
                act.wait_ge(a_gate, c + 1)
                nc.scalar.activation(gate[:, c % 2, :], ps[:, 0, :], ACT.Tanh).then_inc(a_tanh, 1)

            nc.scalar.activation(tg[:, :], rows[:, 4 * D:4 * D + 4], ACT.Tanh).then_inc(tanh_g, 1)

            def probabilities(b, half):
                act.wait_ge(b_st, 2 * b + half + 1)
                nc.scalar.activation(pT[:, 8 * half:8 * half + 8, :].rearrange("p (a h) n -> p a (h n)", a=2),
                                     ps[:, 2 + 2 * half:4 + 2 * half, :], ACT.Exp).then_inc(b_exp, 1)

            def attended(b):
                act.wait_ge(b_av, b + 1)
                nc.scalar.activation(avT[:, :], ps[:, 6, :], ACT.Copy).then_inc(b_avs, 1)

            def output(b):
                act.wait_ge(b_aoT, b + 1)
                nc.scalar.activation(aoT[:, :], ps[:, 7, 0:P], ACT.Copy).then_inc(b_aoTs, 1)

            act.wait_ge(w_lo, NE // SPLIT)
            probabilities(0, 0)
            probabilities(0, 1)
            with act.Fori(1, NB) as b:
                attended(b - 1)
                probabilities(b, 0)
                probabilities(b, 1)
                output(b - 1)
            transposed(NCH, xnT[:, 0, :], 0, bass.ds(0, CH))
            attended(NB - 1)
            output(NB - 1)

            def routed(c):
                act.wait_ge(c_shift, c + 1)
                nc.scalar.activation(r1[:, :, :], logit[:, :, :], ACT.Exp).then_inc(c_exp, 1)

            def weights_T(c, n):
                act.wait_ge(c_wT, c + 1)
                nc.scalar.activation(wT[:, :], ps[0:NE, n, :], ACT.Copy).then_inc(c_wTs, 1)

            def activate(c, e):
                for f in range(NF):
                    n = c * NE * NF + NF * e + f
                    act.wait_ge(c_gate, n + 1)
                    if e or not isinstance(c, int) or c:
                        act.wait_ge(c_h, n - NF + 1)
                    nc.scalar.activation(silu[:, f, :], ps[:, f, :], ACT.Silu, bias=ffn_b[:, 0, e, f:f + 1]).then_inc(c_silu, 1)

            def experts(c, last=False):
                for e in range(NE):
                    if e + 1 < NE:
                        activate(c, e + 1)
                    elif not last:
                        activate(c + 1, 0)
                    if e == 1:
                        weights_T(c, 6)
                    elif e == 2 and not last:
                        transposed(NCH + 1 + c, xnT[:, 0, :], 7, bass.ds(CH * (c + 1), CH))
                    elif e == 4:
                        act.wait_ge(d_ksh, c + 1)
                        nc.scalar.activation(kl[:, :, :], kl[:, :, :], ACT.Exp).then_inc(d_ke, 1)
                        if not last:
                            routed(c + 1)

            routed(0)
            activate(0, 0)
            with act.Fori(0, NCH - 1) as c:
                experts(c)
            experts(NCH - 1, last=True)

            for e in range(0, NE, SPLIT):
                high_weights(2, e)
            for c in range(NCH):
                transposed(2 * NCH + c, xnT_d[:, c, :], 2 * c)
            for c in range(NCH):
                act.wait_ge(d_qsh, c + 1)
                nc.scalar.activation(ql[:, c], ql[:, c], ACT.Exp).then_inc(d_qe, 1)
            for c in range(NCH):
                act.wait_ge(d_qT, c + 1)
                nc.scalar.activation(qnT[:, c, :], ps[:, 2 * c, :], ACT.Copy).then_inc(d_qTs, 1)
            for c in range(NCH):
                act.wait_ge(d_oT, c + 1)
                nc.scalar.activation(loT[:, c, :], ps[:, 2 * c, :], ACT.Copy).then_inc(d_oTs, 1)
            for c in range(NCH):
                transposed(3 * NCH + c, xnT_d[:, c, :], 2 * c, slice(c * CH, (c + 1) * CH))
            for c in range(NCH):
                act.wait_ge(e_shift, c + 1)
                nc.scalar.activation(elog[:, c], elog[:, c], ACT.Exp).then_inc(e_exp, 1)

            for c in range(NCH):
                for e in range(NE + 1):
                    if e < NE:
                        for f in range(NF):
                            act.wait_ge(e_h, (c * NE + e) * NF + f + 1)
                            if c * NE + e >= 2:
                                act.wait_ge(e_down, c * NE + e - 1)
                            nc.scalar.activation(hT[:, e % 2, f, :], ps[:, 2 * (e % 2) + f, :], ACT.Gelu).then_inc(e_gelu, 1)
                    if e:
                        act.wait_ge(e_down, c * NE + e)
                        if c == 0 and e == 1:
                            act.wait_ge(ln_lo, 2 * NCH)
                        if c >= 2:
                            act.wait_ge(e_acc, (c - 2) * NE + e)
                        nc.scalar.activation(parts[:, c % 2, e - 1], bank(4 + (e - 1) % 2), ACT.Copy).then_inc(e_part, 1)

        @block.tensor
        def _(pe):
            mm, tr = nc.tensor.matmul, nc.tensor.transpose
            pe.wait_ge(ld_w, N_W)
            pe.wait_ge(base_hidden, 1)
            mm(ps[:, 0, 0:1], wb[:, 0:D], base_h[:, :], start=True, stop=True).then_inc(base_out, 1)
            pe.wait_ge(set_up, 2)

            def transpose_chunk(k, tiles, n):
                pe.wait_ge(ln_xn, TPC * (k + 1))
                for t in range(TPC):
                    last = tr(ps[:, n, t * P:(t + 1) * P], tiles[:, t, :], ident)
                last.then_inc(ln_T, 1)

            def front(c):
                tok = c * CH
                if c:
                    pe.wait_ge(a_ks, c)
                mm(ps[:, 2, :], square(W_K0), ctxT[:, tok:tok + CH], start=True, stop=True).then_inc(a_k, 1)
                if c:
                    pe.wait_ge(a_vs, c)
                for t in range(TPC):
                    last = mm(ps[:, 3, t * P:(t + 1) * P], ctxT[:, tok + t * P:tok + (t + 1) * P], square(W_V0),
                              start=True, stop=True)
                last.then_inc(a_v, 1)
                if c:
                    pe.wait_ge(ln_Ts, c)
                transpose_chunk(c, xn[:, c % 2], 7)

            def queries(c):
                pe.wait_ge(ln_Ts, c + 1)
                if c:
                    pe.wait_ge(a_qs, c)
                mm(ps[:, 1, :], square(W_Q0), xnT[:, c % 2, :], start=True, stop=True).then_inc(a_q, 1)

            pe.wait_ge(ld_ctx, 16)
            front(0)
            queries(0)
            for c in range(NCH):
                pe.wait_ge(a_qs, c + 1)
                for n in range(2 * HQ):
                    if 2 * HQ * c + n >= 3:
                        pe.wait_ge(a_gelu, 2 * HQ * c + (n - 2 if n >= 3 else 0))
                    mm(ps[:, 4 + n % 3, :], wg1[:, n, :], qT[:, c % 2, :],
                       start=True, stop=True).then_inc(a_hid, 1)
                    if c + 1 < NCH:
                        if n == 2:
                            front(c + 1)
                        elif n == 4:
                            queries(c + 1)
                pe.wait_ge(a_gelu, 2 * HQ * (c + 1))
                if c:
                    pe.wait_ge(a_tanh, c)
                for h in range(2):
                    for g in range(HQ):
                        last = mm(ps[32 * g:32 * g + 32, 0, :], wg2[:, h, :], hid[:, 2 * g + h, :],
                                  start=(h == 0), stop=(h == 1))
                last.then_inc(a_gate, 1)
            pe.wait_ge(a_tanh, NCH)
            pe.wait_ge(a_ks, NCH)

            def route(tokens_T, r, n, ready):
                for t in range(TPC):
                    last = mm(ps[:, n, t * NE:(t + 1) * NE], tokens_T[:, t * P:(t + 1) * P], routers[:, r, :],
                              start=True, stop=True)
                last.then_inc(ready, 1)

            def scores(b, s, g):
                if g == 0:
                    pe.wait_ge(b_prep, 5 * b + 2)
                n = 4 * b + g
                if not isinstance(n, int) or n >= 2:
                    pe.wait_ge(b_max, n - 1)
                mm(ps[:, g % 2, :], q_st[32 * g:32 * g + 32, s, :],
                   k_bd[32 * g:32 * g + 32, s].rearrange("p j m -> p (j m)"), start=True, stop=False)
                mm(ps[:, g % 2, :], ident_b[:, :], mask_b[:, 0, :].unsqueeze(1).broadcast_to([P, HQ, P]),
                   start=False, stop=True).then_inc(b_sn, 1)

            def scores_T(b, s, g):
                if g == 0:
                    pe.wait_ge(b_prep, 5 * b + 4)
                    pe.wait_ge(b_max, 4 * b + 4)
                if g % 2 == 0 and (not isinstance(b, int) or b >= 1):
                    pe.wait_ge(b_exp, 2 * b + g // 2 - 1)
                mm(ps[:, 2 + g, :], k_st[32 * g:32 * g + 32, s, :],
                   q_bd[32 * g:32 * g + 32, s].rearrange("p j n -> p (j n)"), start=True, stop=False)
                for j in range(HQ):
                    h = HQ * g + j
                    mm(ps[:, 2 + g, j * P:(j + 1) * P], nmax[:, s, h:h + 1].to_broadcast([P, P]), ident_b[:, :],
                       start=False, stop=False)
                last = mm(ps[:, 2 + g, :], ident_b[:, :], mask_b[:, 1, :].unsqueeze(1).broadcast_to([P, HQ, P]),
                          start=False, stop=True)
                if g % 2:
                    last.then_inc(b_st, 1)

            def attend(b, s):
                pe.wait_ge(b_prep, 5 * b + 5)
                pe.wait_ge(b_exp, 2 * b + 2)
                for a in range(HQ):
                    for j in range(HQ):
                        last = mm(ps[32 * j:32 * j + 32, 6, a * P:(a + 1) * P], v_st[:, s, HQ * a + j, :],
                                  pT[:, HQ * a + j, :], start=True, stop=True)
                last.then_inc(b_av, 1)

            def natural(b):
                pe.wait_ge(b_avs, b + 1)
                if not isinstance(b, int) or b >= 1:
                    pe.wait_ge(b_x, b)
                for a in range(HQ):
                    last = tr(ps[:, 7, a * P:(a + 1) * P], avT[:, a * P:(a + 1) * P], ident)
                last.then_inc(b_nat, 1)

            def out_T(b):
                pe.wait_ge(b_ao, b + 1)
                tr(ps[:, 7, 0:P], ao[:, :], ident).then_inc(b_aoT, 1)

            def project(b):
                pe.wait_ge(b_aoTs, b + 1)
                mm(ps[:, 7, P:2 * P], aoT[:, :], square(W_O0), start=True, stop=True).then_inc(b_y, 1)

            def slot(b, s, last=False):
                attend(b - 1, 1 - s)
                scores_T(b, s, 0)
                scores_T(b, s, 1)
                natural(b - 1)
                if not last:
                    scores(b + 1, 1 - s, 0)
                scores_T(b, s, 2)
                if not last:
                    scores(b + 1, 1 - s, 1)
                scores_T(b, s, 3)
                out_T(b - 1)
                if not last:
                    scores(b + 1, 1 - s, 2)
                    scores(b + 1, 1 - s, 3)
                project(b - 1)

            for g in range(4):
                scores(0, 0, g)
            for g in range(4):
                scores_T(0, 0, g)
            for g in range(4):
                scores(1, 1, g)
            slot(1, 1)
            with pe.Fori(1, NB // 2 - 1) as r:
                slot(2 * r, 0)
                slot(2 * r + 1, 1)
            slot(NB - 2, 0)
            slot(NB - 1, 1, last=True)
            transpose_chunk(NCH, xn[:, 0], 0)
            attend(NB - 1, 1)
            natural(NB - 1)
            pe.wait_ge(ln_Ts, NCH + 1)
            route(xnT[:, 0, :], 0, 5, c_logit)
            out_T(NB - 1)
            project(NB - 1)

            def split_product(out, weights_hi, weights_lo, tok):
                mm(out, weights_lo, xn_hi[:, tok], start=True, stop=False)
                mm(out, weights_hi, xn_lo[:, tok], start=False, stop=False)
                return mm(out, weights_hi, xn_hi[:, tok], start=False, stop=True)

            pe.wait_ge(ld_ffn, N_FFN)
            pe.wait_ge(w_lo, 2 * NE // SPLIT)

            def gate_up(c, e):
                tok = bass.ds(c * CH, CH)
                if e == 0:
                    pe.wait_ge(ln_lo, c + 1)
                for f in range(NF):
                    cols = slice(f * P, (f + 1) * P)
                    n = c * NE * NF + e * NF + f
                    if e or not isinstance(c, int) or c:
                        pe.wait_ge(c_silu, n - NF + 1)
                        pe.wait_ge(c_h, n - NF + 1)
                    split_product(ps[:, f, :], gate_hi[:, e, cols], gate_lo[:, e, cols], tok).then_inc(c_gate, 1)
                    split_product(ps[:, 2 + f, :], up_hi[:, e, cols], up_lo[:, e, cols], tok).then_inc(c_up, 1)

            def down(c, e):
                pe.wait_ge(c_h, (c * NE + e + 1) * NF)
                for t in range(TPC):
                    for f in range(NF):
                        last = mm(ps[:, 4 + e % 2, t * P:(t + 1) * P], hT[:, e % 2, f, t * P:(t + 1) * P],
                                  down_w[:, e, f, :], start=(f == 0), stop=(f == NF - 1))
                last.then_inc(c_down, 1)

            def weights_T(c, n):
                pe.wait_ge(c_w, c + 1)
                for t in range(TPC):
                    last = tr(ps[0:NE, n, t * P:(t + 1) * P], wexp[:, t, :], ident)
                last.then_inc(c_wT, 1)

            def experts(c, last=False):
                for e in range(NE):
                    if e + 1 < NE:
                        gate_up(c, e + 1)
                    elif not last:
                        gate_up(c + 1, 0)
                    down(c, e)
                    if e == 1:
                        weights_T(c, 6)
                        pe.wait_ge(ld_ctx_c, 16 * (c + 1))
                        for t in range(TPC):
                            done = mm(ps[:, 7, t * P:(t + 1) * P], ctxT_c[:, t * P:(t + 1) * P], square(W_K1),
                                      start=True, stop=True)
                        done.then_inc(d_k, 1)
                    elif e == 2:
                        pe.wait_ge(c_wTs, c + 1)
                        for t in range(TPC):
                            done = mm(ps[:, 6, t * P:(t + 1) * P], wT[:, t * P:(t + 1) * P], down_b[:, :],
                                      start=True, stop=True)
                        done.then_inc(c_bias, 1)
                        if not last:
                            pe.wait_ge(d_kb, c + 1)
                            transpose_chunk(NCH + 1 + c, xn[:, 0], 7)
                    elif e == 3:
                        if not last:
                            pe.wait_ge(ln_Ts, NCH + 2 + c)
                            pe.wait_ge(c_biased, c + 1)
                            route(xnT[:, 0, :], 0, 6, c_logit)
                    elif e == 4:
                        if not last:
                            pe.wait_ge(c_shift, c + 2)
                        else:
                            pe.wait_ge(c_biased, c + 1)
                        for t in range(TPC):
                            done = mm(ps[:, 6, t * P:(t + 1) * P], ctxT_c[:, t * P:(t + 1) * P], square(W_V1),
                                      start=True, stop=True)
                        done.then_inc(d_v, 1)
                    elif e == 6:
                        pe.wait_ge(d_kn, c + 1)
                        pe.wait_ge(d_vs, c + 1)
                        for t in range(TPC):
                            done = mm(ps[:, 7 - t // 2, (t % 2) * 256:(t % 2) * 256 + D + 1],
                                      kl[:, t * H:(t + 1) * H].rearrange("p h d -> p (h d)"), vl[:, t, :],
                                      start=True, stop=True)
                        done.then_inc(d_kv, 1)

            pe.wait_ge(b_x, NB)
            gate_up(0, 0)
            with pe.Fori(0, NCH - 1) as c:
                experts(c)
            experts(NCH - 1, last=True)

            pe.wait_ge(c_x, 1)
            for c in range(NCH):
                transpose_chunk(2 * NCH + c, xn_d[:, c * TPC:(c + 1) * TPC], 2 * c)
            for c in range(NCH):
                pe.wait_ge(ln_Ts, 2 * NCH + c + 1)
                for t in range(TPC):
                    col = ps[:, 2 * c + 1, t * P:(t + 1) * P]
                    mm(col, one_row[:, :], rows[0:1, 0:D], start=True, stop=False)
                    last = mm(col, xnT_d[:, c, t * P:(t + 1) * P], square(W_Q1), start=False, stop=True)
                last.then_inc(d_q, 1)
            for c in range(NCH):
                pe.wait_ge(d_qn, c + 1)
                for t in range(TPC):
                    last = tr(ps[:, 2 * c, t * P:(t + 1) * P], ql[:, c, t * H:(t + 1) * H].rearrange("p h d -> p (h d)"),
                              ident)
                last.then_inc(d_qT, 1)
            for c in range(NCH):
                pe.wait_ge(d_qTs, c + 1)
                for t in range(TPC):
                    q_tile = qnT[:, c, t * P:(t + 1) * P]
                    mm(ps[:, 2 * c + 1, t * P:(t + 1) * P], q_tile, kvd[:, c * TPC + t, 0:D], start=True, stop=True)
                    last = mm(ps[:, 2 * c, t * H:(t + 1) * H], q_tile, kvd[:, c * TPC + t, D:D + H], start=True, stop=True)
                last.then_inc(d_num, 1)
            for c in range(NCH):
                pe.wait_ge(d_o, c + 1)
                for t in range(TPC):
                    last = tr(ps[:, 2 * c, t * P:(t + 1) * P], lo[:, c, t * H:(t + 1) * H].rearrange("p h d -> p (h d)"),
                              ident)
                last.then_inc(d_oT, 1)
            for c in range(NCH):
                pe.wait_ge(d_oTs, c + 1)
                for t in range(TPC):
                    tok, col = slice(t * P, (t + 1) * P), ps[:, 2 * c + 1, t * P:(t + 1) * P]
                    mm(col, qnT[:, c, tok], square(W_P1), start=True, stop=False)
                    mm(col, loT[:, c, tok], square(W_P1), start=False, stop=False)
                    last = mm(col, one_row[:, :], rows[0:1, 3 * D:4 * D], start=False, stop=True)
                last.then_inc(d_y, 1)
            for c in range(NCH):
                transpose_chunk(3 * NCH + c, xn_d[:, c * TPC:(c + 1) * TPC], 2 * c)
            for c in range(NCH):
                pe.wait_ge(ln_Ts, 3 * NCH + c + 1)
                route(xnT_d[:, c, :], 1, 2 * c + 1, e_logit)

            pe.wait_ge(e_p, NCH)
            tr(ps[:, 7, 0:P], probs[:, :, :].rearrange("p e t -> p (e t)"), ident).then_inc(e_pT, 1)

            def threshold_count(n):
                pe.wait_ge(e_cnt, n + 1)
                mm(ps[:, 6, 0:1], sum16, cnt[:, 0:1], start=True, stop=True).then_inc(e_tot, 1)

            def choice_step(n):
                if n < THRESHOLD_BITS:
                    threshold_count(n)
                elif n == THRESHOLD_BITS:
                    pe.wait_ge(e_ties, 1)
                    mm(ps[:, 6, 0:1], sum16, cnt[:, 0:1], start=True, stop=True)
                    mm(ps[:, 6, 1:2], tri16, cnt[:, 1:2], start=True, stop=True).then_inc(e_tie_tot, 1)
                elif n == THRESHOLD_BITS + 1:
                    pe.wait_ge(e_sel, 1)
                    tr(ps[:, 7, 0:P], selT[:, :], ident).then_inc(e_selT, 1)

            choice = 0

            def first(n):
                c, e = n // NE, n % NE
                if n == 0:
                    pe.wait_ge(w_lo, 3 * NE // SPLIT)
                if e == 0:
                    pe.wait_ge(ln_lo, NCH + c + 1)
                for f in range(NF):
                    cols = slice(f * P, (f + 1) * P)
                    if n >= 2:
                        pe.wait_ge(e_gelu, (n - 2) * NF + f + 1)
                    split_product(ps[:, 2 * (e % 2) + f, :], w1_hi[:, e, cols], w1_lo[:, e, cols],
                                  slice(c * CH, (c + 1) * CH)).then_inc(e_h, 1)

            def second(n):
                c, e = n // NE, n % NE
                pe.wait_ge(e_gelu, (n + 1) * NF)
                if n >= 2:
                    pe.wait_ge(e_part, n - 1)
                for t in range(TPC):
                    for f in range(NF):
                        last = mm(ps[:, 4 + e % 2, t * P:(t + 1) * P], hT[:, e % 2, f, t * P:(t + 1) * P],
                                  w2[:, e, f, :], start=(f == 0), stop=(f == NF - 1))
                last.then_inc(e_down, 1)

            first(0)
            for n in range(NCH * NE):
                choice_step(choice)
                if n + 1 < NCH * NE:
                    first(n + 1)
                choice_step(choice + 1)
                choice += 2
                second(n)


def kernel(**inputs):
    import numpy as np
    import concourse.bacc as bacc
    from concourse.bass_utils import run_bass_kernel_spmd

    def a(name):
        return np.asarray(inputs[name])

    f = np.float32
    cst = np.zeros((P, C_END), f)
    r = np.arange(P)
    cst[:, C_IDENT:C_IDENT + P] = np.eye(P)
    cst[:, C_BLOCK:C_BLOCK + P] = r[:, None] // DH == r[None, :] // DH
    cst[:, C_SUM16:C_SUM16 + P] = r[:, None] // NB == r[None, :] // NB
    cst[:, C_TRI16:C_TRI16 + P] = (r[:, None] // NB == r[None, :] // NB) & (r[:, None] < r[None, :])
    cst[:, C_HEAD:C_HEAD + H] = r[:, None] // DH == np.arange(H)[None, :]
    cst[:, C_QUAD:C_QUAD + HQ] = (r[:, None] % 32) // DH == np.arange(HQ)[None, :]
    cst[:, C_KEY:C_KEY + NE] = NE - np.arange(NE)[None, :]
    wg1 = np.zeros((P, 2 * HQ, P), f)
    wg2 = np.zeros((P, 2, 32), f)
    for g in range(HQ):
        for j in range(HQ):
            wg1[32 * g + DH * j:32 * g + DH * (j + 1), 2 * g + j // 2, HID * (j % 2):HID * (j % 2 + 1)] = a("L0_xattn_wg1").T
    for j in range(HQ):
        wg2[HID * (j % 2):HID * (j % 2 + 1), j // 2, DH * j:DH * (j + 1)] = a("L0_xattn_wg2").T
    squares = ["L0_xattn_wq", "L0_xattn_wk", "L0_xattn_wv", "L0_xattn_wo", "L1_xattn_Wq", "L1_xattn_Wk", "L1_xattn_Wv", "L1_xattn_Wp"]
    mask = a("mask_1x1xSxS2_bf1")[0, 0].view(np.uint8)

    def blocks(b):
        return b.reshape(NE, NF, P).transpose(2, 0, 1).reshape(P, NE * NF)

    data = {
        "cst": cst,
        "x": a("x"),
        "ctxT": a("ctx_1024").transpose(2, 0, 1).reshape(D, NB * P),
        "w": np.concatenate([a(n).T for n in squares], axis=1),
        "wg1": wg1,
        "wg2": wg2,
        "wb": np.concatenate([a("L0_xattn_wb2").T, a("L0_xattn_wb1")], axis=1),
        "rows": np.concatenate([a("L1_xattn_bq"), a("L1_xattn_bk"), a("L1_xattn_bv"), a("L1_xattn_bp"),
                                a("g_xattn"), a("g_ffn")])[None, :],
        "mask": np.stack([mask, mask.T], axis=1),
        "routers": np.stack([a("L0_ffn_router_w").T, a("L1_ffn_Wg")], axis=1),
        "down_b": a("L0_ffn_down_b"),
        "gate_w": a("L0_ffn_gate_w"),
        "up_w": a("L0_ffn_up_w"),
        "down_w": a("L0_ffn_down_w"),
        "gate_b": blocks(a("L0_ffn_gate_b")),
        "up_b": blocks(a("L0_ffn_up_b")),
        "w1": a("L1_ffn_W1"),
        "w2": a("L1_ffn_W2"),
    }
    nc = bacc.Bacc("TRN2", target_bir_lowering=False, num_devices=1)
    arrays, aps = {}, {}
    for name, value in data.items():
        value = np.ascontiguousarray(value)
        arrays[f"in_{name}"] = value
        aps[name] = nc.dram_tensor(f"in_{name}", value.shape, mybir.dt.from_np(value.dtype), kind="ExternalInput").ap()
    out = nc.dram_tensor("out", (NB, P, D), mybir.dt.float32, kind="ExternalOutput").ap()
    build(nc, aps, out)
    ran = run_bass_kernel_spmd(nc, [arrays], core_ids=[0])
    return ran.results[0]["out"]
```

```python
import concourse.bass as bass
from concourse import mybir
from contextlib import ExitStack

P = 128
NB = 16
D = 128
H = 16
DH = D // H
HQ = 4
HID = 64
NCH = 4
TPC = NB // NCH
CH = TPC * P
NE = 8
FF = 256
NF = FF // P
CAP = NB * P // NE
EPS = 1e-5
MASKED = -1e30
THRESHOLD_STEPS = 15

C_IDENT, C_BLOCK, C_SUM16, C_TRI16 = 0, 128, 256, 384
C_HEAD, C_QUAD, C_GROUP, C_KEY, C_END = 512, 528, 532, 536, 544
W_Q0, W_K0, W_V0, W_O0, W_Q1, W_K1, W_V1, W_P1 = range(8)


class Count:

    def __init__(self, engine, semaphore):
        self.engine, self.semaphore, self.base, self.k = engine, semaphore, 0, 0

    def done(self, instruction):
        self.k += 1
        return instruction.then_inc(self.semaphore, 1)

    def wait(self):
        self.engine.wait_ge(self.semaphore, self.base + self.k)

    def enter(self, index, per):
        self.start, self.base, self.k = self.base + self.k, self.base + self.k + index * per, 0
        self.per = per

    def leave(self, iterations):
        assert self.k == self.per, (self.k, self.per)
        self.base, self.k = self.start + iterations * self.per, 0


def build(nc, i, out):
    fp32, bf16, i32, fp32r = mybir.dt.float32, mybir.dt.bfloat16, mybir.dt.int32, mybir.dt.float32r
    ALU, ACT, AX = mybir.AluOpType, mybir.ActivationFunctionType, mybir.AxisListType
    ctx = ExitStack()
    with ctx:
        def sb(name, shape, dt=fp32):
            return ctx.enter_context(nc.sbuf_tensor(name, shape, dt))

        def sem(name):
            return ctx.enter_context(nc.semaphore(name))

        x = sb("x", [P, NB, D])
        cst = sb("cst", [P, C_END])
        w = sb("w", [P, 8 * D])
        wg1 = sb("wg1", [P, 2 * HQ, P])
        wg2 = sb("wg2", [P, 2, 32])
        wb = sb("wb", [HID, D + 1])
        routers = sb("routers", [P, 2, NE])
        rows = sb("rows", [P, 4 * D + 4])
        mask_u8 = sb("mask_u8", [P, 2, P], mybir.dt.uint8)
        down_w = sb("down_w", [P, NE, NF, D])
        ffn_b = sb("ffn_b", [P, 2, NE, NF])
        down_b = sb("down_b", [NE, D])
        w1 = sb("w1", [P, NE, FF])
        w2 = sb("w2", [P, NE, NF, D])
        gate_hi = sb("gate_hi", [P, NE, FF], fp32r)
        up_hi = sb("up_hi", [P, NE, FF], fp32r)
        gate_lo = sb("gate_lo", [P, NE, FF], fp32r)
        up_lo = sb("up_lo", [P, NE, FF], fp32r)
        w1_hi, w1_lo = gate_hi, gate_lo
        SPLIT = 2
        ident_b = sb("ident_b", [P, P], bf16)
        mask_b = sb("mask_b", [P, 2, P], bf16)
        mask_f = sb("mask_f", [P, 2, P])
        visible = sb("visible", [P, 2])
        tg = sb("tg", [P, 4])
        base_h = sb("base_h", [HID, 1])
        kscale = sb("kscale", [P, 1])
        minus_half = sb("minus_half", [P, 2 * TPC])
        stats = sb("stats", [P, NB, 6])
        mv = sb("mv", [P, NB, 3])
        var_eps = sb("var_eps", [P, NB])
        rstd = sb("rstd", [P, NB])
        xn = sb("xn", [P, 2, TPC, D])
        xnT = sb("xnT", [P, 2, CH])
        ctxT = sb("ctxT", [P, NB * P])
        ctxT_c = sb("ctxT_c", [P, CH])
        xn_hi = sb("xn_hi", [P, NB * P], fp32r)
        xn_lo = sb("xn_lo", [P, NB * P], fp32r)
        big = sb("big", [P, 4 * NB * P])
        qg_all = big[:, 0:NB * P]
        k_all = big[:, NB * P:2 * NB * P]
        v_all = big[:, 2 * NB * P:3 * NB * P].rearrange("p (b h d) -> p b h d", b=NB, h=H)
        pT = big[:, 3 * NB * P:].rearrange("p (h n) -> p h n", h=H)
        kvd_all = sb("kvd_all", [P, NB * (D + H)])
        kvd = kvd_all[:, :].rearrange("p (t n) -> p t n", t=NB)
        gate_w = big[:, 3 * NB * P:].rearrange("p (e f) -> p e f", e=NE)
        up_w = kvd_all[:, 0:NE * FF].rearrange("p (e f) -> p e f", e=NE)
        SPLITS = [(gate_w, gate_hi, gate_lo), (up_w, up_hi, up_lo), (w1, w1_hi, w1_lo)]
        qT = sb("qT", [P, 2, CH])
        hid = sb("hid", [P, 2 * HQ, CH])
        gate = sb("gate", [P, 2, CH])
        q_st = sb("q_st", [P, 2, HQ, P], bf16)
        k_hi, q_hi = (xn_hi[:, m * 2 * CH:(m + 1) * 2 * CH].rearrange("p (s g n) -> p s g n", s=2, g=HQ) for m in range(2))
        k_lo, q_lo = (xn_lo[:, m * 2 * CH:(m + 1) * 2 * CH].rearrange("p (s g n) -> p s g n", s=2, g=HQ) for m in range(2))
        k_bd = sb("k_bd", [P, 2, HQ, P], bf16)
        v_st = sb("v_st", [P, 2, H, 32])
        nmax = sb("nmax", [P, 2, H], bf16)
        avT = sb("avT", [P, CH])
        rsum = sb("rsum", [P, H])
        rinv = sb("rinv", [P, H])
        ao = sb("ao", [P, D])
        aoT = sb("aoT", [P, P])
        silu = hid[:, 0:NF, :]
        hT = hid[:, NF:3 * NF, :].rearrange("p (s f) n -> p s f n", s=2)
        acc = ctxT[:, 0:CH].rearrange("p (t n) -> p t n", t=TPC)
        wexp = sb("wexp", [P, TPC, NE])
        wT = sb("wT", [NE, CH])
        logit = sb("logit", [P, TPC, NE])
        r1 = sb("r1", [P, TPC, NE])
        r2 = sb("r2", [P, TPC, NE])
        sel1 = sb("sel1", [P, TPC, NE])
        rm = sb("rm", [P, TPC])
        rm2 = sb("rm2", [P, TPC])
        half_k = sb("half_k", [P, TPC * H, DH // 2])
        qm = sb("qm", [P, NCH, TPC * H])
        kl = ctxT[:, 2 * CH:3 * CH].rearrange("p (h d) -> p h d", h=TPC * H)
        km = sb("km", [P, TPC * H])
        vl = sb("vl", [P, TPC, D + 1])
        dinv = sb("dinv", [P, NCH, TPC * H])
        elog = sb("elog", [P, NB, NE])
        em = sb("em", [P, NB])
        one_row = sb("one_row", [1, P])
        bias_p = sb("bias_p", [P, D])
        xn_d = big[:, 0:NB * P].rearrange("p (t n) -> p t n", t=NB)
        xnT_d = big[:, NB * P:2 * NB * P].rearrange("p (c n) -> p c n", c=NCH)
        ql = big[:, 2 * NB * P:3 * NB * P].rearrange("p (c h d) -> p c h d", c=NCH, h=TPC * H)
        lo = big[:, 3 * NB * P:].rearrange("p (c h d) -> p c h d", c=NCH, h=TPC * H)
        qnT = hid[:, 0:NCH, :]
        loT = hid[:, NCH:2 * NCH, :]
        probs = sb("probs", [P, NE, NB])
        pS, ind, ind2, scan = (ctxT[:, 3 * CH + n * P:3 * CH + (n + 1) * P] for n in range(4))
        thr = sb("thr", [P, 1], i32)
        cand = sb("cand", [P, 3], i32)
        inc = sb("inc", [P, 1], i32)
        cnt = sb("cnt", [P, 3])
        enough = sb("enough", [P, 3])
        digit = sb("digit", [P, 1])
        over = gate[:, 0, 0:3 * P].rearrange("p (k n) -> p k n", k=3)
        need = sb("need", [P, 1])
        off = sb("off", [P, 1])
        selT = sb("selT", [P, P])
        c1 = sb("c1", [P, NE, NB])
        c2 = sb("c2", [P, NE, NB])
        cm = sb("cm", [P, NB])
        gates = sb("gates", [P, NE, NB])

        ps = ctx.enter_context(nc.psum_tensor("ps", [P, 8, 512], fp32))

        def bank(n, parts=TPC):
            return ps[:, n, :].rearrange("p (t n) -> p t n", t=parts)

        def numerators_of(c, first, end):
            n, start = (2 * c, 0) if first == TPC - 1 else (2 * c + 1, first * (D + H))
            return ps[:, n, start:start + (end - first) * (D + H)].rearrange("p (t n) -> p t n", n=D + H)

        ident = cst[:, C_IDENT:C_IDENT + P]
        block_mask = cst[:, C_BLOCK:C_BLOCK + P]
        sum16 = cst[:, C_SUM16:C_SUM16 + P]
        tri16 = cst[:, C_TRI16:C_TRI16 + P]
        head_sel = cst[:, C_HEAD:C_HEAD + H]
        quad_sel = cst[:, C_QUAD:C_QUAD + HQ]
        group_sel = cst[:, C_GROUP:C_GROUP + HQ]
        key = cst[:, C_KEY:C_KEY + NE]

        def square(n):
            return w[:, n * D:(n + 1) * D]

        ld_x, ld_w, ld_ffn, ld_ctx = sem("ld_x"), sem("ld_w"), sem("ld_ffn"), sem("ld_ctx")
        stored, ld_ctx_c = sem("stored"), sem("ld_ctx_c")
        dve_step, pool_step = sem("dve_step"), sem("pool_step")
        base_hidden, base_out, set_up, tanh_g = sem("base_hidden"), sem("base_out"), sem("set_up"), sem("tanh_g")
        w_hi, w_lo, ln_lo = sem("w_hi"), sem("w_lo"), sem("ln_lo")
        ln_var, ln_rstd, ln_xn, ln_T, ln_Ts, ln_all = (
            sem(n) for n in ("ln_var", "ln_rstd", "ln_xn", "ln_T", "ln_Ts", "ln_all"))
        a_q, a_k, a_v, a_qs, a_ks, a_vs = (sem(n) for n in ("a_q", "a_k", "a_v", "a_qs", "a_ks", "a_vs"))
        a_hid, a_gelu, a_gate, a_tanh, a_qg = (sem(n) for n in ("a_hid", "a_gelu", "a_gate", "a_tanh", "a_qg"))
        b_low = sem("b_low")
        b_prep, b_sn, b_max, b_st, b_exp = (sem(n) for n in ("b_prep", "b_sn", "b_max", "b_st", "b_exp"))
        b_av, b_avs, b_nat, b_ao, b_aoT, b_aoTs, b_y, b_x = (
            sem(n) for n in ("b_av", "b_avs", "b_nat", "b_ao", "b_aoT", "b_aoTs", "b_y", "b_x"))
        c_logit, c_w, c_wT, c_wTs, c_bias = (sem(n) for n in ("c_logit", "c_w", "c_wT", "c_wTs", "c_bias"))
        c_shift, c_exp, c_biased = sem("c_shift"), sem("c_exp"), sem("c_biased")
        c_gate, c_up, c_silu, c_h, c_down, c_x = (sem(n) for n in ("c_gate", "c_up", "c_silu", "c_h", "c_down", "c_x"))
        d_k, d_v, d_kb, d_kmax, d_ksum, d_kinv, d_ksh, d_ke, d_kn, d_vs, d_kv, d_kvd = (
            sem(n) for n in ("d_k", "d_v", "d_kb", "d_kmax", "d_ksum", "d_kinv", "d_ksh", "d_ke", "d_kn", "d_vs", "d_kv", "d_kvd"))
        d_q, d_qsh, d_qe, d_qinv, d_xb, d_bias, d_sum, d_qn, d_qT, d_qTs, d_num, d_o, d_oT, d_oTs, d_y = (
            sem(n) for n in ("d_q", "d_qsh", "d_qe", "d_qinv", "d_xb", "d_bias", "d_sum", "d_qn", "d_qT", "d_qTs", "d_num", "d_o", "d_oT", "d_oTs",
                             "d_y"))
        e_logit, e_shift, e_exp, e_p, e_pT, e_cnt, e_tot, e_ties, e_tie_tot, e_sel, e_selT, e_gates = (
            sem(n) for n in ("e_logit", "e_shift", "e_exp", "e_p", "e_pT", "e_cnt", "e_tot", "e_ties",
                             "e_tie_tot", "e_sel", "e_selT", "e_gates"))
        e_h, e_gelu, e_down, e_part, e_acc, e_acc_0 = (
            sem(n) for n in ("e_h", "e_gelu", "e_down", "e_part", "e_acc", "e_acc_0"))
        block = ctx.enter_context(nc.Block())

        PARTS = [big[:, k * CH:(k + 1) * CH] for k in range(2 * NE)] + [
            m[:, 2 * k:2 * k + 2].rearrange(r, n=P) for m, r in (
                (w1, "p e (u n) -> p (e u) n"), (down_w, "p e f n -> p (e f) n")) for k in range(NE // 2)]

        LAST, LAST_BANKS = NCH * NE - 1, (5, 0)

        def part(n):
            p = PARTS[n % len(PARTS)]
            return p.rearrange("p (t n) -> p t n", t=TPC) if len(p.shape) == 2 else p

        N_X, N_W, N_FFN = 16, 9 * 16, 7 * 16
        LN_D, LN_E = 2 * NCH, 3 * NCH
        CHOICE = 6

        @block.sync
        def _(sp):
            sp.dma_start(cst[:, :], i["cst"]).then_inc(ld_w, 16)
            sp.dma_start(x[:, :, :], i["x"].rearrange("b p d -> p b d")).then_inc(ld_x, 16)
            sp.dma_start(w[:, :], i["w"]).then_inc(ld_w, 16)
            sp.dma_start(wg1[:, :, :], i["wg1"]).then_inc(ld_w, 16)
            sp.dma_start(wg2[:, :, :], i["wg2"]).then_inc(ld_w, 16)
            sp.dma_start(wb[:, :], i["wb"]).then_inc(ld_w, 16)
            sp.dma_start(rows[:, :], i["rows"].broadcast_to([P, 4 * D + 4])).then_inc(ld_w, 16)
            sp.dma_start(mask_u8[:, :, :], i["mask"]).then_inc(ld_w, 16)
            sp.dma_start(routers[:, :, :], i["routers"]).then_inc(ld_w, 16)
            sp.dma_start(down_b[:, :], i["down_b"]).then_inc(ld_w, 16)
            sp.dma_start(ctxT[:, :], i["ctxT"]).then_inc(ld_ctx, 16)
            sp.dma_start(gate_w[:, :, :], i["gate_w"].rearrange("e d f -> d e f")).then_inc(ld_ffn, 16)
            sp.dma_start(up_w[:, :, :], i["up_w"].rearrange("e d f -> d e f")).then_inc(ld_ffn, 16)
            sp.dma_start(down_w[:, :, :, :], i["down_w"].rearrange("e (f p) d -> p e f d", p=P)).then_inc(ld_ffn, 16)
            sp.dma_start(ffn_b[:, 0], i["gate_b"].rearrange("p (e f) -> p e f", e=NE)).then_inc(ld_ffn, 16)
            sp.dma_start(ffn_b[:, 1], i["up_b"].rearrange("p (e f) -> p e f", e=NE)).then_inc(ld_ffn, 16)
            sp.dma_start(w1[:, :, :], i["w1"].rearrange("e d f -> d e f")).then_inc(ld_ffn, 16)
            sp.dma_start(w2[:, :, :, :], i["w2"].rearrange("e (f p) d -> p e f d", p=P)).then_inc(ld_ffn, 16)
            sp.dma_start(ctxT_c[:, :], i["ctxT"][:, 0:CH]).then_inc(ld_ctx_c, 16)
            with sp.Fori(1, NCH) as c:
                sp.wait_ge(d_v, c)
                sp.dma_start(ctxT_c[:, :], i["ctxT"][:, bass.ds(c * CH, CH)]).then_inc(ld_ctx_c, 16)
            for c in (1, 0, 2, 3):
                if c:
                    sp.wait_ge(e_acc, c * NE)
                else:
                    sp.wait_ge(e_acc_0, NE)
                tiles = slice(c * TPC, (c + 1) * TPC)
                sp.dma_start(out.rearrange("b p d -> p b d")[:, tiles, :], x[:, tiles, :]).then_inc(stored, 16)
            sp.wait_ge(stored, 16 * NCH)

        @block.gpsimd
        def _(pool):
            step = Count(pool, pool_step)
            step.done(nc.gpsimd.memset(minus_half[:, :], -0.5))
            nc.gpsimd.memset(v_st[:, :, :, :], 0.0).then_inc(pool_step, 1)
            step.k += 1
            step.wait()
            step.done(nc.gpsimd.memset(v_st[:, :, :, DH:DH + 1], 1.0))
            step.wait()

            def layer_norm(k, slot, n=TPC):
                pool.wait_ge(ln_var, k + 1)
                nc.gpsimd.tensor_tensor(rstd[:, slot:slot + n], var_eps[:, slot:slot + n], minus_half[:, 0:n],
                                        ALU.pow).then_inc(ln_rstd, 1)

            def low_weights(first, m):
                full, high, low = SPLITS[m]
                for e in range(0, NE, SPLIT):
                    pool.wait_ge(w_hi, first + e // SPLIT + 1)
                    nc.gpsimd.tensor_tensor(low[:, e:e + SPLIT], full[:, e:e + SPLIT], high[:, e:e + SPLIT],
                                            ALU.subtract).then_inc(w_lo, 1)

            for c in range(NCH):
                layer_norm(c, c % 2 * TPC)
            low_weights(0, 0)

            pool.wait_ge(ld_w, N_W)
            def prepare(b, s):
                def expand(result, source, select):
                    nc.gpsimd.tensor_tensor(
                        result[:, s], source[:, bass.ds(b * P, P)].unsqueeze(1).broadcast_to([P, HQ, P]),
                        select.unsqueeze(2).broadcast_to([P, HQ, P]), ALU.mult).then_inc(b_prep, 1)

                if not isinstance(b, int):
                    pool.wait_ge(b_sn, 4 * b - 4)
                expand(q_st, qg_all, group_sel)
                if not isinstance(b, int):
                    pool.wait_ge(b_st, 2 * b - 2)
                expand(k_bd, k_all, quad_sel)
                expand(k_hi, k_all, group_sel)
                expand(q_hi, qg_all, quad_sel)
                if not isinstance(b, int):
                    pool.wait_ge(b_av, b - 1)
                nc.gpsimd.tensor_copy(v_st[:, s, :, 0:DH], v_all[:, b]).then_inc(b_prep, 1)

            pool.wait_ge(a_qg, 1)
            pool.wait_ge(a_ks, 1)
            pool.wait_ge(a_vs, 1)
            prepare(0, 0)
            prepare(1, 1)
            low_weights(NE // SPLIT, 1)

            pool.wait_ge(a_qg, NCH)
            pool.wait_ge(a_ks, NCH)
            pool.wait_ge(a_vs, NCH)
            with pool.Fori(1, NB // 2) as g:
                for s in range(2):
                    b = 2 * g + s
                    prepare(b, s)

            tt = nc.gpsimd.tensor_tensor

            def then(instruction):
                step.done(instruction)
                step.wait()

            def all_keys(a):
                return a.unsqueeze(2).broadcast_to([P, TPC * H, DH])

            def keys_1(c):
                pool.wait_ge(d_kmax, c + 1)
                tt(kl[:, :, :], kl[:, :, :], all_keys(km[:, :]), ALU.subtract).then_inc(d_ksh, 1)

            def keys_2(c):
                pool.wait_ge(d_ke, c + 1)
                then(tt(half_k[:, :, 0:4], kl[:, :, 0:4], kl[:, :, 4:8], ALU.add))
                then(tt(half_k[:, :, 0:2], half_k[:, :, 0:2], half_k[:, :, 2:4], ALU.add))
                tt(km[:, :].unsqueeze(2), half_k[:, :, 0:1], half_k[:, :, 1:2], ALU.add).then_inc(d_ksum, 1)
                pool.wait_ge(d_kinv, c + 1)
                tt(kl[:, :, :], kl[:, :, :], all_keys(km[:, :]), ALU.mult).then_inc(d_kn, 1)

            layer_norm(NCH, 0)
            with pool.Fori(0, NCH - 1) as c:
                step.enter(c, 2)
                layer_norm(NCH + 1 + c, 0)
                keys_1(c)
                keys_2(c)
                step.leave(NCH - 1)
            layer_norm(LN_D, 0)
            keys_1(NCH - 1)
            for c in range(1, NCH - 1):
                layer_norm(LN_D + c, c * TPC)
            keys_2(NCH - 1)
            low_weights(2 * NE // SPLIT, 2)
            layer_norm(LN_D + NCH - 1, (NCH - 1) * TPC)

            def add_bias(c):
                tiles = x[:, c * TPC:(c + 1) * TPC, :]
                pool.wait_ge(ln_xn, TPC * (LN_D + c + 1))
                tt(tiles, tiles, bias_p[:, :].unsqueeze(1).broadcast_to([P, TPC, D]), ALU.add).then_inc(d_xb, 1)

            pool.wait_ge(d_bias, 1)
            for c in range(NCH - 1):
                add_bias(c)
            for c in range(NCH):
                if c == NCH - 1:
                    add_bias(c)
                pool.wait_ge(d_qinv, c + 1)
                tt(ql[:, c], ql[:, c], all_keys(qm[:, c]), ALU.mult).then_inc(d_qn, 1)
            for c in range(NCH):
                pool.wait_ge(d_o, c + 1)
                tt(lo[:, c], lo[:, c], ql[:, c], ALU.add).then_inc(d_sum, 1)
            def low_tokens(c):
                tok = slice(c * CH, (c + 1) * CH)
                pool.wait_ge(ln_Ts, 3 * NCH + c + 1)
                pool.wait_ge(ln_all, NCH + c + 1)
                tt(xn_lo[:, tok], xnT_d[:, c, :], xn_hi[:, tok], ALU.subtract).then_inc(ln_lo, 1)

            for c in range(NCH):
                layer_norm(LN_E + c, c * TPC)
                if c > 1:
                    low_tokens(c - 1)
            low_tokens(NCH - 1)
            pool.wait_ge(e_gates, 1)
            for e in range(NE):
                share = gates[:, e, 0:TPC].unsqueeze(2).broadcast_to([P, TPC, D])
                pool.wait_ge(e_part, e + 1)
                then(tt(part(e), part(e), share, ALU.mult))
                if e:
                    pool.wait_ge(e_acc_0, e)
                tt(x[:, 0:TPC, :], x[:, 0:TPC, :], part(e), ALU.add).then_inc(e_acc_0, 1)

        @block.vector
        def _(dve):
            step = Count(dve, dve_step)
            dve.wait_ge(ld_w, N_W)
            nc.vector.tensor_copy(ident_b[:, :], ident).then_inc(set_up, 1)
            step.done(nc.vector.tensor_copy(mask_f[:, :, :], mask_u8[:, :, :]))
            step.wait()
            nc.vector.tensor_scalar(mask_b[:, :, :], mask_f[:, :, :], -1.0, -MASKED, ALU.add, ALU.mult).then_inc(set_up, 1)
            step.done(nc.vector.tensor_reduce(visible[:, 0:1], mask_f[:, 0, :], AX.X, ALU.add))
            step.wait()
            step.done(nc.vector.reciprocal(visible[:, 0:1], visible[:, 0:1]))
            step.wait()
            step.done(nc.vector.tensor_scalar(visible[:, 1:2], visible[:, 0:1], 0.0, None, ALU.mult))
            dve.wait_ge(base_out, 1)
            step.done(nc.vector.tensor_scalar(kscale[:, :], ps[:, 0, 0:1], float(DH) ** -0.5, None, ALU.mult))
            step.wait()
            dve.wait_ge(ld_x, N_X)

            def variances(slot, tile, n=TPC):
                for t in range(n):
                    step.done(nc.vector.bn_stats(stats[:, slot + t, :], x[:, tile + t, :]))
                step.wait()
                own = stats[:, slot:slot + n]
                even, odd = own[:, :, 0:3], own[:, :, 3:6]
                m = mv[:, slot:slot + n]
                step.done(nc.vector.tensor_tensor(m[:, :, 0], even[:, :, 1], odd[:, :, 1], ALU.add))
                step.done(nc.vector.tensor_tensor(m[:, :, 1], even[:, :, 1], odd[:, :, 1], ALU.subtract))
                step.done(nc.vector.tensor_tensor(m[:, :, 2], even[:, :, 2], odd[:, :, 2], ALU.add))
                step.wait()
                step.done(nc.vector.tensor_scalar(m[:, :, 0], m[:, :, 0], 0.5, None, ALU.mult))
                step.done(nc.vector.scalar_tensor_tensor(m[:, :, 1], m[:, :, 1], 0.25, m[:, :, 1], ALU.mult, ALU.mult))
                step.done(nc.vector.tensor_scalar(m[:, :, 2], m[:, :, 2], 1.0 / D, EPS, ALU.mult, ALU.add))
                step.wait()
                nc.vector.tensor_tensor(var_eps[:, slot:slot + n], m[:, :, 1], m[:, :, 2], ALU.add).then_inc(ln_var, 1)

            def normalised(k, slot, tile, result, n=TPC):
                dve.wait_ge(ln_rstd, k + 1)
                for t in range(n):
                    nc.vector.tensor_scalar(result[:, t, :], x[:, tile + t, :], mv[:, slot + t, 0:1],
                                            rstd[:, slot + t:slot + t + 1], ALU.subtract, ALU.mult).then_inc(ln_xn, 1)

            def layer_norm(k, q, tile):
                variances(q * TPC, tile)
                if k >= 2:
                    dve.wait_ge(ln_T, k - 1)
                normalised(k, q * TPC, tile, xn[:, q])

            LN_STEPS = TPC + 6

            def low_parts(b, s):
                dve.wait_ge(b_prep, 5 * b + 4)
                for source, high, low, select in ((k_all, k_hi, k_lo, group_sel), (qg_all, q_hi, q_lo, quad_sel)):
                    for n in range(HQ):
                        last = nc.vector.scalar_tensor_tensor(low[:, s, n, :], source[:, bass.ds(b * P, P)],
                                                              select[:, n:n + 1], high[:, s, n, :],
                                                              ALU.mult, ALU.subtract)
                last.then_inc(b_low, 1)

            layer_norm(0, 0, 0)
            layer_norm(1, 1, TPC)
            for c in range(NCH):
                dve.wait_ge(a_k, c + 1)
                nc.vector.tensor_scalar(k_all[:, c * CH:(c + 1) * CH], ps[:, 2, :], kscale[:, 0:1], None,
                                        ALU.mult).then_inc(a_ks, 1)
                if c + 2 < NCH:
                    layer_norm(c + 2, c % 2, (c + 2) * TPC)
                if c == NCH - 1:
                    low_parts(0, 0)
                    low_parts(1, 1)
                dve.wait_ge(a_tanh, c + 1)
                nc.vector.scalar_tensor_tensor(qg_all[:, c * CH:(c + 1) * CH], gate[:, c % 2, :], 1.0, qT[:, c % 2, :],
                                               ALU.add, ALU.mult).then_inc(a_qg, 1)

            def maximum(b, s, g):
                dve.wait_ge(b_sn, 4 * b + g + 1)
                nc.vector.tensor_reduce(nmax[:, s, HQ * g:HQ * (g + 1)], bank(g % 2), AX.X, ALU.max,
                                        negate=True).then_inc(b_max, 1)

            def normalise(b):
                dve.wait_ge(b_nat, b + 1)
                av = ps[:, 7, :].rearrange("p (h d) -> p h d", h=H)
                step.done(nc.vector.tensor_scalar(rsum[:, :], av[:, :, DH], visible[:, 1:2], None, ALU.add))
                step.wait()
                step.done(nc.vector.reciprocal(rinv[:, :], rsum[:, :]))
                step.wait()
                nc.vector.tensor_tensor(ao[:, :].rearrange("p (a j d) -> p a j d", a=HQ, j=HQ), ps[:, 7, :].rearrange(
                    "p (a j d) -> p a j d", a=HQ, j=HQ)[:, :, :, 0:DH], rinv[:, :].rearrange(
                    "p (a j) -> p a j", a=HQ).unsqueeze(3).broadcast_to([P, HQ, HQ, DH]), ALU.mult).then_inc(b_ao, 1)

            def residual(b):
                dve.wait_ge(b_y, b + 1)
                nc.vector.scalar_tensor_tensor(x[:, b, :], ps[:, 7, P:2 * P], tg[:, 0:1], x[:, b, :],
                                               ALU.mult, ALU.add).then_inc(b_x, 1)

            def slot(b, s, last=False):
                if not isinstance(b, int) or b >= 2:
                    residual(b - 2)
                if not last:
                    maximum(b + 1, 1 - s, 0)
                    maximum(b + 1, 1 - s, 1)
                normalise(b - 1)
                if not last:
                    low_parts(b + 1, 1 - s)
                    maximum(b + 1, 1 - s, 2)
                    maximum(b + 1, 1 - s, 3)

            dve.wait_ge(tanh_g, 1)
            for b in range(2):
                for g in range(4):
                    maximum(b, b, g)
            slot(1, 1)
            with dve.Fori(1, NB // 2 - 1) as r:
                step.enter(r - 1, 4)
                slot(2 * r, 0)
                slot(2 * r + 1, 1)
                step.leave(NB // 2 - 2)
            slot(NB - 2, 0)
            dve.wait_ge(b_x, NB - 4)
            variances(0, 0)
            residual(NB - 3)
            dve.wait_ge(ln_T, NCH - 1)
            normalised(NCH, 0, 0, xn[:, 0])
            normalise(NB - 2)

            def wide(a):
                return a.unsqueeze(2).broadcast_to([P, TPC, NE])

            keys = key.unsqueeze(1).broadcast_to([P, TPC, NE])

            def then(instruction):
                step.done(instruction)
                step.wait()

            def router_1(c, logit_bank):
                dve.wait_ge(c_logit, c + 1)
                lg = ps[:, logit_bank, 0:TPC * NE].rearrange("p (t e) -> p t e", t=TPC)
                then(nc.vector.tensor_reduce(rm[:, :], lg, AX.X, ALU.max))
                nc.vector.tensor_tensor(logit[:, :, :], lg, wide(rm[:, :]), ALU.subtract).then_inc(c_shift, 1)

            def router_2(c):
                dve.wait_ge(c_exp, c + 1)
                then(nc.vector.tensor_reduce(rm[:, :], r1[:, :, :], AX.X, ALU.add))
                then(nc.vector.reciprocal(rm2[:, :], rm[:, :]))
                then(nc.vector.tensor_tensor(logit[:, :, :], r1[:, :, :], wide(rm2[:, :]), ALU.mult))
                then(nc.vector.tensor_reduce(rm[:, :], logit[:, :, :], AX.X, ALU.max))
                then(nc.vector.tensor_tensor(r1[:, :, :], logit[:, :, :], wide(rm[:, :]), ALU.is_equal))
                then(nc.vector.tensor_tensor(r2[:, :, :], r1[:, :, :], keys, ALU.mult))
                then(nc.vector.tensor_reduce(rm[:, :], r2[:, :, :], AX.X, ALU.max))
                then(nc.vector.tensor_tensor(sel1[:, :, :], r2[:, :, :], wide(rm[:, :]), ALU.is_equal))

            def router_3():
                then(nc.vector.scalar_tensor_tensor(r1[:, :, :], sel1[:, :, :], -2.0, logit[:, :, :], ALU.mult, ALU.add))
                then(nc.vector.tensor_reduce(rm[:, :], r1[:, :, :], AX.X, ALU.max))
                then(nc.vector.tensor_tensor(r2[:, :, :], r1[:, :, :], wide(rm[:, :]), ALU.is_equal))
                then(nc.vector.tensor_tensor(r1[:, :, :], r2[:, :, :], keys, ALU.mult))
                then(nc.vector.tensor_reduce(rm[:, :], r1[:, :, :], AX.X, ALU.max))
                then(nc.vector.tensor_tensor(r2[:, :, :], r1[:, :, :], wide(rm[:, :]), ALU.is_equal))
                then(nc.vector.tensor_tensor(r1[:, :, :], sel1[:, :, :], r2[:, :, :], ALU.add))

            def router_4(c):
                then(nc.vector.tensor_tensor(r2[:, :, :], r1[:, :, :], logit[:, :, :], ALU.mult))
                then(nc.vector.tensor_reduce(rm[:, :], r2[:, :, :], AX.X, ALU.add))
                then(nc.vector.tensor_scalar(rm2[:, :], rm[:, :], 1e-9, None, ALU.add))
                then(nc.vector.reciprocal(rm[:, :], rm2[:, :]))
                nc.vector.tensor_tensor(wexp[:, :, :], r2[:, :, :], wide(rm[:, :]), ALU.mult).then_inc(c_w, 1)
                dve.wait_ge(c_w, c + 1)

            ROUTER_STEPS = 1 + 8 + 7 + 4

            def product(e, c, f):
                n = NF * e + f
                dve.wait_ge(c_silu, c * NE * NF + n + 1)
                dve.wait_ge(c_up, c * NE * NF + n + 1)
                nc.vector.scalar_tensor_tensor(hT[:, e % 2, f, :], ps[:, 2 + f, :], ffn_b[:, 1, e, f:f + 1],
                                               silu[:, f, :], ALU.add, ALU.mult).then_inc(c_h, 1)

            def weigh(e, c):
                dve.wait_ge(c_down, c * NE + e + 1)
                step.wait()
                for t in range(TPC):
                    part, share = ps[:, 4 + e % 2, t * P:(t + 1) * P], wexp[:, t, e:e + 1]
                    if e == 0:
                        step.done(nc.vector.tensor_scalar(acc[:, t, :], part, share, None, ALU.mult))
                    else:
                        step.done(nc.vector.scalar_tensor_tensor(acc[:, t, :], part, share, acc[:, t, :],
                                                                 ALU.mult, ALU.add))

            def biased_keys(c):
                dve.wait_ge(d_k, c + 1)
                nc.vector.tensor_tensor(kl[:, :, :].rearrange("p (t h) d -> p t (h d)", t=TPC), bank(7),
                                        rows[:, D:2 * D].unsqueeze(1).broadcast_to([P, TPC, D]), ALU.add).then_inc(d_kb, 1)
                dve.wait_ge(d_kb, c + 1)
                nc.vector.tensor_reduce(km[:, :], kl[:, :, :], AX.X, ALU.max).then_inc(d_kmax, 1)

            def biased_values(c):
                dve.wait_ge(d_v, c + 1)
                nc.vector.tensor_tensor(vl[:, :, 0:D], bank(6), rows[:, 2 * D:3 * D].unsqueeze(1).broadcast_to([P, TPC, D]),
                                        ALU.add).then_inc(d_vs, 1)

            def key_values(c):
                dve.wait_ge(d_kv, c + 1)
                for a in range(2):
                    kv = ps[:, 7 - a, :].rearrange("p (t n) -> p t n", t=2)
                    two = bass.ds(c * TPC + 2 * a, 2)
                    step.done(nc.vector.tensor_tensor(kvd[:, two, 0:D], kv[:, :, 0:D],
                                                      block_mask.unsqueeze(1).broadcast_to([P, 2, D]), ALU.mult))
                    last = nc.vector.tensor_tensor(kvd[:, two, D:D + H], kv[:, :, D:D + 1].broadcast_to([P, 2, H]),
                                                   head_sel.unsqueeze(1).broadcast_to([P, 2, H]), ALU.mult)
                    if a == 0:
                        step.done(last)
                last.then_inc(d_kvd, 1)

            def low_tokens(c):
                tok = bass.ds(c * CH, CH)
                dve.wait_ge(ln_Ts, NCH + c + 1)
                dve.wait_ge(ln_all, c + 1)
                nc.vector.tensor_tensor(xn_lo[:, tok], xnT[:, 0, :], xn_hi[:, tok], ALU.subtract).then_inc(ln_lo, 1)

            EXPERT_STEPS = NE * TPC + 3 + 1

            def variances_d(c):
                variances(c * TPC, c * TPC)

            def normalised_d(c):
                tiles = slice(c * TPC, (c + 1) * TPC)
                normalised(LN_D + c, c * TPC, c * TPC, xn_d[:, tiles])

            def experts(c, last=False):
                for e in range(NE):
                    if e + 1 < NE:
                        for f in range(NF):
                            product(e + 1, c, f)
                    elif not last:
                        for f in range(NF):
                            product(0, c + 1, f)
                    weigh(e, c)
                    if e == 0 and not last:
                        variances(0, (c + 1) * TPC)
                    elif e == 1:
                        biased_keys(c)
                        if not last:
                            dve.wait_ge(ln_T, NCH + 1 + c)
                            normalised(NCH + 1 + c, 0, (c + 1) * TPC, xn[:, 0])
                    elif e == 2:
                        dve.wait_ge(c_bias, c + 1)
                        step.wait()
                        nc.vector.tensor_tensor(acc[:, :, :], acc[:, :, :], bank(6), ALU.add).then_inc(c_biased, 1)
                        dve.wait_ge(c_biased, c + 1)
                    elif e == 3:
                        if not last:
                            router_1(c + 1, 6)
                    elif e == 4:
                        biased_values(c)
                        if not last:
                            low_tokens(c + 1)
                    elif e == 5:
                        dve.wait_ge(d_ksum, c + 1)
                        nc.vector.reciprocal(km[:, :], km[:, :]).then_inc(d_kinv, 1)
                        if not last:
                            router_2(c + 1)
                    elif e == 6:
                        if not last:
                            router_3()
                    elif e == 7 and not last:
                        key_values(c)
                    if last:
                        if e in (1, 3, 5):
                            normalised_d(e // 2)
                        if e in (0, 2, 4):
                            variances_d(e // 2)
                step.wait()
                done = nc.vector.scalar_tensor_tensor(x[:, bass.ds(c * TPC, TPC), :], acc[:, :, :], tg[:, 2:3],
                                                      x[:, bass.ds(c * TPC, TPC), :], ALU.mult, ALU.add)
                if last:
                    done.then_inc(c_x, 1)
                    dve.wait_ge(c_x, 1)
                    variances_d(c)
                    key_values(c)
                else:
                    step.done(done)
                    router_4(c + 1)

            step.done(nc.vector.memset(vl[:, :, D:D + 1], 1.0))
            step.done(nc.vector.memset(one_row[:, :], 1.0))
            nc.vector.tensor_scalar(bias_p[:, :], rows[:, 3 * D:4 * D], tg[:, 1:2], None, ALU.mult).then_inc(d_bias, 1)
            low_tokens(0)
            residual(NB - 2)
            normalise(NB - 1)
            router_1(0, 5)
            product(0, 0, 0)
            residual(NB - 1)
            router_2(0)
            product(0, 0, 1)
            router_3()
            router_4(0)
            with dve.Fori(0, NCH - 1) as c:
                step.enter(c, EXPERT_STEPS + LN_STEPS + ROUTER_STEPS)
                experts(c)
                step.leave(NCH - 1)
            experts(NCH - 1, last=True)

            def queries(c):
                dve.wait_ge(d_q, c + 1)
                logits = ps[:, 2 * c + 1, :].rearrange("p (h d) -> p h d", h=TPC * H)
                then(nc.vector.tensor_reduce(qm[:, c], logits, AX.X, ALU.max))
                nc.vector.tensor_tensor(ql[:, c], logits, qm[:, c].unsqueeze(2).broadcast_to([P, TPC * H, DH]),
                                        ALU.subtract).then_inc(d_qsh, 1)

            def query_sums(c):
                dve.wait_ge(d_qe, c + 1)
                then(nc.vector.tensor_reduce(qm[:, c], ql[:, c], AX.X, ALU.add))
                nc.vector.reciprocal(qm[:, c], qm[:, c]).then_inc(d_qinv, 1)

            queries(0)
            normalised_d(NCH - 1)
            queries(1)
            query_sums(0)
            queries(2)
            query_sums(1)
            query_sums(2)
            queries(3)
            query_sums(3)
            for c in range(NCH):
                dve.wait_ge(d_num, c + 1)
                groups = (numerators_of(c, 0, TPC - 1), 0, TPC - 1), (numerators_of(c, TPC - 1, TPC), TPC - 1, TPC)
                for both, first, end in groups:
                    inverse = dinv[:, c, first * H:end * H].rearrange("p (t h) -> p t h", h=H)
                    step.done(nc.vector.reciprocal(inverse, both[:, :, D:D + H]))
                step.wait()
                for n, (both, first, end) in enumerate(groups):
                    inverse = dinv[:, c, first * H:end * H].rearrange("p (t h) -> p t h", h=H)
                    last = nc.vector.tensor_tensor(
                        lo[:, c, first * H:end * H].rearrange("p (t h) d -> p t h d", h=H),
                        both[:, :, 0:D].rearrange("p t (h d) -> p t h d", h=H),
                        inverse.unsqueeze(3).broadcast_to([P, end - first, H, DH]), ALU.mult)
                last.then_inc(d_o, 1)

            def residual_d(c):
                tiles = x[:, c * TPC:(c + 1) * TPC, :]
                dve.wait_ge(d_xb, c + 1)
                dve.wait_ge(d_y, c + 1)
                step.done(nc.vector.scalar_tensor_tensor(tiles, bank(2 * c + 1), tg[:, 1:2], tiles, ALU.mult, ALU.add))

            residual_d(0)
            for c in range(NCH):
                step.wait()
                variances(c * TPC, c * TPC)
                if c == 1:
                    dve.wait_ge(ln_Ts, LN_E + 1)
                    dve.wait_ge(ln_all, NCH + 1)
                    nc.vector.tensor_tensor(xn_lo[:, 0:CH], xnT_d[:, 0, :], xn_hi[:, 0:CH], ALU.subtract).then_inc(ln_lo, 1)
                if c + 1 < NCH:
                    residual_d(c + 1)
                normalised(LN_E + c, c * TPC, c * TPC, xn_d[:, c * TPC:(c + 1) * TPC])
            dve.wait_ge(e_logit, NCH)
            lgt = ps[:, 6, 0:NB * NE].rearrange("p (t e) -> p t e", t=NB)
            then(nc.vector.tensor_reduce(em[:, :], lgt, AX.X, ALU.max))
            nc.vector.tensor_tensor(elog[:, :, :], lgt, em[:, :].unsqueeze(2).broadcast_to([P, NB, NE]),
                                    ALU.subtract).then_inc(e_shift, 1)
            dve.wait_ge(e_exp, 1)
            then(nc.vector.tensor_reduce(em[:, :], elog[:, :, :], AX.X, ALU.add))
            then(nc.vector.reciprocal(em[:, :], em[:, :]))
            nc.vector.tensor_tensor(probs[:, :, :], elog[:, :, :].rearrange("p t e -> p e t"),
                                    em[:, :].unsqueeze(1).broadcast_to([P, NE, NB]), ALU.mult).then_inc(e_p, 1)

            dve.wait_ge(e_pT, 1)
            step.done(nc.vector.tensor_copy(pS[:, :], ps[:, 7, 0:P]))
            step.done(nc.vector.memset(thr[:, :], 0))
            step.wait()
            for n in range(THRESHOLD_STEPS):
                unit = 1 << (2 * (THRESHOLD_STEPS - 1 - n))
                for k in range(3):
                    step.done(nc.vector.tensor_scalar(cand[:, k:k + 1], thr[:, :], (k + 1) * unit, None, ALU.bitwise_or))
                step.wait()
                for k in range(3):
                    last = nc.vector.tensor_scalar(over[:, k, :], pS[:, :], cand[:, k:k + 1].bitcast(fp32), 0.0,
                                                   ALU.is_ge, ALU.add, accum_out=cnt[:, k:k + 1])
                    if k < 2:
                        step.done(last)
                last.then_inc(e_cnt, 1)
                dve.wait_ge(e_tot, n + 1)
                then(nc.vector.tensor_scalar(enough[:, :], ps[:, 6, 0:3], CAP - 0.5, 0.0, ALU.is_ge, ALU.add,
                                             accum_out=digit[:, :]))
                then(nc.vector.tensor_scalar(inc[:, :], digit[:, :], float(unit), None, ALU.mult))
                then(nc.vector.tensor_tensor(thr[:, :], thr[:, :], inc[:, :], ALU.bitwise_or))
            level = thr[:, :].bitcast(fp32)
            then(nc.vector.tensor_scalar(ind[:, :], pS[:, :], level, 0.0, ALU.is_gt, ALU.add, accum_out=cnt[:, 0:1]))
            nc.vector.tensor_scalar(ind2[:, :], pS[:, :], level, 0.0, ALU.is_equal, ALU.add,
                                    accum_out=cnt[:, 1:2]).then_inc(e_ties, 1)
            dve.wait_ge(e_ties, 1)
            then(nc.vector.tensor_tensor_scan(scan[:, :], ind2[:, :], ind2[:, :], 0.0, ALU.add, ALU.bypass))
            dve.wait_ge(e_tie_tot, 1)
            then(nc.vector.tensor_scalar(need[:, :], ps[:, 6, 0:1], -1.0, CAP + 0.5, ALU.mult, ALU.add))
            then(nc.vector.tensor_tensor(off[:, :], need[:, :], ps[:, 6, 1:2], ALU.subtract))
            then(nc.vector.tensor_scalar(scan[:, :], scan[:, :], off[:, 0:1], None, ALU.is_le))
            then(nc.vector.tensor_tensor(scan[:, :], scan[:, :], ind2[:, :], ALU.mult))
            nc.vector.tensor_tensor(selT[:, :], scan[:, :], ind[:, :], ALU.add).then_inc(e_sel, 1)
            dve.wait_ge(e_selT, 1)

            def over_experts(a):
                return a.rearrange("p e t -> p t e")

            def wide(a):
                return a.unsqueeze(1).broadcast_to([P, NE, NB])

            chosen = ps[:, 7, 0:P].rearrange("p (e t) -> p e t", e=NE)
            then(nc.vector.tensor_reduce(cm[:, :], over_experts(chosen), AX.X, ALU.max))
            then(nc.vector.tensor_scalar(cm[:, :], cm[:, :], -1.0, 1.0, ALU.mult, ALU.add))
            then(nc.vector.tensor_tensor(c1[:, :, :], chosen, wide(cm[:, :]), ALU.add))
            then(nc.vector.tensor_tensor(c2[:, :, :], c1[:, :, :], probs[:, :, :], ALU.mult))
            then(nc.vector.scalar_tensor_tensor(c1[:, :, :], c1[:, :, :], -1.0, c2[:, :, :], ALU.add, ALU.add))
            then(nc.vector.tensor_reduce(cm[:, :], over_experts(c1[:, :, :]), AX.X, ALU.max))
            then(nc.vector.tensor_tensor(c2[:, :, :], c1[:, :, :], wide(cm[:, :]), ALU.is_equal))
            then(nc.vector.tensor_tensor(c1[:, :, :], c2[:, :, :], key.unsqueeze(2).broadcast_to([P, NE, NB]), ALU.mult))
            then(nc.vector.tensor_reduce(cm[:, :], over_experts(c1[:, :, :]), AX.X, ALU.max))
            then(nc.vector.tensor_tensor(c2[:, :, :], c1[:, :, :], wide(cm[:, :]), ALU.is_equal))
            nc.vector.scalar_tensor_tensor(gates[:, :, :], c2[:, :, :], tg[:, 3:4], probs[:, :, :],
                                           ALU.mult, ALU.mult).then_inc(e_gates, 1)
            dve.wait_ge(e_gates, 1)

            for c in range(1, NCH):
                for e in range(NE):
                    n = c * NE + e
                    if n < LAST:
                        dve.wait_ge(e_part, n + 1)
                    if c > 1 or e:
                        dve.wait_ge(e_acc, n - NE)
                    for t in range(TPC):
                        if n == LAST and t % 2 == 0:
                            dve.wait_ge(e_down, LAST + 1 + t // 2)
                        product = part(n)[:, t, :] if n < LAST else bank(LAST_BANKS[t // 2])[:, t, :]
                        tile = x[:, c * TPC + t, :]
                        last = nc.vector.scalar_tensor_tensor(tile, product, gates[:, e, c * TPC + t:c * TPC + t + 1], tile,
                                                              ALU.mult, ALU.add)
                    last.then_inc(e_acc, 1)

        @block.scalar
        def _(act):
            act.wait_ge(ld_w, N_W)
            nc.scalar.activation(base_h[:, :], wb[:, D:D + 1], ACT.Gelu, scale=5.545177444479562).then_inc(base_hidden, 1)

            def high_weights(m, e):
                full, high, _ = SPLITS[m]
                nc.scalar.activation(high[:, e:e + SPLIT], full[:, e:e + SPLIT], ACT.Copy).then_inc(w_hi, 1)

            def transposed(k, result, n, high=None):
                act.wait_ge(ln_T, k + 1)
                nc.scalar.activation(result, ps[:, n, :], ACT.Copy).then_inc(ln_Ts, 1)
                if high is not None:
                    nc.scalar.activation(xn_hi[:, high], ps[:, n, :], ACT.Copy).then_inc(ln_all, 1)

            def values(c):
                act.wait_ge(a_v, c + 1)
                nc.scalar.activation(v_all[:, c * TPC:(c + 1) * TPC].rearrange("p t h d -> p t (h d)"), bank(3),
                                     ACT.Copy).then_inc(a_vs, 1)

            def queries(c):
                act.wait_ge(a_q, c + 1)
                if c >= 2:
                    act.wait_ge(a_qg, c - 1)
                nc.scalar.activation(qT[:, c % 2, :], ps[:, 1, :], ACT.Copy).then_inc(a_qs, 1)

            values(0)
            transposed(0, xnT[:, 0, :], 7)
            queries(0)
            for c in range(NCH):
                for n in range(2 * HQ):
                    act.wait_ge(a_hid, 2 * HQ * c + n + 1)
                    nc.scalar.activation(hid[:, n, :], ps[:, 4 + n % 3, :], ACT.Gelu).then_inc(a_gelu, 1)
                    if c + 1 < NCH:
                        if n == 2:
                            transposed(c + 1, xnT[:, (c + 1) % 2, :], 7)
                        elif n == 5:
                            queries(c + 1)
                if c + 1 < NCH:
                    values(c + 1)
                if c == 1 or c == 2:
                    act.wait_ge(ld_ffn, N_FFN)
                    for e in range(0, NE, SPLIT):
                        high_weights(c - 1, e)
                act.wait_ge(a_gate, c + 1)
                nc.scalar.activation(gate[:, c % 2, :], ps[:, 0, :], ACT.Tanh).then_inc(a_tanh, 1)

            nc.scalar.activation(tg[:, :], rows[:, 4 * D:4 * D + 4], ACT.Tanh).then_inc(tanh_g, 1)

            def probabilities(b, half):
                act.wait_ge(b_st, 2 * b + half + 1)
                nc.scalar.activation(pT[:, 8 * half:8 * half + 8, :].rearrange("p (a h) n -> p a (h n)", a=2),
                                     ps[:, 2 + 2 * half:4 + 2 * half, :], ACT.Exp).then_inc(b_exp, 1)

            def attended(b):
                act.wait_ge(b_av, b + 1)
                nc.scalar.activation(avT[:, :], ps[:, 6, :], ACT.Copy).then_inc(b_avs, 1)

            def output(b):
                act.wait_ge(b_aoT, b + 1)
                nc.scalar.activation(aoT[:, :], ps[:, 7, 0:P], ACT.Copy).then_inc(b_aoTs, 1)

            act.wait_ge(w_lo, NE // SPLIT)
            probabilities(0, 0)
            probabilities(0, 1)
            with act.Fori(1, NB) as b:
                attended(b - 1)
                probabilities(b, 0)
                probabilities(b, 1)
                output(b - 1)
            transposed(NCH, xnT[:, 0, :], 0, bass.ds(0, CH))
            attended(NB - 1)

            def routed(c):
                act.wait_ge(c_shift, c + 1)
                nc.scalar.activation(r1[:, :, :], logit[:, :, :], ACT.Exp).then_inc(c_exp, 1)

            def weights_T(c, n):
                act.wait_ge(c_wT, c + 1)
                nc.scalar.activation(wT[:, :], ps[0:NE, n, :], ACT.Copy).then_inc(c_wTs, 1)

            def activate(c, e, blocks=range(NF)):
                for f in blocks:
                    n = c * NE * NF + NF * e + f
                    act.wait_ge(c_gate, n + 1)
                    if e or not isinstance(c, int) or c:
                        act.wait_ge(c_h, n - NF + 1)
                    nc.scalar.activation(silu[:, f, :], ps[:, f, :], ACT.Silu, bias=ffn_b[:, 0, e, f:f + 1]).then_inc(c_silu, 1)

            def experts(c, last=False):
                for e in range(NE):
                    if e + 1 < NE:
                        activate(c, e + 1)
                    elif not last:
                        activate(c + 1, 0)
                    if last and e >= 2 and (e % 2 == 0 or e == NE - 1):
                        high_weights(2, e - 2 if e < NE - 1 else NE - SPLIT)
                    if last and e in (2, 4, 6):
                        transposed(LN_D + e // 2 - 1, xnT_d[:, e // 2 - 1, :], 7)
                    if e == 1:
                        weights_T(c, 6)
                    elif e == 2 and not last:
                        transposed(NCH + 1 + c, xnT[:, 0, :], 7, bass.ds(CH * (c + 1), CH))
                    elif e == 4:
                        act.wait_ge(d_ksh, c + 1)
                        nc.scalar.activation(kl[:, :, :], kl[:, :, :], ACT.Exp).then_inc(d_ke, 1)
                        if not last:
                            routed(c + 1)

            routed(0)
            activate(0, 0, [0])
            output(NB - 1)
            activate(0, 0, range(1, NF))
            with act.Fori(0, NCH - 1) as c:
                experts(c)
            experts(NCH - 1, last=True)

            def query_exponentials(c):
                act.wait_ge(d_qsh, c + 1)
                nc.scalar.activation(ql[:, c], ql[:, c], ACT.Exp).then_inc(d_qe, 1)

            query_exponentials(0)
            transposed(LN_D + NCH - 1, xnT_d[:, NCH - 1, :], 6)

            def queries_D(c):
                act.wait_ge(d_qT, c + 1)
                nc.scalar.activation(qnT[:, c, :], ps[:, 2 * c, :], ACT.Copy).then_inc(d_qTs, 1)

            query_exponentials(1)
            query_exponentials(2)
            queries_D(0)
            query_exponentials(3)
            for c in range(1, NCH):
                queries_D(c)
            for c in range(NCH):
                act.wait_ge(d_oT, c + 1)
                nc.scalar.activation(loT[:, c, :], ps[:, 2 * c, :], ACT.Copy).then_inc(d_oTs, 1)
            def front(c, n):
                transposed(3 * NCH + c, xnT_d[:, c, :], n, slice(c * CH, (c + 1) * CH))

            front(0, 0)
            front(1, 4)

            for c in range(NCH):
                for e in range(NE + 1):
                    if e < NE:
                        for f in range(NF):
                            act.wait_ge(e_h, (c * NE + e) * NF + f + 1)
                            if c * NE + e >= 2:
                                act.wait_ge(e_down, c * NE + e - 1)
                            nc.scalar.activation(hT[:, e % 2, f, :], ps[:, 2 * (e % 2) + f, :], ACT.Gelu).then_inc(e_gelu, 1)
                    n = c * NE + e - 1
                    if e and n < LAST:
                        act.wait_ge(e_down, n + 1)
                        if n >= len(PARTS):
                            act.wait_ge(e_acc_0, n - len(PARTS) + 1)
                        if n == NCH:
                            act.wait_ge(ln_lo, 2 * NCH)
                        nc.scalar.activation(part(n), bank(4 + n % 2), ACT.Copy).then_inc(e_part, 1)
                        if n == 0:
                            front(2, 7)
                        elif n == 1:
                            front(3, 7)
                        elif n == 3:
                            act.wait_ge(e_shift, 1)
                            nc.scalar.activation(elog[:, :, :], elog[:, :, :], ACT.Exp).then_inc(e_exp, 1)

        @block.tensor
        def _(pe):
            mm, tr = nc.tensor.matmul, nc.tensor.transpose
            pe.wait_ge(ld_w, N_W)
            pe.wait_ge(base_hidden, 1)
            mm(ps[:, 0, 0:1], wb[:, 0:D], base_h[:, :], start=True, stop=True).then_inc(base_out, 1)
            pe.wait_ge(set_up, 2)

            def transpose_chunk(k, tiles, n):
                pe.wait_ge(ln_xn, TPC * (k + 1))
                for t in range(TPC):
                    last = tr(ps[:, n, t * P:(t + 1) * P], tiles[:, t, :], ident)
                last.then_inc(ln_T, 1)

            def keys_and_values(c):
                tok = c * CH
                if c:
                    pe.wait_ge(a_ks, c)
                mm(ps[:, 2, :], square(W_K0), ctxT[:, tok:tok + CH], start=True, stop=True).then_inc(a_k, 1)
                if c:
                    pe.wait_ge(a_vs, c)
                for t in range(TPC):
                    last = mm(ps[:, 3, t * P:(t + 1) * P], ctxT[:, tok + t * P:tok + (t + 1) * P], square(W_V0),
                              start=True, stop=True)
                last.then_inc(a_v, 1)

            def tokens_T(c):
                if c:
                    pe.wait_ge(ln_Ts, c)
                transpose_chunk(c, xn[:, c % 2], 7)

            def queries(c):
                pe.wait_ge(ln_Ts, c + 1)
                if c:
                    pe.wait_ge(a_qs, c)
                mm(ps[:, 1, :], square(W_Q0), xnT[:, c % 2, :], start=True, stop=True).then_inc(a_q, 1)

            pe.wait_ge(ld_ctx, 16)
            keys_and_values(0)
            tokens_T(0)
            queries(0)
            for c in range(NCH):
                pe.wait_ge(a_qs, c + 1)
                for n in range(2 * HQ):
                    if 2 * HQ * c + n >= 3:
                        pe.wait_ge(a_gelu, 2 * HQ * c + (n - 2 if n >= 3 else 0))
                    mm(ps[:, 4 + n % 3, :], wg1[:, n, :], qT[:, c % 2, :],
                       start=True, stop=True).then_inc(a_hid, 1)
                    if c + 1 < NCH:
                        if n == 2:
                            tokens_T(c + 1)
                        elif n == 5:
                            queries(c + 1)
                if c + 1 < NCH:
                    keys_and_values(c + 1)
                pe.wait_ge(a_gelu, 2 * HQ * (c + 1))
                if c:
                    pe.wait_ge(a_tanh, c)
                for h in range(2):
                    for g in range(HQ):
                        last = mm(ps[32 * g:32 * g + 32, 0, :], wg2[:, h, :], hid[:, 2 * g + h, :],
                                  start=(h == 0), stop=(h == 1))
                last.then_inc(a_gate, 1)
            pe.wait_ge(a_tanh, NCH)
            pe.wait_ge(a_ks, NCH)

            def route(tokens_T, r, n, ready, first=0):
                for t in range(TPC):
                    last = mm(ps[:, n, (first + t) * NE:(first + t + 1) * NE], tokens_T[:, t * P:(t + 1) * P], routers[:, r, :],
                              start=True, stop=True)
                last.then_inc(ready, 1)

            def scores(b, s, g):
                if g == 0:
                    pe.wait_ge(b_prep, 5 * b + 2)
                n = 4 * b + g
                if not isinstance(n, int) or n >= 2:
                    pe.wait_ge(b_max, n - 1)
                mm(ps[:, g % 2, :], q_st[:, s, g, :],
                   k_bd[:, s].rearrange("p j m -> p (j m)"), start=True, stop=False)
                mm(ps[:, g % 2, :], ident_b[:, :], mask_b[:, 0, :].unsqueeze(1).broadcast_to([P, HQ, P]),
                   start=False, stop=True).then_inc(b_sn, 1)

            def scores_T(b, s, g):
                if g == 0:
                    pe.wait_ge(b_low, b + 1)
                    pe.wait_ge(b_max, 4 * b + 4)
                if g % 2 == 0 and (not isinstance(b, int) or b >= 1):
                    pe.wait_ge(b_exp, 2 * b + g // 2 - 1)
                queries = (q[:, s].rearrange("p j n -> p (j n)") for q in (q_hi, q_lo, q_hi))
                for n, (keys, q) in enumerate(zip((k_lo, k_hi, k_hi), queries)):
                    mm(ps[:, 2 + g, :], keys[:, s, g, :], q, start=(n == 0), stop=False)
                for j in range(HQ):
                    h = HQ * g + j
                    mm(ps[:, 2 + g, j * P:(j + 1) * P], nmax[:, s, h:h + 1].to_broadcast([P, P]), ident_b[:, :],
                       start=False, stop=False)
                last = mm(ps[:, 2 + g, :], ident_b[:, :], mask_b[:, 1, :].unsqueeze(1).broadcast_to([P, HQ, P]),
                          start=False, stop=True)
                if g % 2:
                    last.then_inc(b_st, 1)

            def attend(b, s):
                pe.wait_ge(b_prep, 5 * b + 5)
                pe.wait_ge(b_exp, 2 * b + 2)
                for a in range(HQ):
                    for j in range(HQ):
                        last = mm(ps[32 * j:32 * j + 32, 6, a * P:(a + 1) * P], v_st[:, s, HQ * a + j, :],
                                  pT[:, HQ * a + j, :], start=True, stop=True)
                last.then_inc(b_av, 1)

            def natural(b):
                pe.wait_ge(b_avs, b + 1)
                if not isinstance(b, int) or b >= 1:
                    pe.wait_ge(b_x, b)
                for a in range(HQ):
                    last = tr(ps[:, 7, a * P:(a + 1) * P], avT[:, a * P:(a + 1) * P], ident)
                last.then_inc(b_nat, 1)

            def out_T(b):
                pe.wait_ge(b_ao, b + 1)
                tr(ps[:, 7, 0:P], ao[:, :], ident).then_inc(b_aoT, 1)

            def project(b):
                pe.wait_ge(b_aoTs, b + 1)
                mm(ps[:, 7, P:2 * P], aoT[:, :], square(W_O0), start=True, stop=True).then_inc(b_y, 1)

            def slot(b, s, last=False):
                attend(b - 1, 1 - s)
                if not isinstance(b, int) or b >= 2:
                    project(b - 2)
                scores_T(b, s, 0)
                if not last:
                    scores(b + 1, 1 - s, 0)
                scores_T(b, s, 1)
                if not last:
                    scores(b + 1, 1 - s, 1)
                natural(b - 1)
                scores_T(b, s, 2)
                if not last:
                    scores(b + 1, 1 - s, 2)
                scores_T(b, s, 3)
                out_T(b - 1)
                if not last:
                    scores(b + 1, 1 - s, 3)

            for g in range(4):
                scores(0, 0, g)
            for g in range(4):
                scores_T(0, 0, g)
            for g in range(4):
                scores(1, 1, g)
            slot(1, 1)
            with pe.Fori(1, NB // 2 - 1) as r:
                slot(2 * r, 0)
                slot(2 * r + 1, 1)
            slot(NB - 2, 0)
            slot(NB - 1, 1, last=True)
            def split_product(out, weights_hi, weights_lo, tok):
                mm(out, weights_lo, xn_hi[:, tok], start=True, stop=False)
                mm(out, weights_hi, xn_lo[:, tok], start=False, stop=False)
                return mm(out, weights_hi, xn_hi[:, tok], start=False, stop=True)

            def gate_or_up(c, e, f, up):
                tok = bass.ds(c * CH, CH)
                if e == f == up == 0:
                    pe.wait_ge(ln_lo, c + 1)
                cols = slice(f * P, (f + 1) * P)
                n = c * NE * NF + e * NF + f
                if not up and (e or not isinstance(c, int) or c):
                    pe.wait_ge(c_silu, n - NF + 1)
                    pe.wait_ge(c_h, n - NF + 1)
                high, low, ready = (up_hi, up_lo, c_up) if up else (gate_hi, gate_lo, c_gate)
                split_product(ps[:, 2 * up + f, :], high[:, e, cols], low[:, e, cols], tok).then_inc(ready, 1)

            def gate_up(c, e):
                for f in range(NF):
                    for up in range(2):
                        gate_or_up(c, e, f, up)

            transpose_chunk(NCH, xn[:, 0], 0)
            attend(NB - 1, 1)
            project(NB - 2)
            pe.wait_ge(ld_ffn, N_FFN)
            pe.wait_ge(w_lo, 2 * NE // SPLIT)
            gate_or_up(0, 0, 0, 0)
            natural(NB - 1)
            route(xnT[:, 0, :], 0, 5, c_logit)
            gate_or_up(0, 0, 0, 1)
            out_T(NB - 1)
            gate_or_up(0, 0, 1, 0)
            gate_or_up(0, 0, 1, 1)
            project(NB - 1)

            def down(c, e):
                pe.wait_ge(c_h, (c * NE + e + 1) * NF)
                for t in range(TPC):
                    for f in range(NF):
                        last = mm(ps[:, 4 + e % 2, t * P:(t + 1) * P], hT[:, e % 2, f, t * P:(t + 1) * P],
                                  down_w[:, e, f, :], start=(f == 0), stop=(f == NF - 1))
                last.then_inc(c_down, 1)

            def weights_T(c, n):
                pe.wait_ge(c_w, c + 1)
                for t in range(TPC):
                    last = tr(ps[0:NE, n, t * P:(t + 1) * P], wexp[:, t, :], ident)
                last.then_inc(c_wT, 1)

            def experts(c, last=False):
                for e in range(NE):
                    if e + 1 < NE:
                        gate_up(c, e + 1)
                    elif not last:
                        gate_up(c + 1, 0)
                    down(c, e)
                    if e == 1:
                        weights_T(c, 6)
                        pe.wait_ge(ld_ctx_c, 16 * (c + 1))
                        for t in range(TPC):
                            done = mm(ps[:, 7, t * P:(t + 1) * P], ctxT_c[:, t * P:(t + 1) * P], square(W_K1),
                                      start=True, stop=True)
                        done.then_inc(d_k, 1)
                    elif e == 2:
                        pe.wait_ge(c_wTs, c + 1)
                        for t in range(TPC):
                            done = mm(ps[:, 6, t * P:(t + 1) * P], wT[:, t * P:(t + 1) * P], down_b[:, :],
                                      start=True, stop=True)
                        done.then_inc(c_bias, 1)
                        pe.wait_ge(d_kb, c + 1)
                        if not last:
                            transpose_chunk(NCH + 1 + c, xn[:, 0], 7)
                    elif e == 3:
                        if not last:
                            pe.wait_ge(ln_Ts, NCH + 2 + c)
                            pe.wait_ge(c_biased, c + 1)
                            route(xnT[:, 0, :], 0, 6, c_logit)
                    elif e == 4:
                        if not last:
                            pe.wait_ge(c_shift, c + 2)
                        else:
                            pe.wait_ge(c_biased, c + 1)
                        for t in range(TPC):
                            done = mm(ps[:, 6, t * P:(t + 1) * P], ctxT_c[:, t * P:(t + 1) * P], square(W_V1),
                                      start=True, stop=True)
                        done.then_inc(d_v, 1)
                    if last and e in (2, 4, 6):
                        if e > 2:
                            pe.wait_ge(ln_Ts, LN_D + e // 2 - 1)
                        chunk = e // 2 - 1
                        transpose_chunk(LN_D + chunk, xn_d[:, chunk * TPC:(chunk + 1) * TPC], 7)
                    if e == (7 if last else 6):
                        if last:
                            pe.wait_ge(ln_Ts, LN_D + NCH - 1)
                        pe.wait_ge(d_kn, c + 1)
                        pe.wait_ge(d_vs, c + 1)
                        for t in range(TPC):
                            done = mm(ps[:, 7 - t // 2, (t % 2) * 256:(t % 2) * 256 + D + 1],
                                      kl[:, t * H:(t + 1) * H].rearrange("p h d -> p (h d)"), vl[:, t, :],
                                      start=True, stop=True)
                        done.then_inc(d_kv, 1)

            with pe.Fori(0, NCH - 1) as c:
                experts(c)
            experts(NCH - 1, last=True)

            for c in range(NCH):
                if c == 2:
                    pe.wait_ge(c_x, 1)
                if c == NCH - 1:
                    transpose_chunk(LN_D + c, xn_d[:, c * TPC:(c + 1) * TPC], 2 * c)
                pe.wait_ge(ln_Ts, LN_D + c + 1)
                for t in range(TPC):
                    col = ps[:, 2 * c + 1, t * P:(t + 1) * P]
                    mm(col, one_row[:, :], rows[0:1, 0:D], start=True, stop=False)
                    last = mm(col, xnT_d[:, c, t * P:(t + 1) * P], square(W_Q1), start=False, stop=True)
                last.then_inc(d_q, 1)
            def queries_T(c):
                pe.wait_ge(d_qn, c + 1)
                for t in range(TPC):
                    last = tr(ps[:, 2 * c, t * P:(t + 1) * P], ql[:, c, t * H:(t + 1) * H].rearrange("p h d -> p (h d)"),
                              ident)
                last.then_inc(d_qT, 1)

            def numerators(c):
                if c == 0:
                    pe.wait_ge(d_kvd, NCH)
                pe.wait_ge(d_qTs, c + 1)
                for t in range(TPC):
                    last = mm(numerators_of(c, t, t + 1)[:, 0, :], qnT[:, c, t * P:(t + 1) * P], kvd[:, c * TPC + t, :],
                              start=True, stop=True)
                last.then_inc(d_num, 1)

            def output_T(c):
                pe.wait_ge(d_sum, c + 1)
                for t in range(TPC):
                    last = tr(ps[:, 2 * c, t * P:(t + 1) * P], lo[:, c, t * H:(t + 1) * H].rearrange("p h d -> p (h d)"),
                              ident)
                last.then_inc(d_oT, 1)

            def project_d(c):
                pe.wait_ge(d_oTs, c + 1)
                for t in range(TPC):
                    last = mm(ps[:, 2 * c + 1, t * P:(t + 1) * P], loT[:, c, t * P:(t + 1) * P], square(W_P1),
                              start=True, stop=True)
                last.then_inc(d_y, 1)

            queries_T(0)
            for c in range(1, NCH):
                queries_T(c)
                numerators(c - 1)
            output_T(0)
            numerators(NCH - 1)
            project_d(0)
            output_T(1)
            for c in range(2, NCH):
                output_T(c)
                project_d(c - 1)
            project_d(NCH - 1)
            def tokens_T(c, n):
                transpose_chunk(3 * NCH + c, xn_d[:, c * TPC:(c + 1) * TPC], n)

            tokens_T(0, 0)

            def logits(c):
                pe.wait_ge(ln_Ts, 3 * NCH + c + 1)
                route(xnT_d[:, c, :], 1, 6, e_logit, c * TPC)

            def threshold_count(n):
                pe.wait_ge(e_cnt, n + 1)
                mm(ps[:, 6, 0:3], sum16, cnt[:, :], start=True, stop=True).then_inc(e_tot, 1)

            def choice_step(n):
                if n < THRESHOLD_STEPS:
                    threshold_count(n)
                elif n == THRESHOLD_STEPS:
                    pe.wait_ge(e_ties, 1)
                    mm(ps[:, 6, 0:1], sum16, cnt[:, 0:1], start=True, stop=True)
                    mm(ps[:, 6, 1:2], tri16, cnt[:, 1:2], start=True, stop=True).then_inc(e_tie_tot, 1)
                elif n == THRESHOLD_STEPS + 1:
                    pe.wait_ge(e_sel, 1)
                    tr(ps[:, 7, 0:P], selT[:, :], ident).then_inc(e_selT, 1)

            def choice(n, quarter):
                quarters = 4 * (n - CHOICE) + quarter
                if quarters >= 0 and quarters % 3 == 0:
                    choice_step(quarters // 3)

            def first(n):
                c, e = n // NE, n % NE
                if n == 0:
                    pe.wait_ge(w_lo, 3 * NE // SPLIT)
                if e == 0:
                    pe.wait_ge(ln_lo, NCH + c + 1)
                for f in range(NF):
                    cols = slice(f * P, (f + 1) * P)
                    if n >= 2:
                        pe.wait_ge(e_gelu, (n - 2) * NF + f + 1)
                    split_product(ps[:, 2 * (e % 2) + f, :], w1_hi[:, e, cols], w1_lo[:, e, cols],
                                  slice(c * CH, (c + 1) * CH)).then_inc(e_h, 1)
                    choice(n - 1, f)

            def second(n):
                c, e = n // NE, n % NE
                pe.wait_ge(e_gelu, (n + 1) * NF)
                if n >= 2:
                    pe.wait_ge(e_part, n - 1)
                for t in range(TPC):
                    for f in range(NF):
                        last = mm(ps[:, LAST_BANKS[t // 2] if n == LAST else 4 + e % 2, t * P:(t + 1) * P],
                                  hT[:, e % 2, f, t * P:(t + 1) * P], w2[:, e, f, :], start=(f == 0), stop=(f == NF - 1))
                    if t == TPC - 1 or n == LAST and t % 2:
                        last.then_inc(e_down, 1)
                    if t % 2:
                        choice(n, 2 + t // 2)

            logits(0)
            first(0)
            tokens_T(1, 4)
            for n in range(NCH * NE):
                if n + 1 < NCH * NE:
                    first(n + 1)
                if n < NCH - 1:
                    logits(n + 1)
                    if n == 1:
                        pe.wait_ge(ln_all, NCH + 3)
                    if n < 2:
                        tokens_T(2 + n, 7)
                elif n == CHOICE - 1:
                    pe.wait_ge(e_p, 1)
                    tr(ps[:, 7, 0:P], probs[:, :, :].rearrange("p e t -> p (e t)"), ident).then_inc(e_pT, 1)
                second(n)


def kernel(**inputs):
    import numpy as np
    import concourse.bacc as bacc
    from concourse.bass_utils import run_bass_kernel_spmd

    def a(name):
        return np.asarray(inputs[name])

    f = np.float32
    cst = np.zeros((P, C_END), f)
    r = np.arange(P)
    cst[:, C_IDENT:C_IDENT + P] = np.eye(P)
    cst[:, C_BLOCK:C_BLOCK + P] = r[:, None] // DH == r[None, :] // DH
    cst[:, C_SUM16:C_SUM16 + P] = r[:, None] // NB == r[None, :] // NB
    cst[:, C_TRI16:C_TRI16 + P] = (r[:, None] // NB == r[None, :] // NB) & (r[:, None] < r[None, :])
    cst[:, C_HEAD:C_HEAD + H] = r[:, None] // DH == np.arange(H)[None, :]
    cst[:, C_QUAD:C_QUAD + HQ] = (r[:, None] % 32) // DH == np.arange(HQ)[None, :]
    cst[:, C_GROUP:C_GROUP + HQ] = r[:, None] // 32 == np.arange(HQ)[None, :]
    cst[:, C_KEY:C_KEY + NE] = NE - np.arange(NE)[None, :]
    wg1 = np.zeros((P, 2 * HQ, P), f)
    wg2 = np.zeros((P, 2, 32), f)
    for g in range(HQ):
        for j in range(HQ):
            wg1[32 * g + DH * j:32 * g + DH * (j + 1), 2 * g + j // 2, HID * (j % 2):HID * (j % 2 + 1)] = a("L0_xattn_wg1").T
    for j in range(HQ):
        wg2[HID * (j % 2):HID * (j % 2 + 1), j // 2, DH * j:DH * (j + 1)] = a("L0_xattn_wg2").T
    squares = ["L0_xattn_wq", "L0_xattn_wk", "L0_xattn_wv", "L0_xattn_wo", "L1_xattn_Wq", "L1_xattn_Wk", "L1_xattn_Wv", "L1_xattn_Wp"]
    mask = a("mask_1x1xSxS2_bf1")[0, 0].view(np.uint8)

    def blocks(b):
        return b.reshape(NE, NF, P).transpose(2, 0, 1).reshape(P, NE * NF)

    data = {
        "cst": cst,
        "x": a("x"),
        "ctxT": a("ctx_1024").transpose(2, 0, 1).reshape(D, NB * P),
        "w": np.concatenate([a(n).T for n in squares], axis=1),
        "wg1": wg1,
        "wg2": wg2,
        "wb": np.concatenate([a("L0_xattn_wb2").T, a("L0_xattn_wb1")], axis=1),
        "rows": np.concatenate([a("L1_xattn_bq"), a("L1_xattn_bk"), a("L1_xattn_bv"), a("L1_xattn_bp"),
                                a("g_xattn"), a("g_ffn")])[None, :],
        "mask": np.stack([mask, mask.T], axis=1),
        "routers": np.stack([a("L0_ffn_router_w").T, a("L1_ffn_Wg")], axis=1),
        "down_b": a("L0_ffn_down_b"),
        "gate_w": a("L0_ffn_gate_w"),
        "up_w": a("L0_ffn_up_w"),
        "down_w": a("L0_ffn_down_w"),
        "gate_b": blocks(a("L0_ffn_gate_b")),
        "up_b": blocks(a("L0_ffn_up_b")),
        "w1": a("L1_ffn_W1"),
        "w2": a("L1_ffn_W2"),
    }
    nc = bacc.Bacc("TRN2", target_bir_lowering=False, num_devices=1)
    arrays, aps = {}, {}
    for name, value in data.items():
        value = np.ascontiguousarray(value)
        arrays[f"in_{name}"] = value
        aps[name] = nc.dram_tensor(f"in_{name}", value.shape, mybir.dt.from_np(value.dtype), kind="ExternalInput").ap()
    out = nc.dram_tensor("out", (NB, P, D), mybir.dt.float32, kind="ExternalOutput").ap()
    build(nc, aps, out)
    ran = run_bass_kernel_spmd(nc, [arrays], core_ids=[0])
    return ran.results[0]["out"]
```
